# Optimizing a Trainium2 kernel written in Bass

```python
import numpy as np
import jax
import jax.numpy as jnp

def _softmax(x, axis=-1):
    return jax.nn.softmax(x, axis=axis)
def _gelu(x):
    return jax.nn.gelu(x, approximate=True)
def _silu(x):
    return jax.nn.silu(x)
def _sigmoid(x):
    return jax.nn.sigmoid(x)
def _layernorm(x, axis=-1, eps=1e-5):
    m = jnp.mean(x, axis=axis, keepdims=True)
    v = jnp.var(x, axis=axis, keepdims=True)
    return (x - m) / jnp.sqrt(v + eps)
def _scatter_add(tgt, idx, src, axis=0):
    return tgt.at[idx].add(src)
def _segment_sum(src, seg, n):
    return jax.ops.segment_sum(src, seg, n)

kernel_name = 'mk_conv_seq_d2_conv_nchw256_af476f'

def setup_inputs(seed: int = 0):
    np.random.seed(seed)
    _w = jnp.asarray
    def _rec_inputs():
        import jax
        import jax.numpy as jnp
        _gk = jax.random.key(seed)
        x = -0.0002928 + 1 * jax.random.normal(jax.random.fold_in(_gk, 1), (4, 256, 64, 64), jnp.float32)
        return x
    x = _rec_inputs()
    def _L0_conv_setup():
        import jax, jax.numpy as jnp
        from jax import lax
        import numpy as np
        import math
        B, CH, H, W = (4, 256, 64, 64)
        TOK = 8
        GCN = math.ceil(CH / TOK)
        PAD = TOK * GCN
        DIN = 2 * GCN
        DSTATE = 16
        DTR = math.ceil(GCN / 16)
        GROUPS = 4
        EPS = 1e-05

        def _forward(x, W_in, W_x, W_dt, b_dt, A_logs, Ds, W_out, gn_w, gn_b):
            b, c, h, w = x.shape
            M = b * h * w
            xf = jnp.transpose(x, (0, 2, 3, 1)).reshape(M, TOK, GCN)
            xz = xf @ W_in
            xp, z = (xz[..., :DIN], xz[..., DIN:])
            xs = jnp.concatenate([xp, xp[:, ::-1]], axis=0)
            x_dbl = xs @ W_x
            dts = x_dbl[..., :DTR]
            Bs = x_dbl[..., DTR:DTR + DSTATE]
            Cs = x_dbl[..., DTR + DSTATE:]
            dts = dts @ W_dt + b_dt
            A = -jnp.exp(A_logs)
            delta = jax.nn.softplus(dts + b_dt)

            def step(hst, inp):
                d_t, u_t, B_t, C_t = inp
                dA = jnp.exp(d_t[:, :, None] * A)
                hst = dA * hst + (d_t * u_t)[:, :, None] * B_t[:, None, :]
                y_t = jnp.einsum('bdn,bn->bd', hst, C_t)
                return (hst, y_t)
            h0 = jnp.zeros((2 * M, DIN, DSTATE), dtype=x.dtype)
            scan_in = (jnp.swapaxes(delta, 0, 1), jnp.swapaxes(xs, 0, 1), jnp.swapaxes(Bs, 0, 1), jnp.swapaxes(Cs, 0, 1))
            _, ys = lax.scan(step, h0, scan_in)
            ys = jnp.swapaxes(ys, 0, 1) + xs * Ds
            y1, y2 = (ys[:M], ys[M:])
            y = y1 + y2[:, ::-1]
            y = y * jax.nn.gelu(z, approximate=False)
            y = y @ W_out
            y = y.reshape(b, h, w, PAD).transpose(0, 3, 1, 2)
            yg = y.reshape(b, GROUPS, -1)
            mu = yg.mean(-1, keepdims=True)
            var = yg.var(-1, keepdims=True)
            yg = (yg - mu) * lax.rsqrt(var + EPS)
            y = yg.reshape(b, PAD, h, w) * gn_w[None, :, None, None] + gn_b[None, :, None, None]
            return x + y[:, :c]
        key = jax.random.key(seed)
        ks = jax.random.split(key, 8)
        x = jax.random.normal(ks[0], (B, CH, H, W), dtype=jnp.float32)
        W_in = jax.random.normal(ks[1], (GCN, 2 * DIN), dtype=jnp.float32) * 0.05
        W_x = jax.random.normal(ks[2], (DIN, DTR + 2 * DSTATE), dtype=jnp.float32) * 0.05
        dt_init_std = DTR ** (-0.5)
        W_dt = jax.random.uniform(ks[3], (DTR, DIN), dtype=jnp.float32, minval=-dt_init_std, maxval=dt_init_std)
        dt = jnp.exp(jax.random.uniform(ks[4], (DIN,), dtype=jnp.float32) * (math.log(0.1) - math.log(0.001)) + math.log(0.001))
        dt = jnp.clip(dt, 0.0001)
        b_dt = dt + jnp.log(-jnp.expm1(-dt))
        A_logs = jnp.log(jnp.broadcast_to(jnp.arange(1, DSTATE + 1, dtype=jnp.float32), (DIN, DSTATE)))
        Ds = jnp.ones((DIN,), dtype=jnp.float32)
        W_out = jax.random.normal(ks[5], (DIN, GCN), dtype=jnp.float32) * 0.05
        gn_w = jnp.ones((PAD,), dtype=jnp.float32)
        gn_b = jnp.zeros((PAD,), dtype=jnp.float32)
        return {'x': x, 'W_in': W_in, 'W_x': W_x, 'W_dt': W_dt, 'b_dt': b_dt, 'A_logs': A_logs, 'Ds': Ds, 'W_out': W_out, 'gn_w': gn_w, 'gn_b': gn_b}
    _L0_conv_all = _L0_conv_setup()
    _L0_conv_in = {k: v for k, v in _L0_conv_all.items() if k in ('W_in', 'W_x', 'W_dt', 'b_dt', 'A_logs', 'Ds', 'W_out', 'gn_w', 'gn_b', )}
    del _L0_conv_all

    def _L1_conv_setup():
        import jax, jax.numpy as jnp
        import numpy as np

        def conv2d(x, w, b, pad):
            out = jax.lax.conv_general_dilated(x, w, (1, 1), ((pad, pad), (pad, pad)), dimension_numbers=('NCHW', 'OIHW', 'NCHW'))
            return out + b[None, :, None, None]

        def silu(x):
            return x * jax.nn.sigmoid(x)

        def group_norm(x, g, b, groups, eps=1e-05):
            B, C, H, W = x.shape
            xg = x.reshape(B, groups, C // groups, H, W)
            m = xg.mean(axis=(2, 3, 4), keepdims=True)
            v = xg.var(axis=(2, 3, 4), keepdims=True)
            xg = (xg - m) * jax.lax.rsqrt(v + eps)
            return xg.reshape(B, C, H, W) * g[None, :, None, None] + b[None, :, None, None]

        def snake_cumsum(off):
            K = off.shape[1]
            c = K // 2
            upper = jnp.cumsum(off[:, c + 1:], axis=1)
            lower = jnp.flip(jnp.cumsum(jnp.flip(off[:, :c], axis=1), axis=1), axis=1)
            return jnp.concatenate([lower, jnp.zeros_like(off[:, :1]), upper], axis=1)

        def bilinear_gather(img, ys, xs):
            B, C, H, W = img.shape
            K = ys.shape[1]
            ys = jnp.clip(ys, 0.0, H - 1.0)
            xs = jnp.clip(xs, 0.0, W - 1.0)
            y0f = jnp.floor(ys)
            x0f = jnp.floor(xs)
            wy = (ys - y0f)[:, None]
            wx = (xs - x0f)[:, None]
            y0 = y0f.astype(jnp.int32)
            x0 = x0f.astype(jnp.int32)
            y1 = jnp.minimum(y0 + 1, H - 1)
            x1 = jnp.minimum(x0 + 1, W - 1)
            flat = img.reshape(B, C, H * W)

            def gat(yi, xi):
                idx = (yi * W + xi).reshape(B, -1)
                g = jnp.take_along_axis(flat, idx[:, None, :], axis=2)
                return g.reshape(B, C, K, H, W)
            return gat(y0, x0) * (1 - wy) * (1 - wx) + gat(y0, x1) * (1 - wy) * wx + gat(y1, x0) * wy * (1 - wx) + gat(y1, x1) * wy * wx

        def dsconv(x, off_w, off_b, dsc_w, dsc_b, gn_g, gn_b, morph, extend_scope=1.0):
            B, C, H, W = x.shape
            K = dsc_w.shape[-1]
            c = K // 2
            off = jnp.tanh(conv2d(x, off_w, off_b, pad=1))
            bend = snake_cumsum(off[:, :K] if morph == 0 else off[:, K:])
            spread = (jnp.arange(K) - c).astype(x.dtype)[None, :, None, None]
            hh = jnp.arange(H, dtype=x.dtype)[None, None, :, None]
            ww = jnp.arange(W, dtype=x.dtype)[None, None, None, :]
            if morph == 0:
                ys = hh + extend_scope * bend
                xs = jnp.broadcast_to(ww + spread, ys.shape)
            else:
                xs = ww + extend_scope * bend
                ys = jnp.broadcast_to(hh + spread, xs.shape)
            sampled = bilinear_gather(x, ys, xs)
            out = jnp.einsum('bckhw,ock->bohw', sampled, dsc_w) + dsc_b[None, :, None, None]
            O = dsc_w.shape[0]
            return jax.nn.relu(group_norm(out, gn_g, gn_b, groups=O // 4))

        def dysnake_conv(x, p):
            kpad = p['conv0_w'].shape[-1] // 2
            a = silu(conv2d(x, p['conv0_w'], p['conv0_b'], pad=kpad))
            bx = dsconv(x, p['offx_w'], p['offx_b'], p['dscx_w'], p['dscx_b'], p['gnx_g'], p['gnx_b'], morph=0)
            by = dsconv(x, p['offy_w'], p['offy_b'], p['dscy_w'], p['dscy_b'], p['gny_g'], p['gny_b'], morph=1)
            cat = jnp.concatenate([a, bx, by], axis=1)
            return silu(jnp.einsum('bchw,oc->bohw', cat, p['fuse_w']) + p['fuse_b'][None, :, None, None])
        _PNAMES = ['conv0_w', 'conv0_b', 'offx_w', 'offx_b', 'dscx_w', 'dscx_b', 'gnx_g', 'gnx_b', 'offy_w', 'offy_b', 'dscy_w', 'dscy_b', 'gny_g', 'gny_b', 'fuse_w', 'fuse_b']
        key = jax.random.key(seed)
        ks = iter(jax.random.split(key, 64))

        def rn(shape, s=0.05):
            return jax.random.normal(next(ks), shape, dtype=jnp.float32) * s
        B, H, W = (8, 80, 80)
        c1, c2, c_ = (256, 256, 128)
        kk = 3

        def block(inc, ouc, pre):
            return {pre + 'conv0_w': rn((ouc, inc, kk, kk)), pre + 'conv0_b': rn((ouc,)), pre + 'offx_w': rn((2 * kk, inc, 3, 3)), pre + 'offx_b': rn((2 * kk,)), pre + 'dscx_w': rn((ouc, inc, kk)), pre + 'dscx_b': rn((ouc,)), pre + 'gnx_g': jnp.ones((ouc,), jnp.float32), pre + 'gnx_b': jnp.zeros((ouc,), jnp.float32), pre + 'offy_w': rn((2 * kk, inc, 3, 3)), pre + 'offy_b': rn((2 * kk,)), pre + 'dscy_w': rn((ouc, inc, kk)), pre + 'dscy_b': rn((ouc,)), pre + 'gny_g': jnp.ones((ouc,), jnp.float32), pre + 'gny_b': jnp.zeros((ouc,), jnp.float32), pre + 'fuse_w': rn((ouc, 3 * ouc)), pre + 'fuse_b': rn((ouc,))}
        inp = {'x': jax.random.normal(next(ks), (B, c1, H, W), dtype=jnp.float32)}
        inp.update(block(c1, c_, 'cv1_'))
        inp.update(block(c_, c2, 'cv2_'))
        return inp
    _L1_conv_all = _L1_conv_setup()
    _L1_conv_in = {k: v for k, v in _L1_conv_all.items() if k in ('cv1_conv0_w', 'cv1_conv0_b', 'cv1_offx_w', 'cv1_offx_b', 'cv1_dscx_w', 'cv1_dscx_b', 'cv1_gnx_g', 'cv1_gnx_b', 'cv1_offy_w', 'cv1_offy_b', 'cv1_dscy_w', 'cv1_dscy_b', 'cv1_gny_g', 'cv1_gny_b', 'cv1_fuse_w', 'cv1_fuse_b', 'cv2_conv0_w', 'cv2_conv0_b', 'cv2_offx_w', 'cv2_offx_b', 'cv2_dscx_w', 'cv2_dscx_b', 'cv2_gnx_g', 'cv2_gnx_b', 'cv2_offy_w', 'cv2_offy_b', 'cv2_dscy_w', 'cv2_dscy_b', 'cv2_gny_g', 'cv2_gny_b', 'cv2_fuse_w', 'cv2_fuse_b', )}
    del _L1_conv_all

    return {
        "x": x,
        "L0_conv_W_in": _L0_conv_in["W_in"],
        "L0_conv_W_x": _L0_conv_in["W_x"],
        "L0_conv_W_dt": _L0_conv_in["W_dt"],
        "L0_conv_b_dt": _L0_conv_in["b_dt"],
        "L0_conv_A_logs": _L0_conv_in["A_logs"],
        "L0_conv_Ds": _L0_conv_in["Ds"],
        "L0_conv_W_out": _L0_conv_in["W_out"],
        "L0_conv_gn_w": _L0_conv_in["gn_w"],
        "L0_conv_gn_b": _L0_conv_in["gn_b"],
        "L1_conv_cv1_conv0_w": _L1_conv_in["cv1_conv0_w"],
        "L1_conv_cv1_conv0_b": _L1_conv_in["cv1_conv0_b"],
        "L1_conv_cv1_offx_w": _L1_conv_in["cv1_offx_w"],
        "L1_conv_cv1_offx_b": _L1_conv_in["cv1_offx_b"],
        "L1_conv_cv1_dscx_w": _L1_conv_in["cv1_dscx_w"],
        "L1_conv_cv1_dscx_b": _L1_conv_in["cv1_dscx_b"],
        "L1_conv_cv1_gnx_g": _L1_conv_in["cv1_gnx_g"],
        "L1_conv_cv1_gnx_b": _L1_conv_in["cv1_gnx_b"],
        "L1_conv_cv1_offy_w": _L1_conv_in["cv1_offy_w"],
        "L1_conv_cv1_offy_b": _L1_conv_in["cv1_offy_b"],
        "L1_conv_cv1_dscy_w": _L1_conv_in["cv1_dscy_w"],
        "L1_conv_cv1_dscy_b": _L1_conv_in["cv1_dscy_b"],
        "L1_conv_cv1_gny_g": _L1_conv_in["cv1_gny_g"],
        "L1_conv_cv1_gny_b": _L1_conv_in["cv1_gny_b"],
        "L1_conv_cv1_fuse_w": _L1_conv_in["cv1_fuse_w"],
        "L1_conv_cv1_fuse_b": _L1_conv_in["cv1_fuse_b"],
        "L1_conv_cv2_conv0_w": _L1_conv_in["cv2_conv0_w"],
        "L1_conv_cv2_conv0_b": _L1_conv_in["cv2_conv0_b"],
        "L1_conv_cv2_offx_w": _L1_conv_in["cv2_offx_w"],
        "L1_conv_cv2_offx_b": _L1_conv_in["cv2_offx_b"],
        "L1_conv_cv2_dscx_w": _L1_conv_in["cv2_dscx_w"],
        "L1_conv_cv2_dscx_b": _L1_conv_in["cv2_dscx_b"],
        "L1_conv_cv2_gnx_g": _L1_conv_in["cv2_gnx_g"],
        "L1_conv_cv2_gnx_b": _L1_conv_in["cv2_gnx_b"],
        "L1_conv_cv2_offy_w": _L1_conv_in["cv2_offy_w"],
        "L1_conv_cv2_offy_b": _L1_conv_in["cv2_offy_b"],
        "L1_conv_cv2_dscy_w": _L1_conv_in["cv2_dscy_w"],
        "L1_conv_cv2_dscy_b": _L1_conv_in["cv2_dscy_b"],
        "L1_conv_cv2_gny_g": _L1_conv_in["cv2_gny_g"],
        "L1_conv_cv2_gny_b": _L1_conv_in["cv2_gny_b"],
        "L1_conv_cv2_fuse_w": _L1_conv_in["cv2_fuse_w"],
        "L1_conv_cv2_fuse_b": _L1_conv_in["cv2_fuse_b"],
    }

def reference(x, L0_conv_W_in, L0_conv_W_x, L0_conv_W_dt, L0_conv_b_dt, L0_conv_A_logs, L0_conv_Ds, L0_conv_W_out, L0_conv_gn_w, L0_conv_gn_b, L1_conv_cv1_conv0_w, L1_conv_cv1_conv0_b, L1_conv_cv1_offx_w, L1_conv_cv1_offx_b, L1_conv_cv1_dscx_w, L1_conv_cv1_dscx_b, L1_conv_cv1_gnx_g, L1_conv_cv1_gnx_b, L1_conv_cv1_offy_w, L1_conv_cv1_offy_b, L1_conv_cv1_dscy_w, L1_conv_cv1_dscy_b, L1_conv_cv1_gny_g, L1_conv_cv1_gny_b, L1_conv_cv1_fuse_w, L1_conv_cv1_fuse_b, L1_conv_cv2_conv0_w, L1_conv_cv2_conv0_b, L1_conv_cv2_offx_w, L1_conv_cv2_offx_b, L1_conv_cv2_dscx_w, L1_conv_cv2_dscx_b, L1_conv_cv2_gnx_g, L1_conv_cv2_gnx_b, L1_conv_cv2_offy_w, L1_conv_cv2_offy_b, L1_conv_cv2_dscy_w, L1_conv_cv2_dscy_b, L1_conv_cv2_gny_g, L1_conv_cv2_gny_b, L1_conv_cv2_fuse_w, L1_conv_cv2_fuse_b):
    import jax
    import jax.numpy as jnp
    def _L0_conv_ref(x, W_in, W_x, W_dt, b_dt, A_logs, Ds, W_out, gn_w, gn_b):
        import jax, jax.numpy as jnp
        from jax import lax
        import numpy as np
        import math
        B, CH, H, W = (4, 256, 64, 64)
        TOK = 8
        GCN = math.ceil(CH / TOK)
        PAD = TOK * GCN
        DIN = 2 * GCN
        DSTATE = 16
        DTR = math.ceil(GCN / 16)
        GROUPS = 4
        EPS = 1e-05

        def _forward(x, W_in, W_x, W_dt, b_dt, A_logs, Ds, W_out, gn_w, gn_b):
            b, c, h, w = x.shape
            M = b * h * w
            xf = jnp.transpose(x, (0, 2, 3, 1)).reshape(M, TOK, GCN)
            xz = xf @ W_in
            xp, z = (xz[..., :DIN], xz[..., DIN:])
            xs = jnp.concatenate([xp, xp[:, ::-1]], axis=0)
            x_dbl = xs @ W_x
            dts = x_dbl[..., :DTR]
            Bs = x_dbl[..., DTR:DTR + DSTATE]
            Cs = x_dbl[..., DTR + DSTATE:]
            dts = dts @ W_dt + b_dt
            A = -jnp.exp(A_logs)
            delta = jax.nn.softplus(dts + b_dt)

            def step(hst, inp):
                d_t, u_t, B_t, C_t = inp
                dA = jnp.exp(d_t[:, :, None] * A)
                hst = dA * hst + (d_t * u_t)[:, :, None] * B_t[:, None, :]
                y_t = jnp.einsum('bdn,bn->bd', hst, C_t)
                return (hst, y_t)
            h0 = jnp.zeros((2 * M, DIN, DSTATE), dtype=x.dtype)
            scan_in = (jnp.swapaxes(delta, 0, 1), jnp.swapaxes(xs, 0, 1), jnp.swapaxes(Bs, 0, 1), jnp.swapaxes(Cs, 0, 1))
            _, ys = lax.scan(step, h0, scan_in)
            ys = jnp.swapaxes(ys, 0, 1) + xs * Ds
            y1, y2 = (ys[:M], ys[M:])
            y = y1 + y2[:, ::-1]
            y = y * jax.nn.gelu(z, approximate=False)
            y = y @ W_out
            y = y.reshape(b, h, w, PAD).transpose(0, 3, 1, 2)
            yg = y.reshape(b, GROUPS, -1)
            mu = yg.mean(-1, keepdims=True)
            var = yg.var(-1, keepdims=True)
            yg = (yg - mu) * lax.rsqrt(var + EPS)
            y = yg.reshape(b, PAD, h, w) * gn_w[None, :, None, None] + gn_b[None, :, None, None]
            return x + y[:, :c]
        return _forward(x, W_in, W_x, W_dt, b_dt, A_logs, Ds, W_out, gn_w, gn_b)

    def _L1_conv_ref(x, cv1_conv0_w, cv1_conv0_b, cv1_offx_w, cv1_offx_b, cv1_dscx_w, cv1_dscx_b, cv1_gnx_g, cv1_gnx_b, cv1_offy_w, cv1_offy_b, cv1_dscy_w, cv1_dscy_b, cv1_gny_g, cv1_gny_b, cv1_fuse_w, cv1_fuse_b, cv2_conv0_w, cv2_conv0_b, cv2_offx_w, cv2_offx_b, cv2_dscx_w, cv2_dscx_b, cv2_gnx_g, cv2_gnx_b, cv2_offy_w, cv2_offy_b, cv2_dscy_w, cv2_dscy_b, cv2_gny_g, cv2_gny_b, cv2_fuse_w, cv2_fuse_b):
        import jax, jax.numpy as jnp
        import numpy as np

        def conv2d(x, w, b, pad):
            out = jax.lax.conv_general_dilated(x, w, (1, 1), ((pad, pad), (pad, pad)), dimension_numbers=('NCHW', 'OIHW', 'NCHW'))
            return out + b[None, :, None, None]

        def silu(x):
            return x * jax.nn.sigmoid(x)

        def group_norm(x, g, b, groups, eps=1e-05):
            B, C, H, W = x.shape
            xg = x.reshape(B, groups, C // groups, H, W)
            m = xg.mean(axis=(2, 3, 4), keepdims=True)
            v = xg.var(axis=(2, 3, 4), keepdims=True)
            xg = (xg - m) * jax.lax.rsqrt(v + eps)
            return xg.reshape(B, C, H, W) * g[None, :, None, None] + b[None, :, None, None]

        def snake_cumsum(off):
            K = off.shape[1]
            c = K // 2
            upper = jnp.cumsum(off[:, c + 1:], axis=1)
            lower = jnp.flip(jnp.cumsum(jnp.flip(off[:, :c], axis=1), axis=1), axis=1)
            return jnp.concatenate([lower, jnp.zeros_like(off[:, :1]), upper], axis=1)

        def bilinear_gather(img, ys, xs):
            B, C, H, W = img.shape
            K = ys.shape[1]
            ys = jnp.clip(ys, 0.0, H - 1.0)
            xs = jnp.clip(xs, 0.0, W - 1.0)
            y0f = jnp.floor(ys)
            x0f = jnp.floor(xs)
            wy = (ys - y0f)[:, None]
            wx = (xs - x0f)[:, None]
            y0 = y0f.astype(jnp.int32)
            x0 = x0f.astype(jnp.int32)
            y1 = jnp.minimum(y0 + 1, H - 1)
            x1 = jnp.minimum(x0 + 1, W - 1)
            flat = img.reshape(B, C, H * W)

            def gat(yi, xi):
                idx = (yi * W + xi).reshape(B, -1)
                g = jnp.take_along_axis(flat, idx[:, None, :], axis=2)
                return g.reshape(B, C, K, H, W)
            return gat(y0, x0) * (1 - wy) * (1 - wx) + gat(y0, x1) * (1 - wy) * wx + gat(y1, x0) * wy * (1 - wx) + gat(y1, x1) * wy * wx

        def dsconv(x, off_w, off_b, dsc_w, dsc_b, gn_g, gn_b, morph, extend_scope=1.0):
            B, C, H, W = x.shape
            K = dsc_w.shape[-1]
            c = K // 2
            off = jnp.tanh(conv2d(x, off_w, off_b, pad=1))
            bend = snake_cumsum(off[:, :K] if morph == 0 else off[:, K:])
            spread = (jnp.arange(K) - c).astype(x.dtype)[None, :, None, None]
            hh = jnp.arange(H, dtype=x.dtype)[None, None, :, None]
            ww = jnp.arange(W, dtype=x.dtype)[None, None, None, :]
            if morph == 0:
                ys = hh + extend_scope * bend
                xs = jnp.broadcast_to(ww + spread, ys.shape)
            else:
                xs = ww + extend_scope * bend
                ys = jnp.broadcast_to(hh + spread, xs.shape)
            sampled = bilinear_gather(x, ys, xs)
            out = jnp.einsum('bckhw,ock->bohw', sampled, dsc_w) + dsc_b[None, :, None, None]
            O = dsc_w.shape[0]
            return jax.nn.relu(group_norm(out, gn_g, gn_b, groups=O // 4))

        def dysnake_conv(x, p):
            kpad = p['conv0_w'].shape[-1] // 2
            a = silu(conv2d(x, p['conv0_w'], p['conv0_b'], pad=kpad))
            bx = dsconv(x, p['offx_w'], p['offx_b'], p['dscx_w'], p['dscx_b'], p['gnx_g'], p['gnx_b'], morph=0)
            by = dsconv(x, p['offy_w'], p['offy_b'], p['dscy_w'], p['dscy_b'], p['gny_g'], p['gny_b'], morph=1)
            cat = jnp.concatenate([a, bx, by], axis=1)
            return silu(jnp.einsum('bchw,oc->bohw', cat, p['fuse_w']) + p['fuse_b'][None, :, None, None])
        _PNAMES = ['conv0_w', 'conv0_b', 'offx_w', 'offx_b', 'dscx_w', 'dscx_b', 'gnx_g', 'gnx_b', 'offy_w', 'offy_b', 'dscy_w', 'dscy_b', 'gny_g', 'gny_b', 'fuse_w', 'fuse_b']
        p1 = dict(zip(_PNAMES, (cv1_conv0_w, cv1_conv0_b, cv1_offx_w, cv1_offx_b, cv1_dscx_w, cv1_dscx_b, cv1_gnx_g, cv1_gnx_b, cv1_offy_w, cv1_offy_b, cv1_dscy_w, cv1_dscy_b, cv1_gny_g, cv1_gny_b, cv1_fuse_w, cv1_fuse_b)))
        p2 = dict(zip(_PNAMES, (cv2_conv0_w, cv2_conv0_b, cv2_offx_w, cv2_offx_b, cv2_dscx_w, cv2_dscx_b, cv2_gnx_g, cv2_gnx_b, cv2_offy_w, cv2_offy_b, cv2_dscy_w, cv2_dscy_b, cv2_gny_g, cv2_gny_b, cv2_fuse_w, cv2_fuse_b)))
        h = dysnake_conv(x, p1)
        h = dysnake_conv(h, p2)
        return x + h

    def _gn(v, G=32, eps=1e-5):
        B_, C_, H_, W_ = v.shape
        g = v.reshape(B_, G, C_ // G, H_, W_)
        m = jnp.mean(g, axis=(2, 3, 4), keepdims=True)
        s = jnp.var(g, axis=(2, 3, 4), keepdims=True)
        return ((g - m) / jnp.sqrt(s + eps)).reshape(v.shape)

    def _ln_c(v, eps=1e-6):
        m = jnp.mean(v, axis=1, keepdims=True)
        s = jnp.var(v, axis=1, keepdims=True)
        return (v - m) / jnp.sqrt(s + eps)

    def _ln_t(v, eps=1e-5):
        m = jnp.mean(v, axis=-1, keepdims=True)
        s = jnp.var(v, axis=-1, keepdims=True)
        return (v - m) / jnp.sqrt(s + eps)

    def _to_tokens(v):
        B_, C_, H_, W_ = v.shape
        return v.reshape(B_, C_, H_ * W_).transpose(0, 2, 1)
    def _from_tokens(t, like):
        B_, C_, H_, W_ = like.shape
        return t.transpose(0, 2, 1).reshape(B_, C_, H_, W_)

    x = _L0_conv_ref(x, L0_conv_W_in, L0_conv_W_x, L0_conv_W_dt, L0_conv_b_dt, L0_conv_A_logs, L0_conv_Ds, L0_conv_W_out, L0_conv_gn_w, L0_conv_gn_b)
    x = _L1_conv_ref(x, L1_conv_cv1_conv0_w, L1_conv_cv1_conv0_b, L1_conv_cv1_offx_w, L1_conv_cv1_offx_b, L1_conv_cv1_dscx_w, L1_conv_cv1_dscx_b, L1_conv_cv1_gnx_g, L1_conv_cv1_gnx_b, L1_conv_cv1_offy_w, L1_conv_cv1_offy_b, L1_conv_cv1_dscy_w, L1_conv_cv1_dscy_b, L1_conv_cv1_gny_g, L1_conv_cv1_gny_b, L1_conv_cv1_fuse_w, L1_conv_cv1_fuse_b, L1_conv_cv2_conv0_w, L1_conv_cv2_conv0_b, L1_conv_cv2_offx_w, L1_conv_cv2_offx_b, L1_conv_cv2_dscx_w, L1_conv_cv2_dscx_b, L1_conv_cv2_gnx_g, L1_conv_cv2_gnx_b, L1_conv_cv2_offy_w, L1_conv_cv2_offy_b, L1_conv_cv2_dscy_w, L1_conv_cv2_dscy_b, L1_conv_cv2_gny_g, L1_conv_cv2_gny_b, L1_conv_cv2_fuse_w, L1_conv_cv2_fuse_b)
    return x


_drawn_inputs = setup_inputs


def setup_inputs(seed=0):
    import zlib

    import numpy as np

    out = dict(_drawn_inputs(seed))
    spreads = {'L0_conv_Ds': (1.0, 0.2),
     'L0_conv_gn_w': (1.0, 0.2),
     'L0_conv_gn_b': (0.0, 0.1),
     'L1_conv_cv1_gnx_g': (1.0, 0.2),
     'L1_conv_cv1_gnx_b': (0.0, 0.486),
     'L1_conv_cv1_gny_g': (1.0, 0.2),
     'L1_conv_cv1_gny_b': (0.0, 0.449),
     'L1_conv_cv2_gnx_g': (1.0, 0.2),
     'L1_conv_cv2_gnx_b': (0.0, 0.384),
     'L1_conv_cv2_gny_g': (1.0, 0.2),
     'L1_conv_cv2_gny_b': (0.0, 0.336)}
    factors = {'L0_conv_W_x': 64.0,
     'L0_conv_W_dt': 64.0,
     'L0_conv_b_dt': 64.0,
     'L0_conv_A_logs': 8.0,
     'L1_conv_cv1_conv0_b': 6.962,
     'L1_conv_cv1_offx_b': 28.978,
     'L1_conv_cv1_dscx_b': 8.0,
     'L1_conv_cv1_offy_b': 8.0,
     'L1_conv_cv1_dscy_b': 8.0,
     'L1_conv_cv1_fuse_b': 2.882,
     'L1_conv_cv2_conv0_b': 5.621,
     'L1_conv_cv2_offx_b': 5.853,
     'L1_conv_cv2_dscx_b': 4.299,
     'L1_conv_cv2_offy_b': 8.0,
     'L1_conv_cv2_dscy_b': 4.889,
     'L1_conv_cv2_fuse_b': 2.683}
    for name, (base, spread) in spreads.items():
        noise = np.random.default_rng([zlib.crc32(name.encode()), seed]).standard_normal(out[name].shape)
        drawn = base * np.exp(spread * noise) if base else spread * noise
        out[name] = jnp.asarray(drawn.astype(out[name].dtype))
    for name, factor in factors.items():
        out[name] = (out[name] * factor).astype(out[name].dtype)
    return out
```

```python
import concourse.bass as bass
from concourse import mybir
from contextlib import ExitStack


def two_layer_program(nc, w, out):
    F32 = mybir.dt.float32
    ALU = mybir.AluOpType
    ACT = mybir.ActivationFunctionType

    P = 128
    IMAGES, CH, H, W = 4, 256, 64, 64
    CC = CH // P
    QUADS, TOK = 4, 8
    TILE = 256
    TROWS = TILE // W
    TILES = H * W // TILE
    WIDE = 2 * TILE
    HALVES = 2
    GROUPS = 8
    GPH = GROUPS // HALVES
    EPS = 1e-5
    SMALL = 1.0 / 64
    ARENA = 29440
    RB = 8
    BLOCKS = H // RB
    PH, PW = H + 2, W + 2

    ctx = ExitStack()
    with ctx:
        def sb(name, shape, dt=F32):
            return ctx.enter_context(nc.sbuf_tensor(name, shape, dt))

        def ps(name, shape):
            return ctx.enter_context(nc.psum_tensor(name, shape, F32))

        def sem(name):
            return ctx.enter_context(nc.semaphore(name))

        w_in_x = sb("w_in_x", [P, HALVES, P])
        w_in_z = sb("w_in_z", [P, HALVES, P])
        w_dts = sb("w_dts", [P, HALVES, 2 * QUADS])
        w_dt = sb("w_dt", [2 * QUADS, HALVES, P])
        w_b = sb("w_b", [P, QUADS, HALVES, P])
        w_c = sb("w_c", [P, QUADS, HALVES, P])
        w_out = sb("w_out", [P, HALVES, P])
        spread = sb("spread", [P, QUADS, GPH, P])
        gather = sb("gather", [P, GPH, 32])
        a_neg = sb("a_neg", [P, GROUPS])
        ds2 = sb("ds2", [P, HALVES])
        bdt2 = sb("bdt2", [P, HALVES])
        gn0 = sb("gn0", [P, 2, CC])
        same64 = sb("same64", [P, P])

        img = sb("img", [P, CC, H + 2, W + 2])
        xt = sb("xt", [P, 2, CC, TILE])
        th = sb("th", [P, RB * W])
        wx = sb("wx", [P, 4224])
        c1_off = sb("c1_off", [P, CC, 3, 96])
        c2_off = sb("c2_off", [P, 3, 96])
        c2_dsc = sb("c2_dsc", [P, 6, 2 * P])
        pick = sb("pick", [P, 4, P])
        same4 = sb("same4", [P, P])
        v1 = sb("v1", [P, 8])
        v2 = sb("v2", [P, 16])
        off_b = sb("off_b", [4, 2])
        st1 = sb("st1", [P, 4, BLOCKS, 6])
        st0 = sb("st0", [P, CC, TILES, 6])
        gns = sb("gns", [P, 8, 4])
        mv = sb("mv", [P, 4, 2])
        eps = sb("eps", [P, 1])
        logc = sb("logc", [P, 4])

        arena = sb("arena", [P, ARENA])
        cursor = [0]

        def carve(*shape, at=None):
            n = 1
            for d in shape:
                n *= d
            o = cursor[0] if at is None else at
            cursor[0] = o + n
            assert cursor[0] <= ARENA, cursor[0]
            names = "abcd"[:len(shape)]
            flat = arena[:, o:o + n]
            if len(shape) == 1:
                return flat
            dims = {c: d for c, d in zip(names, shape)}
            return flat.rearrange("p (" + " ".join(names) + ") -> p " + " ".join(names), **dims)

        dec = carve(2, TOK, TILE)
        g = carve(TOK, TILE)
        hh = carve(2 * TOK, TILE)
        wc = carve(TOK, TILE)
        brep = carve(TOK, TILE)
        crep = carve(TOK, TILE)
        u = carve(2, HALVES, WIDE)
        gz = carve(2, HALVES, WIDE)
        delta = carve(2, HALVES, WIDE)
        du = carve(2, HALVES, WIDE)
        sp_e = carve(HALVES, WIDE)
        sp_u = carve(HALVES, WIDE)
        dt8 = carve(WIDE)
        yg = carve(HALVES, WIDE)
        x_old = carve(CC, H * W, at=0)

        PIX = RB * W
        pp = carve(4, PH, PW, at=0)
        m1 = carve(2, H * W)
        df = carve(2, 9 * W)
        tm = carve(4, PIX)
        at1 = tm[:, 0:2, :]
        hz = carve(PH, PW, at=0)
        hr = carve(PH, PW)
        m2 = carve(4, H * W)
        dv = carve(9, PW)
        dh = carve(10, PW - 1)
        sm = carve(4, PIX)
        tn = carve(2, PIX)
        at2 = carve(2, 2, PIX, at=2 * PH * PW + 4 * H * W)
        ht = carve(2, 2, PIX)
        acc = xt[:, 0, :, :].rearrange("p c n -> p (c n)")
        c1_conv = wx[:, 0:2304].rearrange("p (c t o) -> p c t o", c=CC, t=9)
        c1_dsc = wx[:, 2304:3840].rearrange("p (c k o) -> p c k o", c=CC, k=6)
        c1_fuse = wx[:, 3840:4224].rearrange("p (k o) -> p k o", k=3)
        c2_conv = wx[:, 0:2304].rearrange("p (t o) -> p t o", t=9)
        c2_fuse = wx[:, 2304:3840].rearrange("p (k o) -> p k o", k=6)

        p_dec = ps("p_dec", [P, 2, 512])
        p_du = ps("p_du", [P, 4, 512])
        p_y = ps("p_y", [P, 512])
        p_misc = ps("p_misc", [P, 512])

        weights = sem("weights")
        cleared = sem("cleared")
        consts = sem("consts")
        a_exp = sem("a_exp")
        x_in = [sem("x_in0"), sem("x_in1")]
        misc_full = sem("misc_full")
        misc_free = sem("misc_free")
        dec_mm = sem("dec_mm")
        exp_done = sem("exp_done")
        du_mm = sem("du_mm")
        g_done = sem("g_done")
        a_used = sem("a_used")
        w_ready = sem("w_ready")
        y_done = sem("y_done")
        soft_act = sem("soft_act")
        delta_ok = sem("delta_ok")
        yg_ok = sem("yg_ok")
        vec = sem("vec")
        gn_vec = sem("gn_vec")
        gn_mm = sem("gn_mm")
        gn_act = sem("gn_act")
        x1_mul = sem("x1_mul")
        x1_ok = sem("x1_ok")
        x_again = sem("x_again")
        stored = [sem("stored0"), sem("stored1")]
        img_free = sem("img_free")

        for_layer_1 = """pp_mm pp_ev pads off_mm off_sum tanh_ok bc_mm bc_used cen_mm cen_used conv_mm conv_ev
            relu_ok fuse_mm fuse_ev h1_ok hz_clear o2_mm o2_ev s_ok vec1 bn1 a2_mm a2_ev relu2_ok f2_mm h2_ok res_ok
            w1_in w2_in""".split()
        (pp_mm, pp_ev, pads, off_mm, off_sum, tanh_ok, bc_mm, bc_used, cen_mm, cen_used, conv_mm, conv_ev,
         relu_ok, fuse_mm, fuse_ev, h1_ok, hz_clear, o2_mm, o2_ev, s_ok, vec1, bn1, a2_mm, a2_ev, relu2_ok,
         f2_mm, h2_ok, res_ok, w1_in, w2_in) = [sem(n) for n in for_layer_1]

        xv = w["x"].rearrange("b (c p) h w -> b p c (h w)", p=P)
        outv = out.rearrange("b (c p) h w -> b p c (h w)", p=P)

        def plane(tok):
            return 2 * (tok % QUADS) + tok // QUADS

        def pair(t, first, second):
            a = t[:, first, :]
            return bass.AP(a.tensor, a.offset, [a.ap[0], [(second - first) * TILE, 2], a.ap[-1]])

        LEAD, PER = 11, 16
        DSTEPS = 7
        NORM_AT = [0, CC + 9, 2 * CC + 18]
        NORM_VEC = NORM_AT[2] + 4 + 9
        NORMS = 3
        VPER = GROUPS * (4 * (TOK - 2) + 2) + 2 + DSTEPS + 2
        PAIRS = TILES // 2

        class Tile:
            def __init__(self, base, k, buf, first=False, last=False):
                self.base, self.k, self.buf, self.first, self.last = base, k, buf, first, last
                self.misc = LEAD if first else LEAD - 1
                self.vec = DSTEPS if first else DSTEPS - 3

            def at(self, per_tile, more):
                return self.base * per_tile + (self.k * per_tile + more)

        def walk(eng, image, tile_steps):
            base = image * TILES
            for k in range(2):
                tile_steps(Tile(base, k, k, first=k == 0), k)
            with eng.Fori(1, PAIRS - 1) as tp:
                for k in range(2):
                    tile_steps(Tile(image * TILES + tp * 2, k, k), tp * 2 + k)
            for k in range(2):
                tile_steps(Tile(base, TILES - 2 + k, k, last=k == 1), TILES - 2 + k)

        PADS = 2 * BLOCKS + 2
        V1, V2 = 20, 12
        VEC1 = (V1 + V2) * BLOCKS
        BNS = 6 * BLOCKS
        H1 = 3 * BLOCKS + 2
        CENTRE = [p_du[:, 3, :], p_y[:]]

        def rows(rb, shift):
            return slice(rb * RB + shift, rb * RB + shift + RB) if isinstance(rb, int) else bass.ds(rb * RB + shift, RB)

        def rows9(rb, shift):
            at = rb * RB + shift
            return slice(at, at + RB + 1) if isinstance(rb, int) else bass.ds(at, RB + 1)

        def rows10(rb):
            return slice(rb * RB, rb * RB + RB + 2) if isinstance(rb, int) else bass.ds(rb * RB, RB + 2)

        def stat(c, rb):
            return st1[:, c, rb, :] if isinstance(rb, int) else st1[:, c, bass.ds(rb, 1), :]

        def cols(rb):
            return slice(rb * PIX, rb * PIX + PIX) if isinstance(rb, int) else bass.ds(rb * PIX, PIX)

        def grid(a):
            return a.rearrange("p (h w) -> p h w", w=W)

        block = ctx.enter_context(nc.Block())

        @block.sync
        def _(sp):
            sp.wait_ge(cleared, 9)
            for h in range(HALVES):
                for q in range(QUADS):
                    r = slice(32 * q, 32 * q + 32)
                    hs = slice(32 * h, 32 * h + 32)
                    sp.dma_start(w_in_x[r, h, r], w["W_in"][:, hs]).then_inc(weights, 16)
                    sp.dma_start(w_in_z[r, h, r], w["W_in"][:, 64 + 32 * h:96 + 32 * h]).then_inc(weights, 16)
                    sp.dma_start(w_out[r, h, r], w["W_out"][hs, :]).then_inc(weights, 16)
                    sp.dma_start(w_dts[r, h, 2 * q:2 * q + 2], w["W_x"][hs, 0:2]).then_inc(weights, 16)
                    sp.dma_start(w_dt[2 * q:2 * q + 2, h, r], w["W_dt"][:, hs]).then_inc(weights, 16)
                    sp.dma_start(w_b[r, q, h, :], w["W_B"][hs, :]).then_inc(weights, 16)
                    sp.dma_start(w_c[r, q, h, :], w["W_C"][hs, :]).then_inc(weights, 16)
                    sp.dma_start(ds2[r, h:h + 1], w["Ds"][hs, :]).then_inc(weights, 16)
                    sp.dma_start(bdt2[r, h:h + 1], w["b_dt"][hs, :]).then_inc(weights, 16)
            sp.dma_start(a_neg[:], w["A_logs"]).then_inc(weights, 16)
            sp.dma_start(spread[:], w["spread"]).then_inc(weights, 16)
            sp.dma_start(gather[:], w["gather"]).then_inc(weights, 16)
            sp.dma_start(same64[:], w["same64"]).then_inc(weights, 16)
            sp.dma_start(gn0[:, 0, :], w["gn_w"]).then_inc(weights, 16)
            sp.dma_start(gn0[:, 1, :], w["gn_b"]).then_inc(weights, 16)

            for t, name in ((c1_off, "off1"), (c2_off, "off2"), (c2_dsc, "dsc2"), (pick, "pick"), (same4, "same4"),
                            (v1, "v1"), (v2, "v2"), (off_b, "off_b")):
                sp.dma_start(t[:], w[name]).then_inc(weights, 16)
            with sp.Fori(0, IMAGES) as image:
                with sp.Fori(0, PAIRS) as tp:
                    for k in range(2):
                        sp.wait_ge(misc_full, (image * TILES + tp * 2) * PER + (k * PER + 7))
                        sp.dma_start(xt[:, k, :, :], xv[image, :, :, bass.ds(tp * WIDE + k * TILE, TILE)]).then_inc(x_in[k], 16)
                sp.dma_start(wx[:], w["block1"]).then_inc(w1_in, 16)
                sp.wait_ge(w_ready, image * (TILES * GROUPS) + (TILES * GROUPS + 1))
                for c in range(CC):
                    sp.dma_start(x_old[:, c, :], xv[image, :, c, :]).then_inc(x_again, 16)
                sp.wait_ge(fuse_mm, image * BLOCKS + (BLOCKS + 2))
                sp.dma_start(wx[:, 0:3840], w["block2"]).then_inc(w2_in, 16)
                with sp.Fori(0, BLOCKS // 2) as r:
                    for k in range(2):
                        sp.wait_ge(res_ok, image * (2 * BLOCKS) + r * 4 + (2 * k + 2))
                        sp.dma_start(outv[image, :, :, bass.ds(r * (2 * PIX) + k * PIX, PIX)],
                                     ht[:, k, :, :]).then_inc(stored[k], 16)
                for k in range(2):
                    sp.wait_ge(stored[k], image * (8 * BLOCKS) + (8 * BLOCKS + 16))
                sp.sem_inc(img_free, 1)

        NWEIGHTS = 16 * (HALVES * QUADS * 9 + 6 + 8)

        @block.gpsimd
        def _(pool):
            for t in (w_in_x, w_in_z, w_out, w_dts, w_dt, w_b, w_c, img, th):
                nc.gpsimd.memset(t[:], 0.0).then_inc(cleared, 1)

        @block.tensor
        def _(pe):
            mm = nc.tensor.matmul
            QS = [slice(32 * q, 32 * q + 32) for q in range(QUADS)]

            def misc(T):
                pe.wait_ge(misc_free, T.at(PER, T.misc + 1))
                T.misc += 1

            def inner(T, buf, h):
                misc(T)
                mm(p_misc[:], w_in_x[:, h, :], xt[:, buf, :, :], start=True, stop=True).then_inc(misc_full, 1)

            def gates(T, buf, h):
                misc(T)
                i = mm(p_misc[:], w_in_z[:, h, :], xt[:, buf, :, :], start=True, stop=True)
                i.then_inc(misc_full, 1)

            def step_sizes(T, buf):
                misc(T)
                for h in range(HALVES):
                    i = mm(p_misc[0:8, :], w_dts[:, h, :], u[:, buf, h, :], start=h == 0, stop=h == 1)
                i.then_inc(misc_full, 1)

            def step_sizes_out(T, h):
                misc(T)
                mm(p_misc[:], w_dt[:, h, :], dt8[0:8, :], start=True, stop=True).then_inc(misc_full, 1)

            def repeat(T, buf, wt, q):
                misc(T)
                for h in range(HALVES):
                    i = mm(p_misc[:], wt[:, q, h, :], u[:, buf, h, :], start=h == 0, stop=h == 1)
                i.then_inc(misc_full, 1)

            def outputs(T):
                pe.wait_ge(yg_ok, T.at(HALVES, 0))
                misc(T)
                for h in range(HALVES):
                    i = mm(p_misc[:], w_out[:, h, :], yg[:, h, :], start=h == 0, stop=h == 1)
                i.then_inc(misc_full, 1)

            def spread_delta(T, buf, gi, more):
                for q in range(QUADS):
                    pe.wait_ge(exp_done, T.at(4 * GROUPS, 4 * more + q + 1))
                    mm(p_dec[:, q % 2, :], spread[:, q, gi % GPH, :], delta[:, buf, gi // GPH, :],
                       start=True, stop=True).then_inc(dec_mm, 1)

            def spread_du(T, buf, gi, more):
                for q in range(QUADS):
                    if q % 2 == 0:
                        pe.wait_ge(g_done, T.at(2 * GROUPS, 2 * more + q // 2 + 1))
                    i = mm(p_du[:, q, :], spread[:, q, gi % GPH, :], du[:, buf, gi // GPH, :],
                           start=True, stop=True)
                    if q % 2:
                        i.then_inc(du_mm, 1)

            def gather_y(T, gi):
                pe.wait_ge(w_ready, T.at(GROUPS, gi + 2))
                for q in range(QUADS):
                    i = mm(p_y[QS[q], :], gather[:, gi % GPH, :], wc[:, 2 * q:2 * q + 2, :],
                           start=gi % GPH == 0, stop=gi % GPH == GPH - 1)
                i.then_inc(y_done, 1)

            def tile_steps(T, t):
                b, nb = T.buf, 1 - T.buf
                for gi in range(GROUPS):
                    more, nxt = gi + 1, (b, gi + 1)
                    slots = []
                    if gi == 0:
                        slots = [lambda q=q: repeat(T, b, w_c, q) for q in range(4)]
                    if gi == 1 and not T.last:
                        slots.append(lambda: (pe.wait_ge(x_in[nb], T.at(8, 24 if b else 16)), inner(T, nb, 0)))
                    if gi == 1 and not T.first:
                        slots.append(lambda: outputs(T))
                    if not T.last:
                        if gi == 1:
                            slots.append(lambda: inner(T, nb, 1))
                        if gi == 2:
                            slots += [lambda: step_sizes(T, nb), lambda: step_sizes_out(T, 0)]
                        if gi == 3:
                            slots += [lambda: step_sizes_out(T, 1)]
                        if gi == 4:
                            slots += [lambda: None, lambda: gates(T, nb, 0), lambda: gates(T, nb, 1)]
                        if gi == 5:
                            slots += [lambda: None]
                        if gi == 7:
                            slots = [lambda q=q: repeat(T, nb, w_b, q) for q in range(4)]
                            nxt = (nb, 0)
                    slots += [lambda: None] * 4
                    slots[0]()
                    if gi < 7 or not T.last:
                        if gi == 7:
                            pe.wait_ge(delta_ok, T.at(1, 2))
                        spread_delta(T, nxt[0], nxt[1], more)
                    slots[1]()
                    if gi < 7 or not T.last:
                        spread_du(T, nxt[0], nxt[1], more)
                    slots[2]()
                    slots[3]()
                    gather_y(T, gi)

            def lead(T):
                pe.wait_ge(x_in[0], T.at(8, 16))
                T.misc = 0
                inner(T, 0, 0)
                inner(T, 0, 1)
                step_sizes(T, 0)
                step_sizes_out(T, 0)
                step_sizes_out(T, 1)
                gates(T, 0, 0)
                gates(T, 0, 1)
                for q in range(4):
                    repeat(T, 0, w_b, q)
                pe.wait_ge(delta_ok, T.at(1, 1))
                spread_delta(T, 0, 0, 0)
                spread_du(T, 0, 0, 0)

            def norm_matmuls(image, use, cols, same):
                pe.wait_ge(gn_vec, image * NORM_VEC + (NORM_AT[use] + cols))
                mm(p_misc[:, 0:cols], same[:], mv[:, 0:cols, 0], start=True, stop=True).then_inc(gn_mm, 1)
                pe.wait_ge(gn_vec, image * NORM_VEC + (NORM_AT[use] + cols + 4))
                mm(p_misc[:, 0:cols], same[:], gns[:, 0, 0:cols], start=True, stop=True).then_inc(gn_mm, 1)

            def side(n, rb):
                return [lambda i=i: side_tap(n, rb, i) for i in range(4)]

            def side_tap(n, rb, i):
                pe.wait_ge(pp_ev, n * 4 + (i + 1))
                for c in range(CC):
                    k = mm(p_dec[:, i % 2, :], c1_dsc[:, c, 3 * (i // 2) + 2 * (i % 2), :],
                           img[:, c, rows(rb, 1), 1:W + 1], start=c == 0, stop=c == CC - 1)
                k.then_inc(pp_mm, 1)

            def offsets(n2, rb, wt, src):
                pe.wait_ge(off_sum, n2 + 1)
                parts = [(c, dy) for c in range(len(wt)) for dy in range(3)]
                for c, dy in parts:
                    k = mm(p_du[0:96, 0, :], wt[c][:, dy, :], src[c][:, rows(rb, dy), 1:W + 1],
                           start=(c, dy) == parts[0], stop=(c, dy) == parts[-1])
                k.then_inc(off_mm, 1)

            def bend(n2, i):
                if i == 0:
                    pe.wait_ge(tanh_ok, n2 + 2)
                pe.wait_ge(bc_used, n2 * 4 + (i + 1))
                mm(p_du[:, 1 + i % 2, :], pick[:, i, :], th[:], start=True, stop=True).then_inc(bc_mm, 1)

            def centre(n, rb, m):
                pe.wait_ge(cen_used, n * 2 + (m + 1))
                for c in range(CC):
                    k = mm(CENTRE[m], c1_dsc[:, c, 3 * m + 1, :], img[:, c, rows(rb, 1), 1:W + 1],
                           start=c == 0, stop=c == CC - 1)
                k.then_inc(cen_mm, 1)

            OFF1 = ([c1_off[:, c, :, :] for c in range(CC)], [img[:, c, :, :] for c in range(CC)])
            OFF2 = ([c2_off[:, :, :]], [hz])

            def block1_sample(image, rb, ahead, nxt):
                n, n2 = image * BLOCKS + rb, image * (2 * BLOCKS) + rb
                later = side(n + 2, rb + 2) if ahead else [lambda: None] * 4
                bend(n2, 0)
                bend(n2, 1)
                if nxt:
                    offsets(n2 + 1, rb + 1, *OFF1)
                centre(n, rb, 0)
                centre(n, rb, 1)
                later[0]()
                later[1]()
                bend(n2, 2)
                later[2]()
                later[3]()
                bend(n2, 3)

            def conv1(n, rb, k):
                pe.wait_ge(conv_ev, n + 1)
                for c in range(CC):
                    for tap in range(9):
                        i = mm(p_dec[:, k, :], c1_conv[:, c, tap, :],
                               img[:, c, rows(rb, tap // 3), tap % 3:tap % 3 + W],
                               start=c == 0 and tap == 0, stop=c == CC - 1 and tap == 8)
                i.then_inc(conv_mm, 1)

            def fuse1(n, rb, k):
                pe.wait_ge(conv_ev, n + 3)
                pe.wait_ge(relu_ok, n * 2 + 2)
                pe.wait_ge(fuse_ev, n + 1)
                mm(p_du[:, k, :], c1_fuse[:, 0, :], at1[:, k, :], start=True, stop=False)
                mm(p_du[:, k, :], c1_fuse[:, 1, :], m1[:, 0, cols(rb)], start=False, stop=False)
                mm(p_du[:, k, :], c1_fuse[:, 2, :], m1[:, 1, cols(rb)], start=False, stop=True).then_inc(fuse_mm, 1)

            def block2_out(n, rb, m):
                pe.wait_ge(s_ok, n * 4 + (2 * m + 2))
                for o in range(2):
                    pe.wait_ge(o2_ev, n * 4 + (2 * m + o + 1))
                    os = slice(P * o, P * o + P)
                    mm(p_dec[:, o, :], c2_dsc[:, 3 * m + 1, os], hz[:, rows(rb, 1), 1:W + 1], start=True, stop=False)
                    mm(p_dec[:, o, :], c2_dsc[:, 3 * m, os], sm[:, 2 * m, :], start=False, stop=False)
                    mm(p_dec[:, o, :], c2_dsc[:, 3 * m + 2, os], sm[:, 2 * m + 1, :],
                       start=False, stop=True).then_inc(o2_mm, 1)

            def block2_sample(image, rb, first, nxt):
                n, n2 = image * BLOCKS + rb, image * (2 * BLOCKS) + (BLOCKS + rb)
                bend(n2, 0)
                bend(n2, 1)
                if not first:
                    block2_out(n - 1, rb - 1, 1)
                if nxt:
                    offsets(n2 + 1, rb + 1, *OFF2)
                bend(n2, 2)
                bend(n2, 3)
                block2_out(n, rb, 0)

            def conv2(n, rb, m):
                pe.wait_ge(a2_ev, n * 2 + (m + 1))
                for tap in range(9):
                    i = mm(p_dec[:, m, :], c2_conv[:, tap, P * m:P * m + P],
                           hz[:, rows(rb, tap // 3), tap % 3:tap % 3 + W], start=tap == 0, stop=tap == 8)
                i.then_inc(a2_mm, 1)

            def fuse2(n, rb, k, o):
                if o == 0:
                    pe.wait_ge(a2_ev, n * 2 + 4)
                    pe.wait_ge(relu2_ok, n * 4 + 4)
                pe.wait_ge(h2_ok, n * 2 + (o + 1))
                os = slice(P * o, P * o + P)
                for c in range(2):
                    mm(p_du[:, o, :], c2_fuse[:, c, os], at2[:, k, c, :], start=c == 0, stop=False)
                for c in range(4):
                    i = mm(p_du[:, o, :], c2_fuse[:, 2 + c, os], m2[:, c, cols(rb)], start=False, stop=c == 3)
                i.then_inc(f2_mm, 1)

            def layer1(image):
                pe.wait_ge(x1_ok, image * CC + CC)
                pe.wait_ge(w1_in, image * 16 + 16)
                n0, n20 = image * BLOCKS, image * (2 * BLOCKS)
                for rb in range(2):
                    for tap in side(n0 + rb, rb):
                        tap()
                offsets(n20, 0, *OFF1)
                with pe.Fori(0, BLOCKS - 2) as rb:
                    block1_sample(image, rb, True, True)
                block1_sample(image, BLOCKS - 2, False, True)
                block1_sample(image, BLOCKS - 1, False, False)
                conv1(n0, 0, 0)
                norm_matmuls(image, 1, 2, same4)
                with pe.Fori(0, BLOCKS // 2 - 1) as r:
                    for k in range(2):
                        conv1(n0 + r * 2 + (k + 1), r * 2 + (k + 1), 1 - k)
                        fuse1(n0 + r * 2 + k, r * 2 + k, k)
                conv1(n0 + (BLOCKS - 1), BLOCKS - 1, 1)
                fuse1(n0 + (BLOCKS - 2), BLOCKS - 2, 0)
                fuse1(n0 + (BLOCKS - 1), BLOCKS - 1, 1)
                pe.wait_ge(fuse_ev, n0 + (BLOCKS + 2))
                pe.wait_ge(hz_clear, image * 4 + 4)
                offsets(n20 + BLOCKS, 0, *OFF2)
                block2_sample(image, 0, True, True)
                with pe.Fori(1, BLOCKS - 1) as rb:
                    block2_sample(image, rb, False, True)
                block2_sample(image, BLOCKS - 1, False, False)
                block2_out(n0 + (BLOCKS - 1), BLOCKS - 1, 1)
                pe.wait_ge(w2_in, image * 16 + 16)
                pe.wait_ge(o2_ev, n0 * 4 + (4 * BLOCKS + 2))
                conv2(n0, 0, 0)
                norm_matmuls(image, 2, 4, same4)
                conv2(n0, 0, 1)
                with pe.Fori(0, BLOCKS // 2 - 1) as r:
                    for k in range(2):
                        for m in range(2):
                            conv2(n0 + r * 2 + (k + 1), r * 2 + (k + 1), m)
                        for m in range(2):
                            fuse2(n0 + r * 2 + k, r * 2 + k, k, m)
                for m in range(2):
                    conv2(n0 + (BLOCKS - 1), BLOCKS - 1, m)
                for k in range(2):
                    for m in range(2):
                        fuse2(n0 + (BLOCKS - 2 + k), BLOCKS - 2 + k, k, m)

            for s, n in ((pp_ev, 2), (off_sum, 1), (bc_used, 2), (cen_used, 2), (conv_ev, 2), (fuse_ev, 2), (o2_ev, 2),
                         (a2_ev, 2), (h2_ok, 2)):
                pe.sem_inc(s, n)
            pe.sem_inc(exp_done, 2)
            pe.sem_inc(g_done, 2)
            pe.sem_inc(misc_free, 1)
            pe.sem_inc(misc_full, 2 * PER)
            pe.wait_ge(weights, NWEIGHTS)
            with pe.Fori(0, IMAGES) as image:
                lead(Tile(image * TILES, 0, 0))
                walk(pe, image, tile_steps)
                T = Tile(image * TILES, TILES, 0)
                T.misc = -1
                outputs(T)
                norm_matmuls(image, 0, CC, same64)
                layer1(image)

        @block.scalar
        def _(act):
            fn = nc.scalar.activation

            def full(T):
                act.wait_ge(misc_full, T.at(PER, T.misc + 1 + 2 * PER))
                T.misc += 1

            def inner(T, buf, h):
                full(T)
                fn(u[:, buf, h, :], p_misc[:], ACT.Identity).then_inc(misc_free, 1)

            def gates(T, buf, h):
                full(T)
                i = fn(gz[:, buf, h, :], p_misc[:], ACT.Gelu)
                i.then_inc(misc_free, 1)

            def step_sizes(T):
                full(T)
                fn(dt8[0:8, :], p_misc[0:8, :], ACT.Identity).then_inc(misc_free, 1)

            def soft_in(T, buf, h):
                full(T)
                fn(delta[:, buf, h, :], p_misc[:], ACT.Identity, bias=bdt2[:, h:h + 1])
                fn(sp_e[:, h, :], p_misc[:], ACT.Abs, bias=bdt2[:, h:h + 1]).then_inc(misc_free, 1)

            def softplus(T, buf, more):
                act.wait_ge(misc_free, T.at(PER, T.misc + 1))
                fn(sp_e[:], sp_e[:], ACT.Exp, scale=-1.0).then_inc(soft_act, 1)
                act.wait_ge(soft_act, T.at(3, 3 * more + 1))
                fn(sp_u[:], sp_e[:], ACT.Relu, bias=logc[:, 0:1]).then_inc(soft_act, 1)
                act.wait_ge(soft_act, T.at(3, 3 * more + 2))
                fn(du[:, buf, :, :], sp_u[:], ACT.Ln, bias=logc[:, 1:2]).then_inc(soft_act, 1)

            def repeat(T, dst, q, done):
                full(T)
                fn(dst[:, 2 * q:2 * q + 2, :], p_misc[:].rearrange("p (a b) -> p a b", a=2), ACT.Identity).then_inc(misc_free, 1)

            def outputs(T, t):
                full(T)
                rows = bass.ds(t * TROWS - (TROWS - 1), TROWS)
                fn(img[:, :, rows, 1:W + 1], p_misc[:].rearrange("p (c r w) -> p c r w", c=CC, w=W),
                   ACT.Identity).then_inc(misc_free, 1)

            def exps(T, gi, more):
                act.wait_ge(a_used, T.at(GROUPS, more + 1))
                for q in range(QUADS):
                    act.wait_ge(dec_mm, T.at(4 * GROUPS, 4 * more + q + 1))
                    fn(dec[:, gi % 2, 2 * q:2 * q + 2, :], p_dec[:, q % 2, :].rearrange("p (a b) -> p a b", a=2),
                       ACT.Exp, scale=a_neg[:, gi:gi + 1]).then_inc(exp_done, 1)

            def tile_steps(T, t):
                b, nb = T.buf, 1 - T.buf
                for gi in range(GROUPS):
                    more = gi + 1
                    if gi == 0:
                        act.wait_ge(w_ready, T.at(GROUPS, 1))
                        repeat(T, crep, 0, None)
                    if gi == 1 and not T.last:
                        if not T.first:
                            act.wait_ge(yg_ok, T.at(HALVES, 0))
                        inner(T, nb, 0)
                    if gi == 1 and T.last:
                        outputs(T, t)
                    if gi == 2 and not T.last:
                        step_sizes(T)
                    if gi == 3 and not T.last:
                        soft_in(T, nb, 1)
                    if gi == 7 and not T.last:
                        act.wait_ge(g_done, T.at(2 * GROUPS, 2 * gi + 4))
                        repeat(T, brep, 0, None)
                    if gi < 7 or not T.last:
                        exps(T, (gi + 1) % GROUPS, more)
                    if gi == 0:
                        for q in range(1, 4):
                            repeat(T, crep, q, None)
                    if gi == 1 and not T.last:
                        if not T.first:
                            outputs(T, t)
                        inner(T, nb, 1)
                    if gi == 2 and not T.last:
                        soft_in(T, nb, 0)
                    if gi == 3 and not T.last:
                        softplus(T, nb, 1)
                    if gi == 4 and not T.last:
                        gates(T, nb, 0)
                        gates(T, nb, 1)
                    if gi == 7 and not T.last:
                        for q in range(1, 4):
                            repeat(T, brep, q, None)

            def lead(T):
                T.misc = 0
                inner(T, 0, 0)
                inner(T, 0, 1)
                step_sizes(T)
                soft_in(T, 0, 0)
                soft_in(T, 0, 1)
                softplus(T, 0, 0)
                gates(T, 0, 0)
                gates(T, 0, 1)
                for q in range(4):
                    repeat(T, brep, q, None)
                exps(T, 0, 0)

            def norm_root(image, use, cols):
                act.wait_ge(gn_vec, image * NORM_VEC + (NORM_AT[use] + cols + 5))
                fn(gns[:, 3, 0:cols], gns[:, 2, 0:cols], ACT.Sqrt, bias=eps[:]).then_inc(gn_act, 1)

            def tap_out(n, rb, i):
                act.wait_ge(pp_mm, n * 4 + (i + 1))
                fn(pp[:, i, rows(rb, 1), 1:W + 1], grid(p_dec[:, i % 2, :]), ACT.Identity).then_inc(pp_ev, 1)

            def tap_edges(n, rb):
                act.wait_ge(pp_ev, n * 4 + 6)
                for to, at in ((0, 1), (PW - 1, W)):
                    fn(pp[:, :, rows(rb, 1), to:to + 1], pp[:, :, rows(rb, 1), at:at + 1], ACT.Identity).then_inc(pads, 1)

            def tap_edge_rows(image, to, at, count):
                act.wait_ge(pads, image * PADS + count)
                fn(pp[:, :, to, :], pp[:, :, at, :], ACT.Identity).then_inc(pads, 1)

            def bends(n2, block):
                act.wait_ge(off_sum, n2 + 2)
                act.wait_ge(bc_mm, n2 * 4 + 4)
                fn(th[0:4, :], acc[0:4, :], ACT.Tanh, bias=off_b[:, block:block + 1]).then_inc(tanh_ok, 1)

            def block1_sample(image, rb, ahead, nxt):
                n, n2 = image * BLOCKS + rb, image * (2 * BLOCKS) + rb
                if ahead:
                    for i in range(4):
                        tap_out(n + 2, rb + 2, i)
                    tap_edges(n + 2, rb + 2)
                if nxt:
                    bends(n2 + 1, 0)

            def conv1(n, k):
                act.wait_ge(conv_mm, n + 1)
                act.wait_ge(fuse_mm, n + 1)
                fn(at1[:, k, :], p_dec[:, k, :], ACT.Silu, bias=v1[:, 0:1]).then_inc(conv_ev, 1)

            def relu1(rb):
                for m in range(2):
                    fn(m1[:, m, cols(rb)], m1[:, m, cols(rb)], ACT.Relu,
                       scale=gns[:, 4, m:m + 1], bias=gns[:, 5, m:m + 1]).then_inc(relu_ok, 1)

            def fuse1(n, rb, k):
                act.wait_ge(fuse_mm, n + 3)
                fn(hz[:, rows(rb, 1), 1:W + 1], grid(p_du[:, k, :]), ACT.Silu, bias=v1[:, 7:8]).then_inc(fuse_ev, 1)

            def block2_out(n, rb, m):
                for o in range(2):
                    act.wait_ge(o2_mm, n * 4 + (2 * m + o + 5))
                    fn(m2[:, 2 * m + o, cols(rb)], p_dec[:, o, :], ACT.Identity,
                       bias=v2[:, 2 + 2 * m + o:3 + 2 * m + o]).then_inc(o2_ev, 1)

            def block2_sample(image, rb, first, nxt):
                n, n2 = image * BLOCKS + rb, image * (2 * BLOCKS) + (BLOCKS + rb)
                if not first:
                    block2_out(n - 1, rb - 1, 1)
                if nxt:
                    bends(n2 + 1, 1)
                block2_out(n, rb, 0)

            def conv2(n, k, m):
                act.wait_ge(a2_mm, n * 2 + (m + 1))
                act.wait_ge(f2_mm, n * 2 + 2)
                fn(at2[:, k, m, :], p_dec[:, m, :], ACT.Silu, bias=v2[:, m:m + 1]).then_inc(a2_ev, 1)

            def relu2(rb):
                for c in range(4):
                    fn(m2[:, c, cols(rb)], m2[:, c, cols(rb)], ACT.Relu,
                       scale=gns[:, 4, c:c + 1], bias=gns[:, 5, c:c + 1]).then_inc(relu2_ok, 1)

            def fuse2(n, k, o, half):
                act.wait_ge(f2_mm, n * 2 + (o + 5))
                if o == 0:
                    act.wait_ge(stored[k], half * 16 + 16)
                fn(ht[:, k, o, :], p_du[:, o, :], ACT.Silu, bias=v2[:, 14 + o:15 + o]).then_inc(h2_ok, 1)

            def normed(image, use, cols):
                act.wait_ge(gn_vec, image * NORM_VEC + (NORM_AT[use] + cols + 9))

            def layer1(image):
                n0, n20, half0 = image * BLOCKS, image * (2 * BLOCKS), image * (BLOCKS // 2)
                for rb in range(2):
                    for i in range(4):
                        tap_out(n0 + rb, rb, i)
                    tap_edges(n0 + rb, rb)
                    if rb == 0:
                        tap_edge_rows(image, 0, 1, 2)
                bends(n20, 0)
                with act.Fori(0, BLOCKS - 2) as rb:
                    block1_sample(image, rb, True, True)
                tap_edge_rows(image, PH - 1, H, PADS - 1)
                block1_sample(image, BLOCKS - 2, False, True)
                act.wait_ge(gn_vec, image * NORM_VEC + (NORM_AT[1] + 1))
                conv1(n0, 0)
                norm_root(image, 1, 2)
                normed(image, 1, 2)
                relu1(0)
                with act.Fori(0, BLOCKS // 2 - 1) as r:
                    for k in range(2):
                        conv1(n0 + r * 2 + (k + 1), 1 - k)
                        relu1(r * 2 + (k + 1))
                        fuse1(n0 + r * 2 + k, r * 2 + k, k)
                conv1(n0 + (BLOCKS - 1), 1)
                relu1(BLOCKS - 1)
                fuse1(n0 + (BLOCKS - 2), BLOCKS - 2, 0)
                fuse1(n0 + (BLOCKS - 1), BLOCKS - 1, 1)
                bends(n20 + BLOCKS, 1)
                block2_sample(image, 0, True, True)
                with act.Fori(1, BLOCKS - 1) as rb:
                    block2_sample(image, rb, False, True)
                block2_sample(image, BLOCKS - 1, False, False)
                block2_out(n0 + (BLOCKS - 1), BLOCKS - 1, 1)
                act.wait_ge(gn_vec, image * NORM_VEC + (NORM_AT[2] + 1))
                conv2(n0, 0, 0)
                norm_root(image, 2, 4)
                conv2(n0, 0, 1)
                normed(image, 2, 4)
                relu2(0)
                with act.Fori(0, BLOCKS // 2 - 1) as r:
                    for k in range(2):
                        for m in range(2):
                            conv2(n0 + r * 2 + (k + 1), 1 - k, m)
                        relu2(r * 2 + (k + 1))
                        for m in range(2):
                            fuse2(n0 + r * 2 + k, k, m, half0 + r)
                for m in range(2):
                    conv2(n0 + (BLOCKS - 1), 1, m)
                relu2(BLOCKS - 1)
                for k in range(2):
                    for m in range(2):
                        fuse2(n0 + (BLOCKS - 2 + k), k, m, half0 + (BLOCKS // 2 - 1))

            for s, n in ((bc_mm, 4), (fuse_mm, 2), (f2_mm, 4), (stored[0], 16), (stored[1], 16)):
                act.sem_inc(s, n)
            act.sem_inc(a_used, 2)
            act.sem_inc(w_ready, 1)
            act.wait_ge(weights, NWEIGHTS)
            fn(a_neg[:], a_neg[:], ACT.Exp).then_inc(a_exp, 1)
            act.wait_ge(a_exp, 2)
            act.wait_ge(consts, 3)
            fn(logc[:, 2:3], logc[:, 3:4], ACT.Ln, bias=logc[:, 1:2]).then_inc(a_exp, 1)
            with act.Fori(0, IMAGES) as image:
                act.wait_ge(img_free, image + 1)
                lead(Tile(image * TILES, 0, 0))
                walk(act, image, tile_steps)
                T = Tile(image * TILES, TILES, 0)
                T.misc = -1
                outputs(T, TILES)
                norm_root(image, 0, CC)
                act.wait_ge(gn_vec, image * NORM_VEC + (NORM_AT[0] + CC + 9))
                for c in range(CC):
                    fn(img[:, c, 1:H + 1, 1:W + 1], img[:, c, 1:H + 1, 1:W + 1], ACT.Identity,
                       scale=gns[:, 4, c:c + 1], bias=gns[:, 5, c:c + 1]).then_inc(x1_mul, 1)
                layer1(image)

        @block.vector
        def _(dve):
            tt = nc.vector.tensor_tensor
            stt = nc.vector.scalar_tensor_tensor

            def step(T, i):
                i.then_inc(vec, 1)
                T.vec += 1

            def settled(T, but=0):
                dve.wait_ge(vec, T.at(VPER, T.vec - but))

            def gate(T, buf, h, tile_more):
                dve.wait_ge(y_done, T.at(GROUPS, GPH * (h + 1) - GROUPS * (1 - tile_more) + 1))
                step(T, stt(out=yg[:, h, :], in0=u[:, buf, h, :], scalar=ds2[:, h:h + 1], in1=p_y[:],
                            op0=ALU.mult, op1=ALU.add))
                settled(T)
                tt(yg[:, h, :], yg[:, h, :], gz[:, buf, h, :], ALU.mult).then_inc(yg_ok, 1)

            def deltas(T, buf, more):
                dve.wait_ge(soft_act, T.at(3, 3 * more + 3))
                step(T, nc.vector.tensor_scalar(sp_e[:], sp_e[:], SMALL, None, ALU.min))
                step(T, stt(out=delta[:, buf, :, :], in0=delta[:, buf, :, :], scalar=0.0, in1=du[:, buf, :, :],
                            op0=ALU.max, op1=ALU.add))
                settled(T)
                step(T, nc.vector.tensor_scalar(sp_u[:], sp_e[:], -0.25, 1.0 / 3.0, ALU.mult, ALU.add))
                settled(T)
                step(T, tt(sp_u[:], sp_u[:], sp_e[:], ALU.mult))
                for add in (-0.5, 1.0):
                    settled(T)
                    step(T, stt(out=sp_u[:], in0=sp_u[:], scalar=add, in1=sp_e[:], op0=ALU.add, op1=ALU.mult))
                settled(T)
                step(T, stt(out=delta[:, buf, :, :], in0=delta[:, buf, :, :], scalar=logc[:, 2:3], in1=sp_u[:],
                            op0=ALU.subtract, op1=ALU.add))
                settled(T)
                tt(du[:, buf, :, :], delta[:, buf, :, :], u[:, buf, :, :], ALU.mult).then_inc(delta_ok, 1)

            def tile_stats(T, t):
                dve.wait_ge(misc_free, T.at(PER, LEAD + (5 if T.last else 6)))
                for c in range(CC):
                    step(T, nc.vector.bn_stats(st0[:, c, bass.ds(t - 1, 1), :],
                                               img[:, c, bass.ds(t * TROWS - (TROWS - 1), TROWS), 1:W + 1]))

            def tile_steps(T, t):
                b, nb = T.buf, 1 - T.buf
                for gi in range(GROUPS):
                    a = dec[:, gi % 2, :, :]
                    if gi == 0:
                        dve.wait_ge(misc_free, T.at(PER, (LEAD if T.first else LEAD - 1) + 1))
                    for half in range(2):
                        dve.wait_ge(du_mm, T.at(2 * GROUPS, 2 * gi + half + 1))
                        pl = slice(4 * half, 4 * half + 4)
                        tt(g[:, pl, :], p_du[:, 2 * half:2 * half + 2, :].rearrange("p q (a b) -> p (q a) b", a=2),
                           brep[:, pl, :], ALU.mult).then_inc(g_done, 1)
                    dve.wait_ge(g_done, T.at(2 * GROUPS, 2 * gi + 4))
                    dve.wait_ge(exp_done, T.at(4 * GROUPS, 4 * gi + 6))
                    for k in range(1, TOK - 1):
                        f, e = plane(k), plane(k - 1)
                        ways = [(hh[:, f, :], a[:, f, :], g[:, f, :], g[:, 0, :] if k == 1 else hh[:, e, :]),
                                (hh[:, 2 * TOK - 1 - f, :], a[:, TOK - 1 - f, :], g[:, TOK - 1 - f, :],
                                 g[:, TOK - 1, :] if k == 1 else hh[:, 2 * TOK - 1 - e, :])]
                        for now, decay, _, before in ways:
                            if k > 1:
                                settled(T, 1)
                            step(T, tt(now, decay, before, ALU.mult))
                        for now, _, new, _ in ways:
                            settled(T, 1)
                            step(T, tt(now, now, new, ALU.add))
                        if k == 3 and gi == 0 and not T.first:
                            gate(T, nb, 1, 0)
                        if k == 3 and gi == 4:
                            if not T.first:
                                dve.wait_ge(misc_free, T.at(PER, LEAD + (5 if T.last else 6)))
                            gate(T, b, 0, 1)
                        if k == 3 and gi == 5 and not T.last:
                            deltas(T, nb, 1)
                        if k == 3 and gi == 2 and not T.first:
                            tile_stats(T, t)
                    settled(T)
                    e = plane(TOK - 2)
                    tt(pair(hh, TOK - 1, 0), pair(a, TOK - 1, 0), pair(hh, e, 2 * TOK - 1 - e),
                       ALU.mult).then_inc(a_used, 1)
                    dve.wait_ge(a_used, T.at(GROUPS, gi + 3))
                    step(T, stt(out=pair(hh, 0, TOK - 1), in0=pair(g, 0, TOK - 1), scalar=2.0,
                                in1=pair(hh, 0, TOK - 1), op0=ALU.mult, op1=ALU.add))
                    step(T, tt(hh[:, 1:TOK - 1, :], hh[:, 1:TOK - 1, :], hh[:, TOK + 1:2 * TOK - 1, :], ALU.add))
                    settled(T)
                    if gi == 0:
                        dve.wait_ge(misc_free, T.at(PER, (LEAD if T.first else LEAD - 1) + 4 + 1))
                    dve.wait_ge(y_done, T.at(GROUPS, gi + 1))
                    tt(wc[:], hh[:, 0:TOK, :], crep[:], ALU.mult).then_inc(w_ready, 1)

            def norm(image, use, cols, rows_stats, gain, shift):
                done = [NORM_AT[use]]

                def counted(i):
                    i.then_inc(gn_vec, 1)
                    done[0] += 1

                def ready():
                    dve.wait_ge(gn_vec, image * NORM_VEC + done[0])

                r = [gns[:, n, 0:cols] for n in range(8)]
                nc.vector.memset(gns[:, 7, :], 0.0)
                for c in range(cols):
                    counted(nc.vector.bn_aggr(mv[:, c, :], rows_stats(c)))
                dve.wait_ge(gn_mm, image * (2 * NORMS) + (2 * use + 1))
                counted(nc.vector.tensor_copy(r[1], p_misc[:, 0:cols]))
                ready()
                counted(tt(r[6], mv[:, 0:cols, 0], r[1], ALU.subtract))
                ready()
                counted(tt(r[7], r[6], r[6], ALU.mult))
                ready()
                counted(tt(r[0], r[7], mv[:, 0:cols, 1], ALU.add))
                dve.wait_ge(gn_mm, image * (2 * NORMS) + (2 * use + 2))
                counted(nc.vector.tensor_copy(r[2], p_misc[:, 0:cols]))
                dve.wait_ge(gn_act, image * NORMS + (use + 1))
                counted(nc.vector.reciprocal(r[3], r[3]))
                ready()
                counted(tt(r[4], r[3], gain, ALU.mult))
                ready()
                counted(tt(r[6], r[1], r[4], ALU.mult))
                ready()
                counted(tt(r[5], shift, r[6], ALU.subtract))

            class Count:
                def __init__(self, base, n):
                    self.base, self.n = base, n

                def step(self, i):
                    i.then_inc(vec1, 1)
                    self.n += 1

                def settled(self, but=0):
                    dve.wait_ge(vec1, self.base + (self.n - but))

            def offset_sum(v, n2):
                dve.wait_ge(off_mm, n2 + 1)
                dve.wait_ge(tanh_ok, n2 + 1)
                off, a4 = [grid(p_du[32 * dx:32 * dx + 4, 0, :]) for dx in range(3)], grid(acc[0:4, :])
                v.step(nc.vector.tensor_copy(a4, off[1]))
                v.settled()
                v.step(tt(a4[:, :, 1:W], off[0][:, :, 0:W - 1], a4[:, :, 1:W], ALU.add))
                v.settled()
                tt(a4[:, :, 0:W - 1], off[2][:, :, 1:W], a4[:, :, 0:W - 1], ALU.add).then_inc(off_sum, 1)

            def weigh(v, n2, m, diffs, to, low):
                for s in range(2):
                    if s == 0:
                        v.settled()
                    dve.wait_ge(bc_mm, n2 * 4 + (2 * m + s + 5))
                    v.step(stt(out=grid(to[s]), in0=grid(p_du[:, 1 + s, :]), scalar=0.0, in1=diffs[s][0],
                               op0=ALU.max, op1=ALU.mult))
                for s in range(2):
                    stt(out=grid(low[s]), in0=grid(p_du[:, 1 + s, :]), scalar=0.0, in1=diffs[s][1],
                        op0=ALU.min, op1=ALU.mult).then_inc(bc_used, 1)
                for s in range(2):
                    dve.wait_ge(bc_used, n2 * 4 + (2 * m + s + 3))
                    v.step(tt(to[s], to[s], low[s], ALU.add))

            def block1_sample(v, image, rb, nxt):
                n, n2 = image * BLOCKS + rb, image * (2 * BLOCKS) + rb
                start = v.n
                dve.wait_ge(pads, image * PADS + (PADS if not nxt else rb * 2 + 5))
                for m in range(2):
                    d, base, diffs = [], [], []
                    for s in range(2):
                        t, by = pp[:, 2 * m + s, :, :], 2 * s - 1
                        if m == 0:
                            d.append(df[:, s, :].rearrange("p (h w) -> p h w", w=W))
                            cs = slice(1 + by, 1 + by + W)
                            v.step(tt(d[s], t[:, rows9(rb, 1), cs], t[:, rows9(rb, 0), cs], ALU.subtract))
                            base.append(t[:, rows(rb, 1), cs])
                            diffs.append((d[s][:, 1:RB + 1, :], d[s][:, 0:RB, :]))
                        else:
                            d.append(df[:, s, 0:RB * (W + 1)].rearrange("p (h w) -> p h w", w=W + 1))
                            rs = rows(rb, 1 + by)
                            v.step(tt(d[s], t[:, rs, 1:PW], t[:, rs, 0:PW - 1], ALU.subtract))
                            base.append(t[:, rs, 1:W + 1])
                            diffs.append((d[s][:, :, 1:W + 1], d[s][:, :, 0:W]))
                    to, low = [tm[:, 0, :], tm[:, 1, :]], [tm[:, 2, :], tm[:, 3, :]]
                    weigh(v, n2, m, diffs, to, low)
                    for s in range(2):
                        v.settled(1)
                        v.step(tt(grid(to[s]), grid(to[s]), base[s], ALU.add))
                    v.settled()
                    v.step(tt(to[0], to[0], to[1], ALU.add))
                    if m == 0 and nxt:
                        offset_sum(v, n2 + 1)
                    v.settled()
                    dve.wait_ge(cen_mm, n * 2 + (m + 1))
                    stt(out=m1[:, m, cols(rb)], in0=CENTRE[m], scalar=v1[:, 1 + m:2 + m], in1=to[0],
                        op0=ALU.add, op1=ALU.add).then_inc(cen_used, 1)
                    dve.wait_ge(cen_used, n * 2 + (m + 3))
                    nc.vector.bn_stats(stat(m, rb), m1[:, m, cols(rb)]).then_inc(bn1, 1)
                assert v.n - start == (V1 if nxt else V1 - 2)

            def copy_back(n, rb):
                dve.wait_ge(fuse_ev, n + 3)
                nc.vector.tensor_copy(hr[:, rows(rb, 1), 1:W + 1], hz[:, rows(rb, 1), 1:W + 1]).then_inc(h1_ok, 1)
                for to, at in ((0, 1), (PW - 1, W)):
                    nc.vector.tensor_copy(hr[:, rows(rb, 1), to:to + 1], hz[:, rows(rb, 1), at:at + 1]).then_inc(h1_ok, 1)

            def block2_stats(n, rb):
                dve.wait_ge(o2_ev, n * 4 + 6)
                for c in range(4):
                    nc.vector.bn_stats(stat(c, rb), m2[:, c, cols(rb)]).then_inc(bn1, 1)

            def block2_sample(v, image, rb, first, nxt):
                n, n2 = image * BLOCKS + rb, image * (2 * BLOCKS) + (BLOCKS + rb)
                start = v.n
                v.step(tt(dv[:], hr[:, rows9(rb, 1), :], hr[:, rows9(rb, 0), :], ALU.subtract))
                v.step(tt(dh[:], hr[:, rows10(rb), 1:PW], hr[:, rows10(rb), 0:PW - 1], ALU.subtract))
                for m in range(2):
                    base, diffs = [], []
                    for s in range(2):
                        by = 2 * s - 1
                        if m == 0:
                            cs = slice(1 + by, 1 + by + W)
                            base.append(hr[:, rows(rb, 1), cs])
                            diffs.append((dv[:, 1:RB + 1, cs], dv[:, 0:RB, cs]))
                        else:
                            rs = slice(1 + by, 1 + by + RB)
                            base.append(hr[:, rows(rb, 1 + by), 1:W + 1])
                            diffs.append((dh[:, rs, 1:W + 1], dh[:, rs, 0:W]))
                    to, low = [sm[:, 2 * m, :], sm[:, 2 * m + 1, :]], [tn[:, 0, :], tn[:, 1, :]]
                    dve.wait_ge(o2_mm, n * 4 + (2 * m + 2))
                    weigh(v, n2, m, diffs, to, low)
                    for s in range(2):
                        v.settled(1 - s)
                        tt(grid(to[s]), grid(to[s]), base[s], ALU.add).then_inc(s_ok, 1)
                    if m == 0 and nxt:
                        offset_sum(v, n2 + 1)
                if not first:
                    block2_stats(n - 1, rb - 1)
                assert v.n - start == (V2 if nxt else V2 - 2)

            def layer1(image):
                n0, n20, at = image * BLOCKS, image * (2 * BLOCKS), image * VEC1
                offset_sum(Count(at, 0), n20)
                with dve.Fori(0, BLOCKS - 2) as rb:
                    block1_sample(Count(at + rb * V1, 2), image, rb, True)
                block1_sample(Count(at, 2 + V1 * (BLOCKS - 2)), image, BLOCKS - 2, True)
                block1_sample(Count(at, 2 + V1 * (BLOCKS - 1)), image, BLOCKS - 1, False)
                dve.wait_ge(bn1, image * BNS + 2 * BLOCKS)
                norm(image, 1, 2, lambda c: st1[:, c, :, :], v1[:, 3:5], v1[:, 5:7])
                for part in (hz[:, 0, :], hz[:, PH - 1, :], hz[:, 1:H + 1, 0:1], hz[:, 1:H + 1, PW - 1:PW]):
                    nc.vector.memset(part, 0.0).then_inc(hz_clear, 1)
                with dve.Fori(0, BLOCKS) as rb:
                    copy_back(n0 + rb, rb)
                dve.wait_ge(h1_ok, image * H1 + 3 * BLOCKS)
                for to, frm in ((0, 1), (PH - 1, H)):
                    nc.vector.tensor_copy(hr[:, to, :], hr[:, frm, :]).then_inc(h1_ok, 1)
                dve.wait_ge(h1_ok, image * H1 + H1)
                offset_sum(Count(at, V1 * BLOCKS), n20 + BLOCKS)
                first = V1 * BLOCKS + 2
                block2_sample(Count(at, first), image, 0, True, True)
                with dve.Fori(1, BLOCKS - 1) as rb:
                    block2_sample(Count(at + rb * V2, first), image, rb, False, True)
                block2_sample(Count(at, first + V2 * (BLOCKS - 1)), image, BLOCKS - 1, False, False)
                block2_stats(n0 + (BLOCKS - 1), BLOCKS - 1)
                dve.wait_ge(bn1, image * BNS + BNS)
                norm(image, 2, 4, lambda c: st1[:, c, :, :], v2[:, 6:10], v2[:, 10:14])
                with dve.Fori(0, BLOCKS // 2) as r:
                    for k in range(2):
                        for o in range(2):
                            dve.wait_ge(h2_ok, n20 + r * 4 + (2 * k + o + 3))
                            tt(grid(ht[:, k, o, :]), grid(ht[:, k, o, :]), img[:, o, rows(r * 2 + k, 1), 1:W + 1],
                               ALU.add).then_inc(res_ok, 1)

            for s, n in ((tanh_ok, 1), (o2_mm, 4)):
                dve.sem_inc(s, n)
            dve.sem_inc(y_done, 1)
            dve.sem_inc(img_free, 1)
            dve.memset(eps[:], EPS).then_inc(consts, 1)
            dve.memset(gns[:], 0.0).then_inc(consts, 1)
            for n, value in enumerate((-SMALL, 1.0 + SMALL, 0.0, 0.0)):
                dve.memset(logc[:, n:n + 1], value)
            dve.wait_ge(weights, NWEIGHTS)
            dve.wait_ge(a_exp, 1)
            nc.vector.tensor_scalar(a_neg[:], a_neg[:], -1.0, None, ALU.mult).then_inc(a_exp, 1)
            nc.vector.tensor_scalar(ds2[:], ds2[:], 2.0, None, ALU.mult)
            nc.vector.tensor_scalar(bdt2[:], bdt2[:], 2.0, None, ALU.mult).then_inc(consts, 1)
            dve.wait_ge(consts, 3)
            dve.wait_ge(a_exp, 3)
            with dve.Fori(0, IMAGES) as image:
                lead = Tile(image * TILES, 0, 0)
                lead.vec = 0
                deltas(lead, 0, 0)
                walk(dve, image, tile_steps)
                T = Tile(image * TILES, TILES, 0)
                T.vec = -3
                gate(T, 1, 1, 0)
                dve.wait_ge(misc_free, T.at(PER, 1))
                for c in range(CC):
                    step(T, nc.vector.bn_stats(st0[:, c, TILES - 1, :], img[:, c, H - TROWS + 1:H + 1, 1:W + 1]))
                settled(T)
                norm(image, 0, CC, lambda c: st0[:, c, :, :], gn0[:, 0, :], gn0[:, 1, :])
                for c in range(CC):
                    dve.wait_ge(x_again, image * 32 + 32)
                    dve.wait_ge(x1_mul, image * CC + (c + 1))
                    tt(img[:, c, 1:H + 1, 1:W + 1], img[:, c, 1:H + 1, 1:W + 1],
                       x_old[:, c, :].rearrange("p (h w) -> p h w", w=W), ALU.add).then_inc(x1_ok, 1)
                layer1(image)


def kernel(**inputs):
    import numpy as np
    import concourse.bacc as bacc
    from concourse import mybir
    from concourse.bass_utils import run_bass_kernel_spmd
    a = {n: np.asarray(v) for n, v in inputs.items()}
    p = {n[len("L0_conv_"):]: v for n, v in a.items() if n.startswith("L0_conv_")}
    d = {"x": a["x"]}
    for n in ("W_in", "W_x", "W_dt", "W_out"):
        d[n] = p[n]
    d["W_B"] = np.tile(p["W_x"][:, 2:18], (1, 8))
    d["W_C"] = np.tile(p["W_x"][:, 18:34], (1, 8))
    d["Ds"] = p["Ds"].reshape(64, 1)
    d["b_dt"] = p["b_dt"].reshape(64, 1)
    d["A_logs"] = p["A_logs"].reshape(8, 128).T
    d["gn_w"] = p["gn_w"].reshape(2, 128).T
    d["gn_b"] = p["gn_b"].reshape(2, 128).T
    rows = np.arange(128)
    spread = np.zeros((128, 4, 4, 128), np.float32)
    gather = np.zeros((128, 4, 32), np.float32)
    for n in range(4):
        for q in range(4):
            spread[:, q, n, :] = rows[:, None] == 32 * q + 8 * n + rows[None, :] // 16
        gather[:, n, :] = 8 * n + rows[:, None] // 16 == np.arange(32)[None, :]
    d["spread"] = spread
    d["gather"] = gather
    d["same64"] = (rows[:, None] // 64 == rows[None, :] // 64).astype(np.float32) / 64
    one = {n[len("L1_conv_cv1_"):]: v for n, v in a.items() if n.startswith("L1_conv_cv1_")}
    two = {n[len("L1_conv_cv2_"):]: v for n, v in a.items() if n.startswith("L1_conv_cv2_")}

    def chunks(m):
        m = m.reshape((m.shape[0] // 128, 128) + m.shape[1:])
        return np.moveaxis(m, 0, 1).reshape(128, -1)

    def layout(b):
        conv = b["conv0_w"].transpose(1, 2, 3, 0)
        dsc = np.stack([b["dscx_w"], b["dscy_w"]]).transpose(2, 0, 3, 1)
        fuse = b["fuse_w"].T
        offs = np.stack([b["offx_w"][0], b["offx_w"][2], b["offy_w"][3], b["offy_w"][5]])
        off = np.zeros((offs.shape[1], 3, 3, 32), np.float32)
        off[..., 0:4] = offs.transpose(1, 2, 3, 0)
        return chunks(conv), chunks(dsc), chunks(fuse), chunks(off)

    conv, dsc, fuse, off = layout(one)
    d["block1"] = np.concatenate([conv, dsc, fuse], axis=1)
    d["off1"] = off.reshape(128, 2, 3, 96)
    conv, dsc, fuse, off = layout(two)
    d["block2"] = np.concatenate([conv, fuse], axis=1)
    d["off2"] = off.reshape(128, 3, 96)
    d["dsc2"] = dsc.reshape(128, 6, 256)
    pick = np.zeros((128, 4, 128), np.float32)
    for n in range(4):
        pick[n, n, :] = 1
    d["pick"] = pick
    d["same4"] = (rows[:, None] // 4 == rows[None, :] // 4).astype(np.float32) / 4
    names = ("conv0_b", "dscx_b", "dscy_b", "gnx_g", "gny_g", "gnx_b", "gny_b", "fuse_b")
    d["v1"] = np.stack([one[n] for n in names], axis=1)
    d["v2"] = np.concatenate([two[n].reshape(2, 128) for n in names]).T
    d["off_b"] = np.stack([np.array([b["offx_b"][0], b["offx_b"][2], b["offy_b"][3], b["offy_b"][5]]) for b in (one, two)], axis=1)
    d = {n: np.ascontiguousarray(v) for n, v in d.items()}
    nc = bacc.Bacc("TRN2", target_bir_lowering=False, num_devices=1)
    aps = {n: nc.dram_tensor("in_" + n, v.shape, mybir.dt.float32, kind="ExternalInput").ap() for n, v in d.items()}
    out = nc.dram_tensor("out_0", (4, 256, 64, 64), mybir.dt.float32, kind="ExternalOutput").ap()
    two_layer_program(nc, aps, out)
    r = run_bass_kernel_spmd(nc, [{"in_" + n: v for n, v in d.items()}], core_ids=[0])
    return r.results[0]["out_0"]
```

```python
import concourse.bass as bass
from concourse import mybir
from contextlib import ExitStack


def two_layer_program(nc, w, out):
    F32 = mybir.dt.float32
    ALU = mybir.AluOpType
    ACT = mybir.ActivationFunctionType

    P = 128
    IMAGES, CH, H, W = 4, 256, 64, 64
    CC = CH // P
    QUADS, TOK = 4, 8
    TILE = 256
    TROWS = TILE // W
    TILES = H * W // TILE
    WIDE = 2 * TILE
    HALVES = 2
    GROUPS = 8
    GPH = GROUPS // HALVES
    EPS = 1e-5
    SMALL = 1.0 / 64
    ARENA = 29440
    RB = 8
    BLOCKS = H // RB
    PH, PW = H + 2, W + 2

    ctx = ExitStack()
    with ctx:
        def sb(name, shape, dt=F32):
            return ctx.enter_context(nc.sbuf_tensor(name, shape, dt))

        def ps(name, shape):
            return ctx.enter_context(nc.psum_tensor(name, shape, F32))

        def sem(name):
            return ctx.enter_context(nc.semaphore(name))

        w_in_x = sb("w_in_x", [P, HALVES, P])
        w_in_z = sb("w_in_z", [P, HALVES, P])
        w_dts = sb("w_dts", [P, HALVES, 2 * QUADS])
        w_dt = sb("w_dt", [2 * QUADS, HALVES, P])
        w_bc = sb("w_bc", [P, HALVES, P])
        w_out = sb("w_out", [P, HALVES, P])
        spread = sb("spread", [P, QUADS, GPH, P])
        gather = sb("gather", [P, GPH, 32])
        copy_b = sb("copy_b", [P, QUADS, P])
        copy_c = sb("copy_c", [P, QUADS, P])
        a_neg = sb("a_neg", [P, GROUPS])
        ds2 = sb("ds2", [P, HALVES])
        bdt2 = sb("bdt2", [P, HALVES])
        gn0 = sb("gn0", [P, 2, CC])
        same64 = sb("same64", [P, P])

        img = sb("img", [P, CC, H + 2, W + 2])
        xt = sb("xt", [P, 2, CC, TILE])
        th = sb("th", [P, RB * W])
        wx = sb("wx", [P, 4224])
        c1_off = sb("c1_off", [P, CC, 3, 96])
        c2_off = sb("c2_off", [P, 3, 96])
        c2_dsc = sb("c2_dsc", [P, 6, 2 * P])
        pick = sb("pick", [P, 4, P])
        same4 = sb("same4", [P, P])
        v1 = sb("v1", [P, 8])
        v2 = sb("v2", [P, 16])
        off_b = sb("off_b", [4, 2])
        st1 = sb("st1", [P, 4, BLOCKS, 6])
        st0 = sb("st0", [P, CC, TILES, 6])
        gns = sb("gns", [P, 8, 4])
        mv = sb("mv", [P, 4, 2])
        eps = sb("eps", [P, 1])
        logc = sb("logc", [P, 4])

        arena = sb("arena", [P, ARENA])
        cursor = [0]

        def carve(*shape, at=None):
            n = 1
            for d in shape:
                n *= d
            o = cursor[0] if at is None else at
            cursor[0] = o + n
            assert cursor[0] <= ARENA, cursor[0]
            names = "abcd"[:len(shape)]
            flat = arena[:, o:o + n]
            if len(shape) == 1:
                return flat
            dims = {c: d for c, d in zip(names, shape)}
            return flat.rearrange("p (" + " ".join(names) + ") -> p " + " ".join(names), **dims)

        dec_f = carve(TILE, TOK)
        dec_b = carve(TILE, TOK)
        g = carve(TILE, TOK)
        hf = carve(TILE, TOK)
        hb = carve(TILE, TOK)
        wc = carve(TOK, TILE, at=cursor[0] - TOK * TILE)
        brep = carve(TOK, TILE)
        crep = carve(2, TOK, TILE)
        bc = carve(WIDE)
        u = carve(2, HALVES, WIDE)
        gz = carve(2, HALVES, WIDE)
        delta = carve(2, HALVES, WIDE)
        du = carve(2, HALVES, WIDE)
        sp_e = carve(HALVES, WIDE)
        sp_u = carve(HALVES, WIDE)
        dt8 = sp_u[:, 0, :]
        yg = carve(HALVES, WIDE)
        x_old = carve(CC, H * W, at=0)

        PIX = RB * W
        pp = carve(4, PH, PW, at=0)
        m1 = carve(2, H * W)
        df = carve(2, 9 * W)
        tm = carve(4, PIX)
        at1 = tm[:, 0:2, :]
        hz = carve(PH, PW, at=0)
        hr = carve(PH, PW)
        m2 = carve(4, H * W)
        dv = carve(9, PW)
        dh = carve(10, PW - 1)
        sm = carve(4, PIX)
        tn = carve(2, PIX)
        at2 = carve(2, 2, PIX, at=2 * PH * PW + 4 * H * W)
        ht = carve(2, 2, PIX)
        acc = xt[:, 0, :, :].rearrange("p c n -> p (c n)")
        c1_conv = wx[:, 0:2304].rearrange("p (c t o) -> p c t o", c=CC, t=9)
        c1_dsc = wx[:, 2304:3840].rearrange("p (c k o) -> p c k o", c=CC, k=6)
        c1_fuse = wx[:, 3840:4224].rearrange("p (k o) -> p k o", k=3)
        c2_conv = wx[:, 0:2304].rearrange("p (t o) -> p t o", t=9)
        c2_fuse = wx[:, 2304:3840].rearrange("p (k o) -> p k o", k=6)

        p_dec = ps("p_dec", [P, 2, 512])
        p_du = ps("p_du", [P, 4, 512])
        p_y = ps("p_y", [P, 512])
        p_misc = ps("p_misc", [P, 512])

        weights = sem("weights")
        cleared = sem("cleared")
        consts = sem("consts")
        a_exp = sem("a_exp")
        x_in = [sem("x_in0"), sem("x_in1")]
        misc_full = sem("misc_full")
        misc_free = sem("misc_free")
        dec_mm = sem("dec_mm")
        exp_done = sem("exp_done")
        du_mm = sem("du_mm")
        g_done = sem("g_done")
        dec_b_in = sem("dec_b_in")
        f_scan = sem("f_scan")
        b_scan = sem("b_scan")
        zeroed = sem("zeroed")
        w_ready = sem("w_ready")
        y_done = sem("y_done")
        soft_act = sem("soft_act")
        delta_ok = sem("delta_ok")
        yg_ok = sem("yg_ok")
        vec = sem("vec")
        gn_vec = sem("gn_vec")
        gn_mm = sem("gn_mm")
        gn_act = sem("gn_act")
        x1_mul = sem("x1_mul")
        x1_ok = sem("x1_ok")
        x_again = sem("x_again")
        stored = [sem("stored0"), sem("stored1")]
        img_free = sem("img_free")

        for_layer_1 = """pp_mm pp_ev pads off_mm off_sum tanh_ok bc_mm bc_used cen_mm cen_used conv_mm conv_ev
            relu_ok fuse_mm fuse_ev h1_ok hz_clear o2_mm o2_ev s_ok vec1 bn1 a2_mm a2_ev relu2_ok f2_mm h2_ok res_ok
            w1_in w2_in""".split()
        (pp_mm, pp_ev, pads, off_mm, off_sum, tanh_ok, bc_mm, bc_used, cen_mm, cen_used, conv_mm, conv_ev,
         relu_ok, fuse_mm, fuse_ev, h1_ok, hz_clear, o2_mm, o2_ev, s_ok, vec1, bn1, a2_mm, a2_ev, relu2_ok,
         f2_mm, h2_ok, res_ok, w1_in, w2_in) = [sem(n) for n in for_layer_1]

        xv = w["x"].rearrange("b (c p) h w -> b p c (h w)", p=P)
        outv = out.rearrange("b (c p) h w -> b p c (h w)", p=P)

        def planes(t, first, count):
            v = t.rearrange("p n (a q) -> p q a n", a=2)
            return v[:, first:first + count, :, :]

        LEAD, PER = 16, 17
        DSTEPS = 7
        NORM_AT = [0, CC + 9, 2 * CC + 18]
        NORM_VEC = NORM_AT[2] + 4 + 9
        NORMS = 3
        VPER = GROUPS + 2 + DSTEPS + 2
        PAIRS = TILES // 2

        class Tile:
            def __init__(self, base, k, buf, first=False, last=False):
                self.base, self.k, self.buf, self.first, self.last = base, k, buf, first, last
                self.misc = LEAD if first else LEAD - 1
                self.vec = DSTEPS if first else DSTEPS - 3

            def at(self, per_tile, more):
                return self.base * per_tile + (self.k * per_tile + more)

        def walk(eng, image, tile_steps):
            base = image * TILES
            for k in range(2):
                tile_steps(Tile(base, k, k, first=k == 0), k)
            with eng.Fori(1, PAIRS - 1) as tp:
                for k in range(2):
                    tile_steps(Tile(image * TILES + tp * 2, k, k), tp * 2 + k)
            for k in range(2):
                tile_steps(Tile(base, TILES - 2 + k, k, last=k == 1), TILES - 2 + k)

        PADS = 2 * BLOCKS + 2
        V1, V2 = 20, 12
        VEC1 = (V1 + V2) * BLOCKS
        BNS = 6 * BLOCKS
        H1 = 3 * BLOCKS + 2
        CENTRE = [p_du[:, 3, :], p_y[:]]

        def rows(rb, shift):
            return slice(rb * RB + shift, rb * RB + shift + RB) if isinstance(rb, int) else bass.ds(rb * RB + shift, RB)

        def rows9(rb, shift):
            at = rb * RB + shift
            return slice(at, at + RB + 1) if isinstance(rb, int) else bass.ds(at, RB + 1)

        def rows10(rb):
            return slice(rb * RB, rb * RB + RB + 2) if isinstance(rb, int) else bass.ds(rb * RB, RB + 2)

        def stat(c, rb):
            return st1[:, c, rb, :] if isinstance(rb, int) else st1[:, c, bass.ds(rb, 1), :]

        def cols(rb):
            return slice(rb * PIX, rb * PIX + PIX) if isinstance(rb, int) else bass.ds(rb * PIX, PIX)

        def grid(a):
            return a.rearrange("p (h w) -> p h w", w=W)

        block = ctx.enter_context(nc.Block())

        @block.sync
        def _(sp):
            sp.wait_ge(cleared, 8)
            for h in range(HALVES):
                for q in range(QUADS):
                    r = slice(32 * q, 32 * q + 32)
                    hs = slice(32 * h, 32 * h + 32)
                    sp.dma_start(w_in_x[r, h, r], w["W_in"][:, hs]).then_inc(weights, 16)
                    sp.dma_start(w_in_z[r, h, r], w["W_in"][:, 64 + 32 * h:96 + 32 * h]).then_inc(weights, 16)
                    sp.dma_start(w_out[r, h, r], w["W_out"][hs, :]).then_inc(weights, 16)
                    sp.dma_start(w_dts[r, h, 2 * q:2 * q + 2], w["W_x"][hs, 0:2]).then_inc(weights, 16)
                    sp.dma_start(w_dt[2 * q:2 * q + 2, h, r], w["W_dt"][:, hs]).then_inc(weights, 16)
                    sp.dma_start(w_bc[r, h, r], w["W_x"][hs, 2:34]).then_inc(weights, 16)
                    sp.dma_start(ds2[r, h:h + 1], w["Ds"][hs, :]).then_inc(weights, 16)
                    sp.dma_start(bdt2[r, h:h + 1], w["b_dt"][hs, :]).then_inc(weights, 16)
            sp.dma_start(a_neg[:], w["A_logs"]).then_inc(weights, 16)
            sp.dma_start(spread[:], w["spread"]).then_inc(weights, 16)
            sp.dma_start(gather[:], w["gather"]).then_inc(weights, 16)
            sp.dma_start(copy_b[:], w["copy_b"]).then_inc(weights, 16)
            sp.dma_start(copy_c[:], w["copy_c"]).then_inc(weights, 16)
            sp.dma_start(same64[:], w["same64"]).then_inc(weights, 16)
            sp.dma_start(gn0[:, 0, :], w["gn_w"]).then_inc(weights, 16)
            sp.dma_start(gn0[:, 1, :], w["gn_b"]).then_inc(weights, 16)

            for t, name in ((c1_off, "off1"), (c2_off, "off2"), (c2_dsc, "dsc2"), (pick, "pick"), (same4, "same4"),
                            (v1, "v1"), (v2, "v2"), (off_b, "off_b")):
                sp.dma_start(t[:], w[name]).then_inc(weights, 16)
            with sp.Fori(0, IMAGES) as image:
                with sp.Fori(0, PAIRS) as tp:
                    for k in range(2):
                        sp.wait_ge(misc_full, (image * TILES + tp * 2) * PER + (k * PER + 8))
                        sp.dma_start(xt[:, k, :, :], xv[image, :, :, bass.ds(tp * WIDE + k * TILE, TILE)]).then_inc(x_in[k], 16)
                sp.dma_start(wx[:], w["block1"]).then_inc(w1_in, 16)
                sp.wait_ge(w_ready, image * (TILES * GROUPS) + (TILES * GROUPS + 1))
                for c in range(CC):
                    sp.dma_start(x_old[:, c, :], xv[image, :, c, :]).then_inc(x_again, 16)
                sp.wait_ge(fuse_mm, image * BLOCKS + (BLOCKS + 2))
                sp.dma_start(wx[:, 0:3840], w["block2"]).then_inc(w2_in, 16)
                with sp.Fori(0, BLOCKS // 2) as r:
                    for k in range(2):
                        sp.wait_ge(res_ok, image * (2 * BLOCKS) + r * 4 + (2 * k + 2))
                        sp.dma_start(outv[image, :, :, bass.ds(r * (2 * PIX) + k * PIX, PIX)],
                                     ht[:, k, :, :]).then_inc(stored[k], 16)
                for k in range(2):
                    sp.wait_ge(stored[k], image * (8 * BLOCKS) + (8 * BLOCKS + 16))
                sp.sem_inc(img_free, 1)

        NWEIGHTS = 16 * (HALVES * QUADS * 8 + 8 + 8)

        @block.gpsimd
        def _(pool):
            for t in (w_in_x, w_in_z, w_out, w_dts, w_dt, w_bc, img, th):
                nc.gpsimd.memset(t[:], 0.0).then_inc(cleared, 1)

        @block.tensor
        def _(pe):
            mm = nc.tensor.matmul
            QS = [slice(32 * q, 32 * q + 32) for q in range(QUADS)]

            def misc(T):
                pe.wait_ge(misc_free, T.at(PER, T.misc + 1))
                T.misc += 1

            def inner(T, buf, h):
                misc(T)
                mm(p_misc[:], w_in_x[:, h, :], xt[:, buf, :, :], start=True, stop=True).then_inc(misc_full, 1)

            def gates(T, buf, h):
                misc(T)
                i = mm(p_misc[:], w_in_z[:, h, :], xt[:, buf, :, :], start=True, stop=True)
                i.then_inc(misc_full, 1)

            def step_sizes(T, buf):
                misc(T)
                for h in range(HALVES):
                    i = mm(p_misc[0:8, :], w_dts[:, h, :], u[:, buf, h, :], start=h == 0, stop=h == 1)
                i.then_inc(misc_full, 1)

            def step_sizes_out(T, h):
                misc(T)
                mm(p_misc[:], w_dt[:, h, :], dt8[0:8, :], start=True, stop=True).then_inc(misc_full, 1)

            def b_and_c(T, buf):
                misc(T)
                for h in range(HALVES):
                    i = mm(p_misc[:], w_bc[:, h, :], u[:, buf, h, :], start=h == 0, stop=h == 1)
                i.then_inc(misc_full, 1)

            def repeat(T, wt, q):
                misc(T)
                mm(p_misc[:], wt[:, q, :], bc[:], start=True, stop=True).then_inc(misc_full, 1)

            def outputs(T):
                pe.wait_ge(yg_ok, T.at(HALVES, 0))
                misc(T)
                for h in range(HALVES):
                    i = mm(p_misc[:], w_out[:, h, :], yg[:, h, :], start=h == 0, stop=h == 1)
                i.then_inc(misc_full, 1)

            def spread_delta(T, buf, gi, more, n):
                pe.wait_ge(exp_done, T.at(4 * GROUPS, 4 * more + n + 1))
                mm(p_dec[:, n % 2, :], spread[:, (n + 1) % QUADS, gi % GPH, :], delta[:, buf, gi // GPH, :],
                   start=True, stop=True).then_inc(dec_mm, 1)

            def spread_du(T, buf, gi, more, half):
                pe.wait_ge(g_done, T.at(2 * GROUPS, 2 * more + half + 1))
                for q in (2 * half, 2 * half + 1):
                    i = mm(p_du[:, q, :], spread[:, q, gi % GPH, :], du[:, buf, gi // GPH, :],
                           start=True, stop=True)
                i.then_inc(du_mm, 1)

            def gather_y(T, gi):
                pe.wait_ge(w_ready, T.at(GROUPS, gi + 2))
                for q in range(QUADS):
                    i = mm(p_y[QS[q], :], gather[:, gi % GPH, :], wc[:, 2 * q:2 * q + 2, :],
                           start=gi % GPH == 0, stop=gi % GPH == GPH - 1)
                i.then_inc(y_done, 1)

            def tile_steps(T, t):
                b, nb = T.buf, 1 - T.buf
                for gi in range(GROUPS):
                    more, nxt = gi + 1, (b, gi + 1)
                    uses = []
                    if gi == 1 and not T.last:
                        pe.wait_ge(x_in[nb], T.at(8, 24 if b else 16))
                        uses.append(lambda: inner(T, nb, 0))
                    if gi == 1 and not T.first:
                        uses.append(lambda: outputs(T))
                    if not T.last:
                        if gi == 1:
                            uses.append(lambda: inner(T, nb, 1))
                        if gi == 2:
                            uses += [lambda: step_sizes(T, nb), lambda: step_sizes_out(T, 0)]
                        if gi == 3:
                            uses += [lambda: step_sizes_out(T, 1), lambda: b_and_c(T, nb)]
                        if gi == 4:
                            uses += [lambda: gates(T, nb, 0), lambda: gates(T, nb, 1)]
                        if gi in (5, 6):
                            uses += [lambda q=q: repeat(T, copy_c, q) for q in (2 * gi - 10, 2 * gi - 9)]
                        if gi == 7:
                            uses += [lambda q=q: repeat(T, copy_b, q) for q in range(4)]
                            nxt = (nb, 0)
                    nothing = [lambda: None]
                    first = uses[0:1] if gi == 7 else nothing
                    uses = (uses[1:] if gi == 7 else uses) + 3 * nothing
                    ahead = gi < 7 or not T.last
                    if ahead:
                        if gi == 7:
                            pe.wait_ge(delta_ok, T.at(1, 2))
                        (first + nothing)[0]()
                        spread_delta(T, *nxt, more, 0)
                        spread_delta(T, *nxt, more, 1)
                    uses[0]()
                    if ahead:
                        spread_du(T, *nxt, more, 0)
                    uses[1]()
                    if ahead:
                        spread_du(T, *nxt, more, 1)
                    uses[2]()
                    if ahead:
                        spread_delta(T, *nxt, more, 2)
                        spread_delta(T, *nxt, more, 3)
                    gather_y(T, gi)

            def lead(T):
                pe.wait_ge(x_in[0], T.at(8, 16))
                T.misc = 0
                inner(T, 0, 0)
                inner(T, 0, 1)
                step_sizes(T, 0)
                step_sizes_out(T, 0)
                step_sizes_out(T, 1)
                b_and_c(T, 0)
                gates(T, 0, 0)
                gates(T, 0, 1)
                for wt in (copy_c, copy_b):
                    for q in range(QUADS):
                        repeat(T, wt, q)
                pe.wait_ge(delta_ok, T.at(1, 1))
                for n in range(QUADS):
                    spread_delta(T, 0, 0, 0, n)
                for half in range(2):
                    spread_du(T, 0, 0, 0, half)

            def norm_matmuls(image, use, cols, same):
                pe.wait_ge(gn_vec, image * NORM_VEC + (NORM_AT[use] + cols))
                mm(p_misc[:, 0:cols], same[:], mv[:, 0:cols, 0], start=True, stop=True).then_inc(gn_mm, 1)
                pe.wait_ge(gn_vec, image * NORM_VEC + (NORM_AT[use] + cols + 4))
                mm(p_misc[:, 0:cols], same[:], gns[:, 0, 0:cols], start=True, stop=True).then_inc(gn_mm, 1)

            def side(n, rb):
                return [lambda i=i: side_tap(n, rb, i) for i in range(4)]

            def side_tap(n, rb, i):
                pe.wait_ge(pp_ev, n * 4 + (i + 1))
                for c in range(CC):
                    k = mm(p_dec[:, i % 2, :], c1_dsc[:, c, 3 * (i // 2) + 2 * (i % 2), :],
                           img[:, c, rows(rb, 1), 1:W + 1], start=c == 0, stop=c == CC - 1)
                k.then_inc(pp_mm, 1)

            def offsets(n2, rb, wt, src):
                pe.wait_ge(off_sum, n2 + 1)
                parts = [(c, dy) for c in range(len(wt)) for dy in range(3)]
                for c, dy in parts:
                    k = mm(p_du[0:96, 0, :], wt[c][:, dy, :], src[c][:, rows(rb, dy), 1:W + 1],
                           start=(c, dy) == parts[0], stop=(c, dy) == parts[-1])
                k.then_inc(off_mm, 1)

            def bend(n2, i):
                if i == 0:
                    pe.wait_ge(tanh_ok, n2 + 2)
                pe.wait_ge(bc_used, n2 * 4 + (i + 1))
                mm(p_du[:, 1 + i % 2, :], pick[:, i, :], th[:], start=True, stop=True).then_inc(bc_mm, 1)

            def centre(n, rb, m):
                pe.wait_ge(cen_used, n * 2 + (m + 1))
                for c in range(CC):
                    k = mm(CENTRE[m], c1_dsc[:, c, 3 * m + 1, :], img[:, c, rows(rb, 1), 1:W + 1],
                           start=c == 0, stop=c == CC - 1)
                k.then_inc(cen_mm, 1)

            OFF1 = ([c1_off[:, c, :, :] for c in range(CC)], [img[:, c, :, :] for c in range(CC)])
            OFF2 = ([c2_off[:, :, :]], [hz])

            def block1_sample(image, rb, ahead, nxt):
                n, n2 = image * BLOCKS + rb, image * (2 * BLOCKS) + rb
                later = side(n + 2, rb + 2) if ahead else [lambda: None] * 4
                bend(n2, 0)
                bend(n2, 1)
                if nxt:
                    offsets(n2 + 1, rb + 1, *OFF1)
                centre(n, rb, 0)
                centre(n, rb, 1)
                later[0]()
                later[1]()
                bend(n2, 2)
                later[2]()
                later[3]()
                bend(n2, 3)

            def conv1(n, rb, k):
                pe.wait_ge(conv_ev, n + 1)
                for c in range(CC):
                    for tap in range(9):
                        i = mm(p_dec[:, k, :], c1_conv[:, c, tap, :],
                               img[:, c, rows(rb, tap // 3), tap % 3:tap % 3 + W],
                               start=c == 0 and tap == 0, stop=c == CC - 1 and tap == 8)
                i.then_inc(conv_mm, 1)

            def fuse1(n, rb, k):
                pe.wait_ge(conv_ev, n + 3)
                pe.wait_ge(relu_ok, n * 2 + 2)
                pe.wait_ge(fuse_ev, n + 1)
                mm(p_du[:, k, :], c1_fuse[:, 0, :], at1[:, k, :], start=True, stop=False)
                mm(p_du[:, k, :], c1_fuse[:, 1, :], m1[:, 0, cols(rb)], start=False, stop=False)
                mm(p_du[:, k, :], c1_fuse[:, 2, :], m1[:, 1, cols(rb)], start=False, stop=True).then_inc(fuse_mm, 1)

            def block2_out(n, rb, m):
                pe.wait_ge(s_ok, n * 4 + (2 * m + 2))
                for o in range(2):
                    pe.wait_ge(o2_ev, n * 4 + (2 * m + o + 1))
                    os = slice(P * o, P * o + P)
                    mm(p_dec[:, o, :], c2_dsc[:, 3 * m + 1, os], hz[:, rows(rb, 1), 1:W + 1], start=True, stop=False)
                    mm(p_dec[:, o, :], c2_dsc[:, 3 * m, os], sm[:, 2 * m, :], start=False, stop=False)
                    mm(p_dec[:, o, :], c2_dsc[:, 3 * m + 2, os], sm[:, 2 * m + 1, :],
                       start=False, stop=True).then_inc(o2_mm, 1)

            def block2_sample(image, rb, first, nxt):
                n, n2 = image * BLOCKS + rb, image * (2 * BLOCKS) + (BLOCKS + rb)
                bend(n2, 0)
                bend(n2, 1)
                if not first:
                    block2_out(n - 1, rb - 1, 1)
                if nxt:
                    offsets(n2 + 1, rb + 1, *OFF2)
                bend(n2, 2)
                bend(n2, 3)
                block2_out(n, rb, 0)

            def conv2(n, rb, m):
                pe.wait_ge(a2_ev, n * 2 + (m + 1))
                for tap in range(9):
                    i = mm(p_dec[:, m, :], c2_conv[:, tap, P * m:P * m + P],
                           hz[:, rows(rb, tap // 3), tap % 3:tap % 3 + W], start=tap == 0, stop=tap == 8)
                i.then_inc(a2_mm, 1)

            def fuse2(n, rb, k, o):
                if o == 0:
                    pe.wait_ge(a2_ev, n * 2 + 4)
                    pe.wait_ge(relu2_ok, n * 4 + 4)
                pe.wait_ge(h2_ok, n * 2 + (o + 1))
                os = slice(P * o, P * o + P)
                for c in range(2):
                    mm(p_du[:, o, :], c2_fuse[:, c, os], at2[:, k, c, :], start=c == 0, stop=False)
                for c in range(4):
                    i = mm(p_du[:, o, :], c2_fuse[:, 2 + c, os], m2[:, c, cols(rb)], start=False, stop=c == 3)
                i.then_inc(f2_mm, 1)

            def layer1(image):
                pe.wait_ge(x1_ok, image * CC + CC)
                pe.wait_ge(w1_in, image * 16 + 16)
                n0, n20 = image * BLOCKS, image * (2 * BLOCKS)
                for rb in range(2):
                    for tap in side(n0 + rb, rb):
                        tap()
                offsets(n20, 0, *OFF1)
                with pe.Fori(0, BLOCKS - 2) as rb:
                    block1_sample(image, rb, True, True)
                block1_sample(image, BLOCKS - 2, False, True)
                block1_sample(image, BLOCKS - 1, False, False)
                conv1(n0, 0, 0)
                norm_matmuls(image, 1, 2, same4)
                with pe.Fori(0, BLOCKS // 2 - 1) as r:
                    for k in range(2):
                        conv1(n0 + r * 2 + (k + 1), r * 2 + (k + 1), 1 - k)
                        fuse1(n0 + r * 2 + k, r * 2 + k, k)
                conv1(n0 + (BLOCKS - 1), BLOCKS - 1, 1)
                fuse1(n0 + (BLOCKS - 2), BLOCKS - 2, 0)
                fuse1(n0 + (BLOCKS - 1), BLOCKS - 1, 1)
                pe.wait_ge(fuse_ev, n0 + (BLOCKS + 2))
                pe.wait_ge(hz_clear, image * 4 + 4)
                offsets(n20 + BLOCKS, 0, *OFF2)
                block2_sample(image, 0, True, True)
                with pe.Fori(1, BLOCKS - 1) as rb:
                    block2_sample(image, rb, False, True)
                block2_sample(image, BLOCKS - 1, False, False)
                block2_out(n0 + (BLOCKS - 1), BLOCKS - 1, 1)
                pe.wait_ge(w2_in, image * 16 + 16)
                pe.wait_ge(o2_ev, n0 * 4 + (4 * BLOCKS + 2))
                conv2(n0, 0, 0)
                norm_matmuls(image, 2, 4, same4)
                conv2(n0, 0, 1)
                with pe.Fori(0, BLOCKS // 2 - 1) as r:
                    for k in range(2):
                        for m in range(2):
                            conv2(n0 + r * 2 + (k + 1), r * 2 + (k + 1), m)
                        for m in range(2):
                            fuse2(n0 + r * 2 + k, r * 2 + k, k, m)
                for m in range(2):
                    conv2(n0 + (BLOCKS - 1), BLOCKS - 1, m)
                for k in range(2):
                    for m in range(2):
                        fuse2(n0 + (BLOCKS - 2 + k), BLOCKS - 2 + k, k, m)

            for s, n in ((pp_ev, 2), (off_sum, 1), (bc_used, 2), (cen_used, 2), (conv_ev, 2), (fuse_ev, 2), (o2_ev, 2),
                         (a2_ev, 2), (h2_ok, 2)):
                pe.sem_inc(s, n)
            pe.sem_inc(exp_done, 2)
            pe.sem_inc(g_done, 2)
            pe.sem_inc(misc_free, 1)
            pe.sem_inc(misc_full, 2 * PER)
            pe.wait_ge(weights, NWEIGHTS)
            with pe.Fori(0, IMAGES) as image:
                lead(Tile(image * TILES, 0, 0))
                walk(pe, image, tile_steps)
                T = Tile(image * TILES, TILES, 0)
                T.misc = -1
                outputs(T)
                norm_matmuls(image, 0, CC, same64)
                layer1(image)

        @block.scalar
        def _(act):
            fn = nc.scalar.activation

            def full(T):
                act.wait_ge(misc_full, T.at(PER, T.misc + 1 + 2 * PER))
                T.misc += 1

            def inner(T, buf, h):
                full(T)
                fn(u[:, buf, h, :], p_misc[:], ACT.Identity).then_inc(misc_free, 1)

            def gates(T, buf, h):
                full(T)
                i = fn(gz[:, buf, h, :], p_misc[:], ACT.Gelu)
                i.then_inc(misc_free, 1)

            def step_sizes(T):
                full(T)
                fn(dt8[0:8, :], p_misc[0:8, :], ACT.Identity).then_inc(misc_free, 1)

            def soft_in(T, buf, h):
                full(T)
                fn(delta[:, buf, h, :], p_misc[:], ACT.Identity, bias=bdt2[:, h:h + 1])
                fn(sp_e[:, h, :], p_misc[:], ACT.Abs, bias=bdt2[:, h:h + 1]).then_inc(misc_free, 1)

            def softplus(T, buf, more):
                act.wait_ge(misc_free, T.at(PER, T.misc + 1))
                fn(sp_e[:], sp_e[:], ACT.Exp, scale=-1.0).then_inc(soft_act, 1)
                act.wait_ge(soft_act, T.at(3, 3 * more + 1))
                fn(sp_u[:], sp_e[:], ACT.Relu, bias=logc[:, 0:1]).then_inc(soft_act, 1)
                act.wait_ge(soft_act, T.at(3, 3 * more + 2))
                fn(du[:, buf, :, :], sp_u[:], ACT.Ln, bias=logc[:, 1:2]).then_inc(soft_act, 1)

            def b_and_c(T):
                full(T)
                fn(bc[:], p_misc[:], ACT.Identity).then_inc(misc_free, 1)

            def repeat(T, dst, q):
                full(T)
                fn(dst[:, 2 * q:2 * q + 2, :], p_misc[:].rearrange("p (a b) -> p a b", a=2), ACT.Identity).then_inc(misc_free, 1)

            def outputs(T, t):
                full(T)
                rows = bass.ds(t * TROWS - (TROWS - 1), TROWS)
                fn(img[:, :, rows, 1:W + 1], p_misc[:].rearrange("p (c r w) -> p c r w", c=CC, w=W),
                   ACT.Identity).then_inc(misc_free, 1)

            def exps(T, gi, more, n):
                q = (n + 1) % QUADS
                if n == 0:
                    act.wait_ge(f_scan, T.at(GROUPS, more + 1))
                    act.wait_ge(dec_b_in, T.at(GROUPS, more + 1))
                act.wait_ge(dec_mm, T.at(4 * GROUPS, 4 * more + n + 1))
                bank = p_dec[:, n % 2, :].rearrange("p (a b) -> p a b", a=2)
                if q:
                    fn(planes(dec_f, q, 1), bank.rearrange("p (o a) b -> p o a b", o=1),
                       ACT.Exp, scale=a_neg[:, gi:gi + 1]).then_inc(exp_done, 1)
                else:
                    fn(dec_f[:, :, QUADS], bank[:, 1, :], ACT.Exp, scale=a_neg[:, gi:gi + 1])
                    act.wait_ge(b_scan, T.at(GROUPS, more + 1))
                    fn(dec_b[:, :, 0], bank[:, 0, :], ACT.Exp, scale=a_neg[:, gi:gi + 1]).then_inc(exp_done, 1)
                    act.wait_ge(exp_done, T.at(4 * GROUPS, 4 * more + 6))
                    fn(dec_b[:, :, 1:TOK - 1], dec_f[:, :, 1:TOK - 1], ACT.Identity).then_inc(dec_b_in, 1)

            def tile_steps(T, t):
                b, nb = T.buf, 1 - T.buf
                for gi in range(GROUPS):
                    more, following = gi + 1, (gi + 1) % GROUPS
                    ahead = gi < 7 or not T.last
                    if gi == 7 and not T.last:
                        act.wait_ge(g_done, T.at(2 * GROUPS, 2 * gi + 4))
                        repeat(T, brep, 0)
                    if ahead:
                        exps(T, following, more, 0)
                        exps(T, following, more, 1)
                    if gi == 1 and not T.last:
                        if not T.first:
                            act.wait_ge(yg_ok, T.at(HALVES, 0))
                        inner(T, nb, 0)
                    if gi == 1 and not T.first:
                        outputs(T, t)
                    if gi == 1 and not T.last:
                        inner(T, nb, 1)
                    if gi == 2 and not T.last:
                        step_sizes(T)
                        soft_in(T, nb, 0)
                    if gi == 3 and not T.last:
                        soft_in(T, nb, 1)
                        b_and_c(T)
                    if gi in (5, 6) and not T.last:
                        for q in (2 * gi - 10, 2 * gi - 9):
                            repeat(T, crep[:, nb, :, :], q)
                    if gi == 7 and not T.last:
                        for q in range(1, 4):
                            repeat(T, brep, q)
                    if gi == 4 and not T.last:
                        gates(T, nb, 0)
                        gates(T, nb, 1)
                    if ahead:
                        exps(T, following, more, 2)
                        exps(T, following, more, 3)
                    if gi == 3 and not T.last:
                        softplus(T, nb, 1)

            def lead(T):
                T.misc = 0
                inner(T, 0, 0)
                inner(T, 0, 1)
                step_sizes(T)
                soft_in(T, 0, 0)
                soft_in(T, 0, 1)
                b_and_c(T)
                softplus(T, 0, 0)
                gates(T, 0, 0)
                gates(T, 0, 1)
                for dst in (crep[:, 0, :, :], brep):
                    for q in range(QUADS):
                        repeat(T, dst, q)
                for n in range(QUADS):
                    exps(T, 0, 0, n)

            def norm_root(image, use, cols):
                act.wait_ge(gn_vec, image * NORM_VEC + (NORM_AT[use] + cols + 5))
                fn(gns[:, 3, 0:cols], gns[:, 2, 0:cols], ACT.Sqrt, bias=eps[:]).then_inc(gn_act, 1)

            def tap_out(n, rb, i):
                act.wait_ge(pp_mm, n * 4 + (i + 1))
                fn(pp[:, i, rows(rb, 1), 1:W + 1], grid(p_dec[:, i % 2, :]), ACT.Identity).then_inc(pp_ev, 1)

            def tap_edges(n, rb):
                act.wait_ge(pp_ev, n * 4 + 6)
                for to, at in ((0, 1), (PW - 1, W)):
                    fn(pp[:, :, rows(rb, 1), to:to + 1], pp[:, :, rows(rb, 1), at:at + 1], ACT.Identity).then_inc(pads, 1)

            def tap_edge_rows(image, to, at, count):
                act.wait_ge(pads, image * PADS + count)
                fn(pp[:, :, to, :], pp[:, :, at, :], ACT.Identity).then_inc(pads, 1)

            def bends(n2, block):
                act.wait_ge(off_sum, n2 + 2)
                act.wait_ge(bc_mm, n2 * 4 + 4)
                fn(th[0:4, :], acc[0:4, :], ACT.Tanh, bias=off_b[:, block:block + 1]).then_inc(tanh_ok, 1)

            def block1_sample(image, rb, ahead, nxt):
                n, n2 = image * BLOCKS + rb, image * (2 * BLOCKS) + rb
                if ahead:
                    for i in range(4):
                        tap_out(n + 2, rb + 2, i)
                    tap_edges(n + 2, rb + 2)
                if nxt:
                    bends(n2 + 1, 0)

            def conv1(n, k):
                act.wait_ge(conv_mm, n + 1)
                act.wait_ge(fuse_mm, n + 1)
                fn(at1[:, k, :], p_dec[:, k, :], ACT.Silu, bias=v1[:, 0:1]).then_inc(conv_ev, 1)

            def relu1(rb):
                for m in range(2):
                    fn(m1[:, m, cols(rb)], m1[:, m, cols(rb)], ACT.Relu,
                       scale=gns[:, 4, m:m + 1], bias=gns[:, 5, m:m + 1]).then_inc(relu_ok, 1)

            def fuse1(n, rb, k):
                act.wait_ge(fuse_mm, n + 3)
                fn(hz[:, rows(rb, 1), 1:W + 1], grid(p_du[:, k, :]), ACT.Silu, bias=v1[:, 7:8]).then_inc(fuse_ev, 1)

            def block2_out(n, rb, m):
                for o in range(2):
                    act.wait_ge(o2_mm, n * 4 + (2 * m + o + 5))
                    fn(m2[:, 2 * m + o, cols(rb)], p_dec[:, o, :], ACT.Identity,
                       bias=v2[:, 2 + 2 * m + o:3 + 2 * m + o]).then_inc(o2_ev, 1)

            def block2_sample(image, rb, first, nxt):
                n, n2 = image * BLOCKS + rb, image * (2 * BLOCKS) + (BLOCKS + rb)
                if not first:
                    block2_out(n - 1, rb - 1, 1)
                if nxt:
                    bends(n2 + 1, 1)
                block2_out(n, rb, 0)

            def conv2(n, k, m):
                act.wait_ge(a2_mm, n * 2 + (m + 1))
                act.wait_ge(f2_mm, n * 2 + 2)
                fn(at2[:, k, m, :], p_dec[:, m, :], ACT.Silu, bias=v2[:, m:m + 1]).then_inc(a2_ev, 1)

            def relu2(rb):
                for c in range(4):
                    fn(m2[:, c, cols(rb)], m2[:, c, cols(rb)], ACT.Relu,
                       scale=gns[:, 4, c:c + 1], bias=gns[:, 5, c:c + 1]).then_inc(relu2_ok, 1)

            def fuse2(n, k, o, half):
                act.wait_ge(f2_mm, n * 2 + (o + 5))
                if o == 0:
                    act.wait_ge(stored[k], half * 16 + 16)
                fn(ht[:, k, o, :], p_du[:, o, :], ACT.Silu, bias=v2[:, 14 + o:15 + o]).then_inc(h2_ok, 1)

            def normed(image, use, cols):
                act.wait_ge(gn_vec, image * NORM_VEC + (NORM_AT[use] + cols + 9))

            def layer1(image):
                n0, n20, half0 = image * BLOCKS, image * (2 * BLOCKS), image * (BLOCKS // 2)
                for rb in range(2):
                    for i in range(4):
                        tap_out(n0 + rb, rb, i)
                    tap_edges(n0 + rb, rb)
                    if rb == 0:
                        tap_edge_rows(image, 0, 1, 2)
                bends(n20, 0)
                with act.Fori(0, BLOCKS - 2) as rb:
                    block1_sample(image, rb, True, True)
                tap_edge_rows(image, PH - 1, H, PADS - 1)
                block1_sample(image, BLOCKS - 2, False, True)
                act.wait_ge(gn_vec, image * NORM_VEC + (NORM_AT[1] + 1))
                conv1(n0, 0)
                norm_root(image, 1, 2)
                normed(image, 1, 2)
                relu1(0)
                with act.Fori(0, BLOCKS // 2 - 1) as r:
                    for k in range(2):
                        conv1(n0 + r * 2 + (k + 1), 1 - k)
                        relu1(r * 2 + (k + 1))
                        fuse1(n0 + r * 2 + k, r * 2 + k, k)
                conv1(n0 + (BLOCKS - 1), 1)
                relu1(BLOCKS - 1)
                fuse1(n0 + (BLOCKS - 2), BLOCKS - 2, 0)
                fuse1(n0 + (BLOCKS - 1), BLOCKS - 1, 1)
                bends(n20 + BLOCKS, 1)
                block2_sample(image, 0, True, True)
                with act.Fori(1, BLOCKS - 1) as rb:
                    block2_sample(image, rb, False, True)
                block2_sample(image, BLOCKS - 1, False, False)
                block2_out(n0 + (BLOCKS - 1), BLOCKS - 1, 1)
                act.wait_ge(gn_vec, image * NORM_VEC + (NORM_AT[2] + 1))
                conv2(n0, 0, 0)
                norm_root(image, 2, 4)
                conv2(n0, 0, 1)
                normed(image, 2, 4)
                relu2(0)
                with act.Fori(0, BLOCKS // 2 - 1) as r:
                    for k in range(2):
                        for m in range(2):
                            conv2(n0 + r * 2 + (k + 1), 1 - k, m)
                        relu2(r * 2 + (k + 1))
                        for m in range(2):
                            fuse2(n0 + r * 2 + k, k, m, half0 + r)
                for m in range(2):
                    conv2(n0 + (BLOCKS - 1), 1, m)
                relu2(BLOCKS - 1)
                for k in range(2):
                    for m in range(2):
                        fuse2(n0 + (BLOCKS - 2 + k), k, m, half0 + (BLOCKS // 2 - 1))

            for s, n in ((bc_mm, 4), (fuse_mm, 2), (f2_mm, 4), (stored[0], 16), (stored[1], 16)):
                act.sem_inc(s, n)
            act.sem_inc(f_scan, 1)
            act.sem_inc(b_scan, 1)
            act.sem_inc(dec_b_in, 1)
            act.sem_inc(w_ready, 1)
            act.wait_ge(weights, NWEIGHTS)
            fn(a_neg[:], a_neg[:], ACT.Exp).then_inc(a_exp, 1)
            act.wait_ge(a_exp, 2)
            act.wait_ge(consts, 3)
            fn(logc[:, 2:3], logc[:, 3:4], ACT.Ln, bias=logc[:, 1:2]).then_inc(a_exp, 1)
            with act.Fori(0, IMAGES) as image:
                act.wait_ge(img_free, image + 1)
                lead(Tile(image * TILES, 0, 0))
                walk(act, image, tile_steps)
                T = Tile(image * TILES, TILES, 0)
                T.misc = -1
                outputs(T, TILES)
                norm_root(image, 0, CC)
                act.wait_ge(gn_vec, image * NORM_VEC + (NORM_AT[0] + CC + 9))
                for c in range(CC):
                    fn(img[:, c, 1:H + 1, 1:W + 1], img[:, c, 1:H + 1, 1:W + 1], ACT.Identity,
                       scale=gns[:, 4, c:c + 1], bias=gns[:, 5, c:c + 1]).then_inc(x1_mul, 1)
                layer1(image)

        @block.vector
        def _(dve):
            tt = nc.vector.tensor_tensor
            stt = nc.vector.scalar_tensor_tensor

            def step(T, i):
                i.then_inc(vec, 1)
                T.vec += 1

            def settled(T, but=0):
                dve.wait_ge(vec, T.at(VPER, T.vec - but))

            def gate(T, buf, h, tile_more):
                dve.wait_ge(y_done, T.at(GROUPS, GPH * (h + 1) - GROUPS * (1 - tile_more) + 1))
                step(T, stt(out=yg[:, h, :], in0=u[:, buf, h, :], scalar=ds2[:, h:h + 1], in1=p_y[:],
                            op0=ALU.mult, op1=ALU.add))
                settled(T)
                tt(yg[:, h, :], yg[:, h, :], gz[:, buf, h, :], ALU.mult).then_inc(yg_ok, 1)

            def deltas(T, buf, more):
                dve.wait_ge(soft_act, T.at(3, 3 * more + 3))
                step(T, nc.vector.tensor_scalar(sp_e[:], sp_e[:], SMALL, None, ALU.min))
                step(T, stt(out=delta[:, buf, :, :], in0=delta[:, buf, :, :], scalar=0.0, in1=du[:, buf, :, :],
                            op0=ALU.max, op1=ALU.add))
                settled(T)
                step(T, nc.vector.tensor_scalar(sp_u[:], sp_e[:], -0.25, 1.0 / 3.0, ALU.mult, ALU.add))
                settled(T)
                step(T, tt(sp_u[:], sp_u[:], sp_e[:], ALU.mult))
                for add in (-0.5, 1.0):
                    settled(T)
                    step(T, stt(out=sp_u[:], in0=sp_u[:], scalar=add, in1=sp_e[:], op0=ALU.add, op1=ALU.mult))
                settled(T)
                step(T, stt(out=delta[:, buf, :, :], in0=delta[:, buf, :, :], scalar=logc[:, 2:3], in1=sp_u[:],
                            op0=ALU.subtract, op1=ALU.add))
                settled(T)
                tt(du[:, buf, :, :], delta[:, buf, :, :], u[:, buf, :, :], ALU.mult).then_inc(delta_ok, 1)

            def tile_stats(T, t):
                dve.wait_ge(misc_free, T.at(PER, LEAD + (1 if T.last else 2)))
                for c in range(CC):
                    step(T, nc.vector.bn_stats(st0[:, c, bass.ds(t - 1, 1), :],
                                               img[:, c, bass.ds(t * TROWS - (TROWS - 1), TROWS), 1:W + 1]))

            def tile_steps(T, t):
                b, nb = T.buf, 1 - T.buf
                for gi in range(GROUPS):
                    for half in range(2):
                        if gi == 0:
                            dve.wait_ge(misc_free, T.at(PER, (LEAD if T.first else LEAD - 1) + 2 * half - 1))
                        dve.wait_ge(du_mm, T.at(2 * GROUPS, 2 * gi + half + 1))
                        pl = slice(4 * half, 4 * half + 4)
                        tt(planes(g, 2 * half, 2), p_du[:, 2 * half:2 * half + 2, :].rearrange("p q (a b) -> p q a b", a=2),
                           brep[:, pl, :].rearrange("p (q a) b -> p q a b", a=2), ALU.mult).then_inc(g_done, 1)
                    dve.wait_ge(g_done, T.at(2 * GROUPS, 2 * gi + 4))
                    dve.wait_ge(exp_done, T.at(4 * GROUPS, 4 * gi + 6))
                    flat = [t.rearrange("p n j -> p (n j)") for t in (hf, dec_f, g, hb, dec_b)]
                    nc.vector.tensor_tensor_scan(flat[0], flat[1], flat[2], 0.0, ALU.mult, ALU.add).then_inc(f_scan, 1)
                    dve.wait_ge(dec_b_in, T.at(GROUPS, gi + 2))
                    dve.wait_ge(y_done, T.at(GROUPS, gi + 1))
                    nc.vector.tensor_tensor_scan(flat[3][:, ::-1], flat[4][:, ::-1], flat[2][:, ::-1], 0.0,
                                                 ALU.mult, ALU.add).then_inc(b_scan, 1)
                    if gi == 0 and not T.first:
                        gate(T, nb, 1, 0)
                    if gi == 4:
                        if not T.first:
                            dve.wait_ge(misc_free, T.at(PER, LEAD + (1 if T.last else 2)))
                        gate(T, b, 0, 1)
                    if gi == 5 and not T.last:
                        deltas(T, nb, 1)
                    if gi == 2 and not T.first:
                        tile_stats(T, t)
                    dve.wait_ge(b_scan, T.at(GROUPS, gi + 2))
                    step(T, tt(hf[:], hf[:], hb[:], ALU.add))
                    settled(T)
                    by_quad = "p (q a) b -> p q a b"
                    tt(wc.rearrange(by_quad, a=2), planes(hf, 0, QUADS), crep[:, b, :, :].rearrange(by_quad, a=2),
                       ALU.mult).then_inc(w_ready, 1)

            def norm(image, use, cols, rows_stats, gain, shift):
                done = [NORM_AT[use]]

                def counted(i):
                    i.then_inc(gn_vec, 1)
                    done[0] += 1

                def ready():
                    dve.wait_ge(gn_vec, image * NORM_VEC + done[0])

                r = [gns[:, n, 0:cols] for n in range(8)]
                nc.vector.memset(gns[:, 7, :], 0.0)
                for c in range(cols):
                    counted(nc.vector.bn_aggr(mv[:, c, :], rows_stats(c)))
                dve.wait_ge(gn_mm, image * (2 * NORMS) + (2 * use + 1))
                counted(nc.vector.tensor_copy(r[1], p_misc[:, 0:cols]))
                ready()
                counted(tt(r[6], mv[:, 0:cols, 0], r[1], ALU.subtract))
                ready()
                counted(tt(r[7], r[6], r[6], ALU.mult))
                ready()
                counted(tt(r[0], r[7], mv[:, 0:cols, 1], ALU.add))
                dve.wait_ge(gn_mm, image * (2 * NORMS) + (2 * use + 2))
                counted(nc.vector.tensor_copy(r[2], p_misc[:, 0:cols]))
                dve.wait_ge(gn_act, image * NORMS + (use + 1))
                counted(nc.vector.reciprocal(r[3], r[3]))
                ready()
                counted(tt(r[4], r[3], gain, ALU.mult))
                ready()
                counted(tt(r[6], r[1], r[4], ALU.mult))
                ready()
                counted(tt(r[5], shift, r[6], ALU.subtract))

            class Count:
                def __init__(self, base, n):
                    self.base, self.n = base, n

                def step(self, i):
                    i.then_inc(vec1, 1)
                    self.n += 1

                def settled(self, but=0):
                    dve.wait_ge(vec1, self.base + (self.n - but))

            def offset_sum(v, n2):
                dve.wait_ge(off_mm, n2 + 1)
                dve.wait_ge(tanh_ok, n2 + 1)
                off, a4 = [grid(p_du[32 * dx:32 * dx + 4, 0, :]) for dx in range(3)], grid(acc[0:4, :])
                v.step(nc.vector.tensor_copy(a4, off[1]))
                v.settled()
                v.step(tt(a4[:, :, 1:W], off[0][:, :, 0:W - 1], a4[:, :, 1:W], ALU.add))
                v.settled()
                tt(a4[:, :, 0:W - 1], off[2][:, :, 1:W], a4[:, :, 0:W - 1], ALU.add).then_inc(off_sum, 1)

            def weigh(v, n2, m, diffs, to, low):
                for s in range(2):
                    if s == 0:
                        v.settled()
                    dve.wait_ge(bc_mm, n2 * 4 + (2 * m + s + 5))
                    v.step(stt(out=grid(to[s]), in0=grid(p_du[:, 1 + s, :]), scalar=0.0, in1=diffs[s][0],
                               op0=ALU.max, op1=ALU.mult))
                for s in range(2):
                    stt(out=grid(low[s]), in0=grid(p_du[:, 1 + s, :]), scalar=0.0, in1=diffs[s][1],
                        op0=ALU.min, op1=ALU.mult).then_inc(bc_used, 1)
                for s in range(2):
                    dve.wait_ge(bc_used, n2 * 4 + (2 * m + s + 3))
                    v.step(tt(to[s], to[s], low[s], ALU.add))

            def block1_sample(v, image, rb, nxt):
                n, n2 = image * BLOCKS + rb, image * (2 * BLOCKS) + rb
                start = v.n
                dve.wait_ge(pads, image * PADS + (PADS if not nxt else rb * 2 + 5))
                for m in range(2):
                    d, base, diffs = [], [], []
                    for s in range(2):
                        t, by = pp[:, 2 * m + s, :, :], 2 * s - 1
                        if m == 0:
                            d.append(df[:, s, :].rearrange("p (h w) -> p h w", w=W))
                            cs = slice(1 + by, 1 + by + W)
                            v.step(tt(d[s], t[:, rows9(rb, 1), cs], t[:, rows9(rb, 0), cs], ALU.subtract))
                            base.append(t[:, rows(rb, 1), cs])
                            diffs.append((d[s][:, 1:RB + 1, :], d[s][:, 0:RB, :]))
                        else:
                            d.append(df[:, s, 0:RB * (W + 1)].rearrange("p (h w) -> p h w", w=W + 1))
                            rs = rows(rb, 1 + by)
                            v.step(tt(d[s], t[:, rs, 1:PW], t[:, rs, 0:PW - 1], ALU.subtract))
                            base.append(t[:, rs, 1:W + 1])
                            diffs.append((d[s][:, :, 1:W + 1], d[s][:, :, 0:W]))
                    to, low = [tm[:, 0, :], tm[:, 1, :]], [tm[:, 2, :], tm[:, 3, :]]
                    weigh(v, n2, m, diffs, to, low)
                    for s in range(2):
                        v.settled(1)
                        v.step(tt(grid(to[s]), grid(to[s]), base[s], ALU.add))
                    v.settled()
                    v.step(tt(to[0], to[0], to[1], ALU.add))
                    if m == 0 and nxt:
                        offset_sum(v, n2 + 1)
                    v.settled()
                    dve.wait_ge(cen_mm, n * 2 + (m + 1))
                    stt(out=m1[:, m, cols(rb)], in0=CENTRE[m], scalar=v1[:, 1 + m:2 + m], in1=to[0],
                        op0=ALU.add, op1=ALU.add).then_inc(cen_used, 1)
                    dve.wait_ge(cen_used, n * 2 + (m + 3))
                    nc.vector.bn_stats(stat(m, rb), m1[:, m, cols(rb)]).then_inc(bn1, 1)
                assert v.n - start == (V1 if nxt else V1 - 2)

            def copy_back(n, rb):
                dve.wait_ge(fuse_ev, n + 3)
                nc.vector.tensor_copy(hr[:, rows(rb, 1), 1:W + 1], hz[:, rows(rb, 1), 1:W + 1]).then_inc(h1_ok, 1)
                for to, at in ((0, 1), (PW - 1, W)):
                    nc.vector.tensor_copy(hr[:, rows(rb, 1), to:to + 1], hz[:, rows(rb, 1), at:at + 1]).then_inc(h1_ok, 1)

            def block2_stats(n, rb):
                dve.wait_ge(o2_ev, n * 4 + 6)
                for c in range(4):
                    nc.vector.bn_stats(stat(c, rb), m2[:, c, cols(rb)]).then_inc(bn1, 1)

            def block2_sample(v, image, rb, first, nxt):
                n, n2 = image * BLOCKS + rb, image * (2 * BLOCKS) + (BLOCKS + rb)
                start = v.n
                v.step(tt(dv[:], hr[:, rows9(rb, 1), :], hr[:, rows9(rb, 0), :], ALU.subtract))
                v.step(tt(dh[:], hr[:, rows10(rb), 1:PW], hr[:, rows10(rb), 0:PW - 1], ALU.subtract))
                for m in range(2):
                    base, diffs = [], []
                    for s in range(2):
                        by = 2 * s - 1
                        if m == 0:
                            cs = slice(1 + by, 1 + by + W)
                            base.append(hr[:, rows(rb, 1), cs])
                            diffs.append((dv[:, 1:RB + 1, cs], dv[:, 0:RB, cs]))
                        else:
                            rs = slice(1 + by, 1 + by + RB)
                            base.append(hr[:, rows(rb, 1 + by), 1:W + 1])
                            diffs.append((dh[:, rs, 1:W + 1], dh[:, rs, 0:W]))
                    to, low = [sm[:, 2 * m, :], sm[:, 2 * m + 1, :]], [tn[:, 0, :], tn[:, 1, :]]
                    dve.wait_ge(o2_mm, n * 4 + (2 * m + 2))
                    weigh(v, n2, m, diffs, to, low)
                    for s in range(2):
                        v.settled(1 - s)
                        tt(grid(to[s]), grid(to[s]), base[s], ALU.add).then_inc(s_ok, 1)
                    if m == 0 and nxt:
                        offset_sum(v, n2 + 1)
                if not first:
                    block2_stats(n - 1, rb - 1)
                assert v.n - start == (V2 if nxt else V2 - 2)

            def layer1(image):
                n0, n20, at = image * BLOCKS, image * (2 * BLOCKS), image * VEC1
                offset_sum(Count(at, 0), n20)
                with dve.Fori(0, BLOCKS - 2) as rb:
                    block1_sample(Count(at + rb * V1, 2), image, rb, True)
                block1_sample(Count(at, 2 + V1 * (BLOCKS - 2)), image, BLOCKS - 2, True)
                block1_sample(Count(at, 2 + V1 * (BLOCKS - 1)), image, BLOCKS - 1, False)
                dve.wait_ge(bn1, image * BNS + 2 * BLOCKS)
                norm(image, 1, 2, lambda c: st1[:, c, :, :], v1[:, 3:5], v1[:, 5:7])
                for part in (hz[:, 0, :], hz[:, PH - 1, :], hz[:, 1:H + 1, 0:1], hz[:, 1:H + 1, PW - 1:PW]):
                    nc.vector.memset(part, 0.0).then_inc(hz_clear, 1)
                with dve.Fori(0, BLOCKS) as rb:
                    copy_back(n0 + rb, rb)
                dve.wait_ge(h1_ok, image * H1 + 3 * BLOCKS)
                for to, frm in ((0, 1), (PH - 1, H)):
                    nc.vector.tensor_copy(hr[:, to, :], hr[:, frm, :]).then_inc(h1_ok, 1)
                dve.wait_ge(h1_ok, image * H1 + H1)
                offset_sum(Count(at, V1 * BLOCKS), n20 + BLOCKS)
                first = V1 * BLOCKS + 2
                block2_sample(Count(at, first), image, 0, True, True)
                with dve.Fori(1, BLOCKS - 1) as rb:
                    block2_sample(Count(at + rb * V2, first), image, rb, False, True)
                block2_sample(Count(at, first + V2 * (BLOCKS - 1)), image, BLOCKS - 1, False, False)
                block2_stats(n0 + (BLOCKS - 1), BLOCKS - 1)
                dve.wait_ge(bn1, image * BNS + BNS)
                norm(image, 2, 4, lambda c: st1[:, c, :, :], v2[:, 6:10], v2[:, 10:14])
                with dve.Fori(0, BLOCKS // 2) as r:
                    for k in range(2):
                        for o in range(2):
                            dve.wait_ge(h2_ok, n20 + r * 4 + (2 * k + o + 3))
                            tt(grid(ht[:, k, o, :]), grid(ht[:, k, o, :]), img[:, o, rows(r * 2 + k, 1), 1:W + 1],
                               ALU.add).then_inc(res_ok, 1)

            for s, n in ((tanh_ok, 1), (o2_mm, 4)):
                dve.sem_inc(s, n)
            dve.sem_inc(y_done, 1)
            dve.sem_inc(img_free, 1)
            dve.memset(eps[:], EPS).then_inc(consts, 1)
            dve.memset(gns[:], 0.0).then_inc(consts, 1)
            for n, value in enumerate((-SMALL, 1.0 + SMALL, 0.0, 0.0)):
                dve.memset(logc[:, n:n + 1], value)
            dve.wait_ge(weights, NWEIGHTS)
            dve.wait_ge(a_exp, 1)
            nc.vector.tensor_scalar(a_neg[:], a_neg[:], -1.0, None, ALU.mult).then_inc(a_exp, 1)
            nc.vector.tensor_scalar(ds2[:], ds2[:], 2.0, None, ALU.mult)
            nc.vector.tensor_scalar(bdt2[:], bdt2[:], 2.0, None, ALU.mult).then_inc(consts, 1)
            dve.wait_ge(consts, 3)
            dve.wait_ge(a_exp, 3)
            with dve.Fori(0, IMAGES) as image:
                lead = Tile(image * TILES, 0, 0)
                lead.vec = 0
                deltas(lead, 0, 0)
                nc.vector.memset(dec_f[:, :, 0], 0.0).then_inc(zeroed, 1)
                nc.vector.memset(dec_b[:, :, TOK - 1], 0.0).then_inc(zeroed, 1)
                dve.wait_ge(zeroed, image * 2 + 2)
                walk(dve, image, tile_steps)
                T = Tile(image * TILES, TILES, 0)
                T.vec = -3
                gate(T, 1, 1, 0)
                dve.wait_ge(misc_free, T.at(PER, 1))
                for c in range(CC):
                    step(T, nc.vector.bn_stats(st0[:, c, TILES - 1, :], img[:, c, H - TROWS + 1:H + 1, 1:W + 1]))
                settled(T)
                norm(image, 0, CC, lambda c: st0[:, c, :, :], gn0[:, 0, :], gn0[:, 1, :])
                for c in range(CC):
                    dve.wait_ge(x_again, image * 32 + 32)
                    dve.wait_ge(x1_mul, image * CC + (c + 1))
                    tt(img[:, c, 1:H + 1, 1:W + 1], img[:, c, 1:H + 1, 1:W + 1],
                       x_old[:, c, :].rearrange("p (h w) -> p h w", w=W), ALU.add).then_inc(x1_ok, 1)
                layer1(image)


def kernel(**inputs):
    import numpy as np
    import concourse.bacc as bacc
    from concourse import mybir
    from concourse.bass_utils import run_bass_kernel_spmd
    a = {n: np.asarray(v) for n, v in inputs.items()}
    p = {n[len("L0_conv_"):]: v for n, v in a.items() if n.startswith("L0_conv_")}
    d = {"x": a["x"]}
    for n in ("W_in", "W_x", "W_dt", "W_out"):
        d[n] = p[n]
    d["Ds"] = p["Ds"].reshape(64, 1)
    d["b_dt"] = p["b_dt"].reshape(64, 1)
    d["A_logs"] = p["A_logs"].reshape(8, 128).T
    d["gn_w"] = p["gn_w"].reshape(2, 128).T
    d["gn_b"] = p["gn_b"].reshape(2, 128).T
    rows = np.arange(128)
    spread = np.zeros((128, 4, 4, 128), np.float32)
    gather = np.zeros((128, 4, 32), np.float32)
    for n in range(4):
        for q in range(4):
            spread[:, q, n, :] = rows[:, None] == 32 * q + 8 * n + rows[None, :] // 16
        gather[:, n, :] = 8 * n + rows[:, None] // 16 == np.arange(32)[None, :]
    d["spread"] = spread
    for name, at in (("copy_b", 0), ("copy_c", 16)):
        d[name] = np.stack([rows[:, None] == 32 * q + at + rows[None, :] % 16 for q in range(4)], axis=1).astype(np.float32)
    d["gather"] = gather
    d["same64"] = (rows[:, None] // 64 == rows[None, :] // 64).astype(np.float32) / 64
    one = {n[len("L1_conv_cv1_"):]: v for n, v in a.items() if n.startswith("L1_conv_cv1_")}
    two = {n[len("L1_conv_cv2_"):]: v for n, v in a.items() if n.startswith("L1_conv_cv2_")}

    def chunks(m):
        m = m.reshape((m.shape[0] // 128, 128) + m.shape[1:])
        return np.moveaxis(m, 0, 1).reshape(128, -1)

    def layout(b):
        conv = b["conv0_w"].transpose(1, 2, 3, 0)
        dsc = np.stack([b["dscx_w"], b["dscy_w"]]).transpose(2, 0, 3, 1)
        fuse = b["fuse_w"].T
        offs = np.stack([b["offx_w"][0], b["offx_w"][2], b["offy_w"][3], b["offy_w"][5]])
        off = np.zeros((offs.shape[1], 3, 3, 32), np.float32)
        off[..., 0:4] = offs.transpose(1, 2, 3, 0)
        return chunks(conv), chunks(dsc), chunks(fuse), chunks(off)

    conv, dsc, fuse, off = layout(one)
    d["block1"] = np.concatenate([conv, dsc, fuse], axis=1)
    d["off1"] = off.reshape(128, 2, 3, 96)
    conv, dsc, fuse, off = layout(two)
    d["block2"] = np.concatenate([conv, fuse], axis=1)
    d["off2"] = off.reshape(128, 3, 96)
    d["dsc2"] = dsc.reshape(128, 6, 256)
    pick = np.zeros((128, 4, 128), np.float32)
    for n in range(4):
        pick[n, n, :] = 1
    d["pick"] = pick
    d["same4"] = (rows[:, None] // 4 == rows[None, :] // 4).astype(np.float32) / 4
    names = ("conv0_b", "dscx_b", "dscy_b", "gnx_g", "gny_g", "gnx_b", "gny_b", "fuse_b")
    d["v1"] = np.stack([one[n] for n in names], axis=1)
    d["v2"] = np.concatenate([two[n].reshape(2, 128) for n in names]).T
    d["off_b"] = np.stack([np.array([b["offx_b"][0], b["offx_b"][2], b["offy_b"][3], b["offy_b"][5]]) for b in (one, two)], axis=1)
    d = {n: np.ascontiguousarray(v) for n, v in d.items()}
    nc = bacc.Bacc("TRN2", target_bir_lowering=False, num_devices=1)
    aps = {n: nc.dram_tensor("in_" + n, v.shape, mybir.dt.float32, kind="ExternalInput").ap() for n, v in d.items()}
    out = nc.dram_tensor("out_0", (4, 256, 64, 64), mybir.dt.float32, kind="ExternalOutput").ap()
    two_layer_program(nc, aps, out)
    r = run_bass_kernel_spmd(nc, [{"in_" + n: v for n, v in d.items()}], core_ids=[0])
    return r.results[0]["out_0"]
```

```python
import concourse.bass as bass
from concourse import mybir
from contextlib import ExitStack


def two_layer_program(nc, w, out):
    F32 = mybir.dt.float32
    ALU = mybir.AluOpType
    ACT = mybir.ActivationFunctionType

    P = 128
    IMAGES, CH, H, W = 4, 256, 64, 64
    CC = CH // P
    QUADS, TOK = 4, 8
    TILE = 256
    TROWS = TILE // W
    TILES = H * W // TILE
    WIDE = 2 * TILE
    HALVES = 2
    GROUPS = 8
    GPH = GROUPS // HALVES
    EPS = 1e-5
    SMALL = 1.0 / 64
    ARENA = 30216
    RB = 8
    BLOCKS = H // RB
    PH, PW = H + 2, W + 2

    ctx = ExitStack()
    with ctx:
        def sb(name, shape, dt=F32):
            return ctx.enter_context(nc.sbuf_tensor(name, shape, dt))

        def ps(name, shape):
            return ctx.enter_context(nc.psum_tensor(name, shape, F32))

        def sem(name):
            return ctx.enter_context(nc.semaphore(name))

        w_in_x = sb("w_in_x", [P, HALVES, P])
        w_in_z = sb("w_in_z", [P, HALVES, P])
        w_dts = sb("w_dts", [P, HALVES, 2 * QUADS])
        w_dt = sb("w_dt", [2 * QUADS, HALVES, P])
        w_bc = sb("w_bc", [P, HALVES, P])
        w_out = sb("w_out", [P, HALVES, P])
        spread = sb("spread", [P, QUADS, GPH, P])
        gather = sb("gather", [P, GPH, 32])
        copy_b = sb("copy_b", [P, QUADS, P])
        copy_c = sb("copy_c", [P, QUADS, P])
        a_neg = sb("a_neg", [P, GROUPS])
        ds = sb("ds", [P, HALVES])
        skip = sb("skip", [P, HALVES, P])
        bdt2 = sb("bdt2", [P, HALVES])
        gn0 = sb("gn0", [P, 2, CC])
        same64 = sb("same64", [P, P])

        img = sb("img", [P, CC, H + 2, W + 2])
        xt = sb("xt", [P, 2, CC, TILE])
        th = sb("th", [P, RB * W])
        wx = sb("wx", [P, 4224])
        c1_off = sb("c1_off", [P, CC, 3, 96])
        c2_off = sb("c2_off", [P, 3, 96])
        c2_dsc = sb("c2_dsc", [P, 6, 2 * P])
        pick = sb("pick", [P, 4, P])
        same4 = sb("same4", [P, P])
        v1 = sb("v1", [P, 8])
        v2 = sb("v2", [P, 16])
        off_b = sb("off_b", [4, 2])
        st1 = sb("st1", [P, 4, BLOCKS, 6])
        st0 = sb("st0", [P, CC, TILES, 6])
        gns = sb("gns", [P, 8, 4])
        mv = sb("mv", [P, 4, 2])
        eps = sb("eps", [P, 1])
        logc = sb("logc", [P, 6])

        arena = sb("arena", [P, ARENA])
        cursor = [0]

        def carve(*shape, at=None):
            n = 1
            for d in shape:
                n *= d
            o = cursor[0] if at is None else at
            cursor[0] = o + n
            assert cursor[0] <= ARENA, cursor[0]
            names = "abcd"[:len(shape)]
            flat = arena[:, o:o + n]
            if len(shape) == 1:
                return flat
            dims = {c: d for c, d in zip(names, shape)}
            return flat.rearrange("p (" + " ".join(names) + ") -> p " + " ".join(names), **dims)

        per_tile = carve(2, 4, HALVES * WIDE)
        u, delta, du = [per_tile[:, :, n, :].rearrange("p k (h n) -> p k h n", h=HALVES) for n in range(3)]
        sp_e, yg = [per_tile[:, k, 3, :].rearrange("p (h n) -> p h n", h=HALVES) for k in range(2)]
        g2 = carve(2, TILE * TOK)
        g = g2.rearrange("p k (n j) -> p k n j", j=TOK)
        wc = g2.rearrange("p k (j n) -> p k j n", j=TOK)
        dec_b = carve(TILE, TOK)
        dec_f = carve(TILE, TOK)
        hf = carve(TILE, TOK)
        hb = carve(TILE, TOK)
        brep = carve(TOK, TILE)
        crep = carve(2, TOK, TILE)
        bc = carve(WIDE)
        gz = carve(2, HALVES, WIDE)
        sp_u = carve(HALVES, WIDE, at=ARENA - HALVES * WIDE)
        dt8 = sp_u[:, 0, :]
        ident = carve(P, at=0)

        PIX = RB * W
        pp = carve(4, PH, PW, at=0)
        m1 = carve(2, H * W)
        x_old = m1
        df = carve(2, 9 * W)
        tm = carve(4, PIX)
        at1 = tm[:, 0:2, :]
        hr = carve(PH, PW, at=0)
        hz = carve(PH, PW)
        m2 = carve(4, H * W)
        dv = carve(9, PW)
        dh = carve(10, PW - 1)
        sm = carve(4, PIX)
        tn = carve(2, PIX)
        at2 = carve(2, 2, PIX, at=2 * PH * PW + 4 * H * W)
        ht = carve(2, 2, PIX)
        assert 4 * HALVES * WIDE <= PH * PW and cursor[0] <= ARENA - HALVES * WIDE
        acc = xt[:, 0, :, :].rearrange("p c n -> p (c n)")
        c1_conv = wx[:, 0:2304].rearrange("p (c t o) -> p c t o", c=CC, t=9)
        c1_dsc = wx[:, 2304:3840].rearrange("p (c k o) -> p c k o", c=CC, k=6)
        c1_fuse = wx[:, 3840:4224].rearrange("p (k o) -> p k o", k=3)
        c2_conv = wx[:, 0:2304].rearrange("p (t o) -> p t o", t=9)
        c2_fuse = wx[:, 2304:3840].rearrange("p (k o) -> p k o", k=6)

        p_dec = ps("p_dec", [P, 2, 512])
        p_du = ps("p_du", [P, 4, 512])
        p_y = ps("p_y", [P, 512])
        p_misc = ps("p_misc", [P, 512])

        weights = sem("weights")
        cleared = sem("cleared")
        consts = sem("consts")
        a_exp = sem("a_exp")
        x_in = [sem("x_in0"), sem("x_in1")]
        misc_full = sem("misc_full")
        misc_free = sem("misc_free")
        dec_mm = sem("dec_mm")
        exp_done = sem("exp_done")
        du_mm = sem("du_mm")
        g_done = sem("g_done")
        dec_f_in = sem("dec_f_in")
        f_scan = sem("f_scan")
        b_scan = sem("b_scan")
        zeroed = sem("zeroed")
        w_ready = sem("w_ready")
        y_done = sem("y_done")
        soft_act = sem("soft_act")
        delta_ok = sem("delta_ok")
        yg_ok = sem("yg_ok")
        vec = sem("vec")
        gn_vec = sem("gn_vec")
        gn_mm = sem("gn_mm")
        gn_act = sem("gn_act")
        x1_mul = sem("x1_mul")
        x1_ok = sem("x1_ok")
        x_again = sem("x_again")
        stored = [sem("stored0"), sem("stored1")]
        img_free = sem("img_free")

        pp_mm = sem("pp_mm")
        pp_ev = sem("pp_ev")
        pads = sem("pads")
        off_mm = sem("off_mm")
        off_sum = sem("off_sum")
        tanh_ok = sem("tanh_ok")
        bc_mm = sem("bc_mm")
        bc_used = sem("bc_used")
        cen_mm = sem("cen_mm")
        cen_used = sem("cen_used")
        conv_mm = sem("conv_mm")
        conv_ev = sem("conv_ev")
        relu_ok = sem("relu_ok")
        fuse_mm = sem("fuse_mm")
        fuse_ev = sem("fuse_ev")
        h1_ok = sem("h1_ok")
        hz_clear = sem("hz_clear")
        o2_mm = sem("o2_mm")
        o2_ev = sem("o2_ev")
        s_ok = sem("s_ok")
        vec1 = sem("vec1")
        bn1 = sem("bn1")
        a2_mm = sem("a2_mm")
        a2_ev = sem("a2_ev")
        relu2_ok = sem("relu2_ok")
        f2_mm = sem("f2_mm")
        h2_ok = sem("h2_ok")
        res_ok = sem("res_ok")
        w1_in = sem("w1_in")
        w2_in = sem("w2_in")

        xv = w["x"].rearrange("b (c p) h w -> b p c (h w)", p=P)
        outv = out.rearrange("b (c p) h w -> b p c (h w)", p=P)

        def planes(t, first, count):
            v = t.rearrange("p n (a q) -> p q a n", a=2)
            return v[:, first:first + count, :, :]

        LEAD, PER = 16, 17
        DSTEPS = 5
        NORM_AT = [0, CC + 9, 2 * CC + 18]
        NORM_VEC = NORM_AT[2] + 4 + 9
        NORMS = 3
        VPER = GROUPS + DSTEPS + 2
        PAIRS = TILES // 2
        XROWS = 2 * RB
        XPARTS = H // XROWS * CC

        class Tile:
            def __init__(self, base, k, buf, first=False, last=False):
                self.base, self.k, self.buf, self.first, self.last = base, k, buf, first, last
                self.misc = LEAD if first else LEAD - 1
                self.vec = DSTEPS if first else DSTEPS - 2

            def at(self, per_tile, more):
                return self.base * per_tile + (self.k * per_tile + more)

        def walk(eng, image, tile_steps):
            base = image * TILES
            for k in range(2):
                tile_steps(Tile(base, k, k, first=k == 0), k)
            with eng.Fori(1, PAIRS - 1) as tp:
                for k in range(2):
                    tile_steps(Tile(image * TILES + tp * 2, k, k), tp * 2 + k)
            for k in range(2):
                tile_steps(Tile(base, TILES - 2 + k, k, last=k == 1), TILES - 2 + k)

        PADS = 2 * BLOCKS + 2
        V1, V2 = 20, 12
        VEC1 = (V1 + V2) * BLOCKS
        BNS = 6 * BLOCKS
        H1 = 3 * BLOCKS + 2
        CENTRE = [p_du[:, 3, :], p_y[:]]

        def rows(rb, shift):
            return slice(rb * RB + shift, rb * RB + shift + RB) if isinstance(rb, int) else bass.ds(rb * RB + shift, RB)

        def rows9(rb, shift):
            at = rb * RB + shift
            return slice(at, at + RB + 1) if isinstance(rb, int) else bass.ds(at, RB + 1)

        def rows10(rb):
            return slice(rb * RB, rb * RB + RB + 2) if isinstance(rb, int) else bass.ds(rb * RB, RB + 2)

        def stat(c, rb):
            return st1[:, c, rb, :] if isinstance(rb, int) else st1[:, c, bass.ds(rb, 1), :]

        def cols(rb):
            return slice(rb * PIX, rb * PIX + PIX) if isinstance(rb, int) else bass.ds(rb * PIX, PIX)

        def grid(a):
            return a.rearrange("p (h w) -> p h w", w=W)

        WEIGHTS = ((a_neg, "A_logs"), (w_in_x, "W_in_x"), (w_in_z, "W_in_z"), (w_dts, "W_dts"), (w_dt, "W_dt"),
                   (w_bc, "W_BC"), (w_out, "W_out"), (ds, "Ds"), (bdt2, "b_dt"), (spread, "spread"), (gather, "gather"),
                   (copy_b, "copy_b"), (copy_c, "copy_c"), (ident, "ident"), (same64, "same64"), (gn0, "gn"),
                   (c1_off, "off1"), (c2_off, "off2"), (c2_dsc, "dsc2"), (pick, "pick"), (same4, "same4"), (v1, "v1"),
                   (v2, "v2"), (off_b, "off_b"))
        NWEIGHTS = 16 * len(WEIGHTS)

        block = ctx.enter_context(nc.Block())

        @block.sync
        def _(sp):
            for t, name in WEIGHTS:
                sp.dma_start(t[:], w[name]).then_inc(weights, 16)

            def load(image, tp, k, use, images=xv):
                if images is xv:
                    sp.wait_ge(misc_full, (image * TILES + tp * 2) * PER + (k * PER + use))
                at = tp * WIDE + k * TILE
                px = slice(at, at + TILE) if isinstance(tp, int) else bass.ds(at, TILE)
                sp.dma_start(xt[:, k, :, :], images[image, :, :, px]).then_inc(x_in[k], 16)

            def one_image(image, nxt):
                load(image, 1, 0, LEAD)
                load(image, 1, 1, 8)
                with sp.Fori(2, PAIRS) as tp:
                    load(image, tp, 0, 8)
                    load(image, tp, 1, 8)
                sp.dma_start(wx[:, 0:3840], w["block1"][:, 0:3840]).then_inc(w1_in, 16)
                sp.wait_ge(w_ready, image * (TILES * GROUPS) + (TILES * GROUPS + 1))
                sp.dma_start(wx[:, 3840:4224], w["block1"][:, 3840:4224]).then_inc(w1_in, 16)
                sp.dma_start(x_old[:], xv[image]).then_inc(x_again, 16)
                sp.wait_ge(fuse_mm, image * BLOCKS + (BLOCKS + 2))
                sp.dma_start(wx[:, 0:3840], w["block2"]).then_inc(w2_in, 16)
                if nxt:
                    sp.wait_ge(o2_mm, image * (4 * BLOCKS) + (4 * BLOCKS + 4))
                    for k in range(2):
                        load(image, 0, k, LEAD, images=xv[1:IMAGES])
                with sp.Fori(0, BLOCKS // 2) as r:
                    for k in range(2):
                        sp.wait_ge(res_ok, image * (2 * BLOCKS) + r * 4 + (2 * k + 2))
                        sp.dma_start(outv[image, :, :, bass.ds(r * (2 * PIX) + k * PIX, PIX)],
                                     ht[:, k, :, :]).then_inc(stored[k], 16)
                for k in range(2):
                    sp.wait_ge(stored[k], image * (8 * BLOCKS) + (8 * BLOCKS + 16))
                sp.sem_inc(img_free, 1)

            for k in range(2):
                load(0, 0, k, LEAD)
            with sp.Fori(0, IMAGES - 1) as image:
                one_image(image, True)
            one_image(IMAGES - 1, False)

        @block.gpsimd
        def _(pool):
            for t in (img, th):
                nc.gpsimd.memset(t[:], 0.0).then_inc(cleared, 1)

        @block.tensor
        def _(pe):
            mm = nc.tensor.matmul
            QS = [slice(32 * q, 32 * q + 32) for q in range(QUADS)]

            def misc(T):
                pe.wait_ge(misc_free, T.at(PER, T.misc + 1))
                T.misc += 1

            def inner(T, buf, h):
                misc(T)
                mm(p_misc[:], w_in_x[:, h, :], xt[:, buf, :, :], start=True, stop=True).then_inc(misc_full, 1)

            def gates(T, buf, h):
                misc(T)
                i = mm(p_misc[:], w_in_z[:, h, :], xt[:, buf, :, :], start=True, stop=True)
                i.then_inc(misc_full, 1)

            def step_sizes(T, buf):
                misc(T)
                for h in range(HALVES):
                    i = mm(p_misc[0:8, :], w_dts[:, h, :], u[:, buf, h, :], start=h == 0, stop=h == 1)
                i.then_inc(misc_full, 1)

            def step_sizes_out(T, h):
                misc(T)
                mm(p_misc[:], w_dt[:, h, :], dt8[0:8, :], start=True, stop=True).then_inc(misc_full, 1)

            def b_and_c(T, buf):
                misc(T)
                for h in range(HALVES):
                    i = mm(p_misc[:], w_bc[:, h, :], u[:, buf, h, :], start=h == 0, stop=h == 1)
                i.then_inc(misc_full, 1)

            def repeat(T, wt, q):
                misc(T)
                mm(p_misc[:], wt[:, q, :], bc[:], start=True, stop=True).then_inc(misc_full, 1)

            def outputs(T):
                pe.wait_ge(yg_ok, T.at(HALVES, 0))
                misc(T)
                for h in range(HALVES):
                    i = mm(p_misc[:], w_out[:, h, :], yg[:, h, :], start=h == 0, stop=h == 1)
                i.then_inc(misc_full, 1)

            def spread_delta(T, buf, gi, more, q):
                pe.wait_ge(exp_done, T.at(4 * GROUPS, 4 * more + q + 1))
                mm(p_dec[:, q % 2, :], spread[:, q, gi % GPH, :], delta[:, buf, gi // GPH, :],
                   start=True, stop=True).then_inc(dec_mm, 1)

            def spread_du(T, buf, gi, more, half):
                pe.wait_ge(g_done, T.at(2 * GROUPS, 2 * more + half + 1))
                for q in (2 * half, 2 * half + 1):
                    i = mm(p_du[:, q, :], spread[:, q, gi % GPH, :], du[:, buf, gi // GPH, :],
                           start=True, stop=True)
                i.then_inc(du_mm, 1)

            def gather_y(T, gi):
                pe.wait_ge(w_ready, T.at(GROUPS, gi + 2))
                if gi % GPH == 0:
                    h = gi // GPH
                    mm(p_y[:], skip[:, h, :], u[:, T.buf, h, :], start=True, stop=False)
                for q in range(QUADS):
                    i = mm(p_y[QS[q], :], gather[:, gi % GPH, :], wc[:, gi % 2, 2 * q:2 * q + 2, :],
                           start=False, stop=gi % GPH == GPH - 1)
                i.then_inc(y_done, 1)

            def misc_use(T, gi, slot):
                nb = 1 - T.buf
                if (gi, slot) == (1, 2) and not T.first:
                    outputs(T)
                if T.last:
                    return
                if (gi, slot) == (1, 1):
                    pe.wait_ge(x_in[nb], T.at(8, 16 if nb else 24))
                    inner(T, nb, 0)
                if (gi, slot) == (1, 3):
                    inner(T, nb, 1)
                if (gi, slot) == (2, 1):
                    step_sizes(T, nb)
                if (gi, slot) in ((2, 2), (3, 1)):
                    step_sizes_out(T, gi - 2)
                if (gi, slot) == (3, 2):
                    b_and_c(T, nb)
                if (gi, slot) in ((4, 2), (4, 3)):
                    gates(T, nb, slot - 2)
                if (gi, slot) in ((5, 1), (5, 2)):
                    repeat(T, copy_c, slot - 1)
                if (gi, slot) in ((6, 2), (6, 3)):
                    repeat(T, copy_b, slot - 2)
                if (gi, slot) in ((7, 0), (7, 1)):
                    repeat(T, copy_b, slot + 2)
                if (gi, slot) in ((7, 2), (7, 3)):
                    repeat(T, copy_c, slot)

            def tile_steps(T, t):
                b, nb = T.buf, 1 - T.buf
                for gi in range(GROUPS):
                    dec_of = (b, gi + 1) if gi < 7 else (nb, 0)
                    du_of = (b, gi + 2) if gi < 6 else (nb, gi - 6)
                    misc_use(T, gi, 0)
                    for half in range(2):
                        if gi < 7 or not T.last:
                            spread_delta(T, *dec_of, gi + 1, 2 * half)
                            spread_delta(T, *dec_of, gi + 1, 2 * half + 1)
                        misc_use(T, gi, 1 + half)
                    if gi == 6 and not T.last:
                        pe.wait_ge(delta_ok, T.at(1, 2))
                    for half in range(2):
                        if gi < 6 or not T.last:
                            spread_du(T, *du_of, gi + 2, half)
                        misc_use(T, gi, 3 + half)
                    gather_y(T, gi)

            def begin(T, n):
                if n == 0:
                    pe.wait_ge(x_in[0], T.at(8, 16))
                    T.misc = 0
                if n < 2:
                    inner(T, 0, n)
                if n == 2:
                    step_sizes(T, 0)
                if n > 2:
                    step_sizes_out(T, n - 3)

            def lead(T):
                T.misc = 5
                b_and_c(T, 0)
                pe.wait_ge(delta_ok, T.at(1, 1))
                spread_delta(T, 0, 0, 0, 0)
                spread_delta(T, 0, 0, 0, 1)
                for q in range(QUADS):
                    repeat(T, copy_b, q)
                spread_delta(T, 0, 0, 0, 2)
                spread_delta(T, 0, 0, 0, 3)
                for gi in range(2):
                    for half in range(2):
                        spread_du(T, 0, gi, gi, half)
                    if gi == 0:
                        for q in range(QUADS):
                            repeat(T, copy_c, q)
                gates(T, 0, 0)
                gates(T, 0, 1)

            def norm_matmuls(image, use, cols, same):
                pe.wait_ge(gn_vec, image * NORM_VEC + (NORM_AT[use] + cols))
                mm(p_misc[:, 0:cols], same[:], mv[:, 0:cols, 0], start=True, stop=True).then_inc(gn_mm, 1)
                pe.wait_ge(gn_vec, image * NORM_VEC + (NORM_AT[use] + cols + 4))
                mm(p_misc[:, 0:cols], same[:], gns[:, 0, 0:cols], start=True, stop=True).then_inc(gn_mm, 1)

            def side_tap(n, rb, i):
                pe.wait_ge(pp_ev, n * 4 + (i + 1))
                for c in range(CC):
                    k = mm(p_dec[:, i % 2, :], c1_dsc[:, c, 3 * (i // 2) + 2 * (i % 2), :],
                           img[:, c, rows(rb, 1), 1:W + 1], start=c == 0, stop=c == CC - 1)
                k.then_inc(pp_mm, 1)

            def offsets(n2, rb, wt, src):
                pe.wait_ge(off_sum, n2 + 1)
                parts = [(c, dy) for c in range(len(wt)) for dy in range(3)]
                for c, dy in parts:
                    k = mm(p_du[0:96, 0, :], wt[c][:, dy, :], src[c][:, rows(rb, dy), 1:W + 1],
                           start=(c, dy) == parts[0], stop=(c, dy) == parts[-1])
                k.then_inc(off_mm, 1)

            def bend(n2, i):
                if i == 0:
                    pe.wait_ge(tanh_ok, n2 + 2)
                pe.wait_ge(bc_used, n2 * 4 + (i + 1))
                mm(p_du[:, 1 + i % 2, :], pick[:, i, :], th[:], start=True, stop=True).then_inc(bc_mm, 1)

            def centre(n, rb, m):
                pe.wait_ge(cen_used, n * 2 + (m + 1))
                for c in range(CC):
                    k = mm(CENTRE[m], c1_dsc[:, c, 3 * m + 1, :], img[:, c, rows(rb, 1), 1:W + 1],
                           start=c == 0, stop=c == CC - 1)
                k.then_inc(cen_mm, 1)

            OFF1 = ([c1_off[:, c, :, :] for c in range(CC)], [img[:, c, :, :] for c in range(CC)])
            OFF2 = ([c2_off[:, :, :]], [hz])

            def block1_sample(image, rb, ahead, nxt):
                n, n2 = image * BLOCKS + rb, image * (2 * BLOCKS) + rb

                def later(i):
                    if ahead:
                        side_tap(n + 2, rb + 2, i)

                bend(n2, 0)
                bend(n2, 1)
                if nxt:
                    offsets(n2 + 1, rb + 1, *OFF1)
                centre(n, rb, 0)
                centre(n, rb, 1)
                later(0)
                later(1)
                bend(n2, 2)
                later(2)
                later(3)
                bend(n2, 3)

            def conv1(n, rb, k):
                pe.wait_ge(conv_ev, n + 1)
                for c in range(CC):
                    for tap in range(9):
                        i = mm(p_dec[:, k, :], c1_conv[:, c, tap, :],
                               img[:, c, rows(rb, tap // 3), tap % 3:tap % 3 + W],
                               start=c == 0 and tap == 0, stop=c == CC - 1 and tap == 8)
                i.then_inc(conv_mm, 1)

            def fuse1(n, rb, k):
                pe.wait_ge(conv_ev, n + 3)
                pe.wait_ge(relu_ok, n * 2 + 2)
                pe.wait_ge(fuse_ev, n + 1)
                mm(p_du[:, k, :], c1_fuse[:, 0, :], at1[:, k, :], start=True, stop=False)
                mm(p_du[:, k, :], c1_fuse[:, 1, :], m1[:, 0, cols(rb)], start=False, stop=False)
                mm(p_du[:, k, :], c1_fuse[:, 2, :], m1[:, 1, cols(rb)], start=False, stop=True).then_inc(fuse_mm, 1)

            def block2_out(n, rb, m):
                pe.wait_ge(s_ok, n * 4 + (2 * m + 2))
                for o in range(2):
                    pe.wait_ge(o2_ev, n * 4 + (2 * m + o + 1))
                    os = slice(P * o, P * o + P)
                    mm(p_dec[:, o, :], c2_dsc[:, 3 * m + 1, os], hz[:, rows(rb, 1), 1:W + 1], start=True, stop=False)
                    mm(p_dec[:, o, :], c2_dsc[:, 3 * m, os], sm[:, 2 * m, :], start=False, stop=False)
                    mm(p_dec[:, o, :], c2_dsc[:, 3 * m + 2, os], sm[:, 2 * m + 1, :],
                       start=False, stop=True).then_inc(o2_mm, 1)

            def block2_sample(image, rb, first, nxt):
                n, n2 = image * BLOCKS + rb, image * (2 * BLOCKS) + (BLOCKS + rb)
                bend(n2, 0)
                bend(n2, 1)
                if not first:
                    block2_out(n - 1, rb - 1, 1)
                if nxt:
                    offsets(n2 + 1, rb + 1, *OFF2)
                bend(n2, 2)
                bend(n2, 3)
                block2_out(n, rb, 0)

            def conv2(n, rb, m):
                pe.wait_ge(a2_ev, n * 2 + (m + 1))
                for tap in range(9):
                    i = mm(p_dec[:, m, :], c2_conv[:, tap, P * m:P * m + P],
                           hz[:, rows(rb, tap // 3), tap % 3:tap % 3 + W], start=tap == 0, stop=tap == 8)
                i.then_inc(a2_mm, 1)

            def fuse2(n, rb, k, o):
                if o == 0:
                    pe.wait_ge(a2_ev, n * 2 + 4)
                    pe.wait_ge(relu2_ok, n * 4 + 4)
                pe.wait_ge(h2_ok, n * 2 + (o + 1))
                os = slice(P * o, P * o + P)
                for c in range(2):
                    mm(p_du[:, o, :], c2_fuse[:, c, os], at2[:, k, c, :], start=c == 0, stop=False)
                for c in range(4):
                    i = mm(p_du[:, o, :], c2_fuse[:, 2 + c, os], m2[:, c, cols(rb)], start=False, stop=c == 3)
                i.then_inc(f2_mm, 1)

            def layer1(image, nxt):
                pe.wait_ge(x1_ok, image * XPARTS + CC)
                pe.wait_ge(w1_in, image * 32 + 32)
                n0, n20 = image * BLOCKS, image * (2 * BLOCKS)
                for i in range(4):
                    side_tap(n0, 0, i)
                offsets(n20, 0, *OFF1)
                pe.wait_ge(x1_ok, image * XPARTS + XPARTS)
                for i in range(4):
                    side_tap(n0 + 1, 1, i)
                with pe.Fori(0, BLOCKS - 2) as rb:
                    block1_sample(image, rb, True, True)
                block1_sample(image, BLOCKS - 2, False, True)
                block1_sample(image, BLOCKS - 1, False, False)
                conv1(n0, 0, 0)
                norm_matmuls(image, 1, 2, same4)
                with pe.Fori(0, BLOCKS // 2 - 1) as r:
                    for k in range(2):
                        conv1(n0 + r * 2 + (k + 1), r * 2 + (k + 1), 1 - k)
                        fuse1(n0 + r * 2 + k, r * 2 + k, k)
                conv1(n0 + (BLOCKS - 1), BLOCKS - 1, 1)
                fuse1(n0 + (BLOCKS - 2), BLOCKS - 2, 0)
                fuse1(n0 + (BLOCKS - 1), BLOCKS - 1, 1)
                pe.wait_ge(fuse_ev, n0 + (BLOCKS + 2))
                pe.wait_ge(hz_clear, image * 4 + 4)
                offsets(n20 + BLOCKS, 0, *OFF2)
                block2_sample(image, 0, True, True)
                with pe.Fori(1, BLOCKS - 1) as rb:
                    block2_sample(image, rb, False, True)
                block2_sample(image, BLOCKS - 1, False, False)
                block2_out(n0 + (BLOCKS - 1), BLOCKS - 1, 1)
                pe.wait_ge(w2_in, image * 16 + 16)
                pe.wait_ge(o2_ev, n0 * 4 + (4 * BLOCKS + 2))
                conv2(n0, 0, 0)
                norm_matmuls(image, 2, 4, same4)
                conv2(n0, 0, 1)
                with pe.Fori(0, BLOCKS // 2 - 1) as r:
                    for k in range(2):
                        for m in range(2):
                            conv2(n0 + r * 2 + (k + 1), r * 2 + (k + 1), m)
                        for m in range(2):
                            fuse2(n0 + r * 2 + k, r * 2 + k, k, m)
                T = Tile(image * TILES, TILES, 0)
                for m in range(2):
                    if nxt:
                        begin(T, m)
                    conv2(n0 + (BLOCKS - 1), BLOCKS - 1, m)
                for k in range(2):
                    for m in range(2):
                        if nxt and 2 * k + m < 3:
                            begin(T, 2 + 2 * k + m)
                        fuse2(n0 + (BLOCKS - 2 + k), BLOCKS - 2 + k, k, m)

            for s, n in ((pp_ev, 2), (off_sum, 1), (bc_used, 2), (cen_used, 2), (conv_ev, 2), (fuse_ev, 2), (o2_ev, 2),
                         (a2_ev, 2), (h2_ok, 2)):
                pe.sem_inc(s, n)
            pe.sem_inc(exp_done, 2)
            pe.sem_inc(g_done, 2)
            pe.sem_inc(misc_free, 1)
            pe.sem_inc(misc_full, 2 * PER)
            pe.wait_ge(weights, NWEIGHTS)
            pe.wait_ge(cleared, 2)

            def one_image(image, nxt):
                lead(Tile(image * TILES, 0, 0))
                walk(pe, image, tile_steps)
                T = Tile(image * TILES, TILES, 0)
                T.misc = -1
                outputs(T)
                norm_matmuls(image, 0, CC, same64)
                layer1(image, nxt)

            T = Tile(0, 0, 0)
            for n in range(5):
                begin(T, n)
            with pe.Fori(0, IMAGES - 1) as image:
                one_image(image, True)
            one_image(IMAGES - 1, False)

        @block.scalar
        def _(act):
            fn = nc.scalar.activation

            def full(T):
                act.wait_ge(misc_full, T.at(PER, T.misc + 1 + 2 * PER))
                T.misc += 1

            def inner(T, buf, h):
                full(T)
                fn(u[:, buf, h, :], p_misc[:], ACT.Identity).then_inc(misc_free, 1)

            def gates(T, buf, h):
                full(T)
                i = fn(gz[:, buf, h, :], p_misc[:], ACT.Gelu)
                i.then_inc(misc_free, 1)

            def step_sizes(T):
                full(T)
                fn(dt8[0:8, :], p_misc[0:8, :], ACT.Identity).then_inc(misc_free, 1)

            def soft_in(T, buf, h):
                full(T)
                fn(delta[:, buf, h, :], p_misc[:], ACT.Identity, bias=bdt2[:, h:h + 1])
                fn(sp_e[:, h, :], p_misc[:], ACT.Abs, bias=bdt2[:, h:h + 1]).then_inc(misc_free, 1)

            def softplus(T, buf, more):
                act.wait_ge(misc_free, T.at(PER, T.misc + 1))
                fn(sp_e[:], sp_e[:], ACT.Exp, scale=-1.0).then_inc(soft_act, 1)
                act.wait_ge(soft_act, T.at(5, 5 * more + 1))
                fn(sp_u[:], sp_e[:], ACT.Relu, bias=logc[:, 0:1]).then_inc(soft_act, 1)
                act.wait_ge(soft_act, T.at(5, 5 * more + 2))
                fn(du[:, buf, :, :], sp_u[:], ACT.Ln, bias=logc[:, 1:2]).then_inc(soft_act, 1)
                act.wait_ge(soft_act, T.at(5, 5 * more + 3))
                fn(sp_u[:], sp_e[:], ACT.Relu, scale=-1.0, bias=logc[:, 4:5]).then_inc(soft_act, 1)
                act.wait_ge(soft_act, T.at(5, 5 * more + 4))
                fn(sp_u[:], sp_u[:], ACT.Square, scale=-0.5, bias=logc[:, 5:6]).then_inc(soft_act, 1)

            def b_and_c(T):
                full(T)
                fn(bc[:], p_misc[:], ACT.Identity).then_inc(misc_free, 1)

            def repeat(T, dst, q):
                full(T)
                fn(dst[:, 2 * q:2 * q + 2, :], p_misc[:].rearrange("p (a b) -> p a b", a=2),
                   ACT.Identity).then_inc(misc_free, 1)

            def outputs(T, t):
                full(T)
                rows = bass.ds(t * TROWS - (TROWS - 1), TROWS)
                fn(img[:, :, rows, 1:W + 1], p_misc[:].rearrange("p (c r w) -> p c r w", c=CC, w=W),
                   ACT.Identity).then_inc(misc_free, 1)

            def exps(T, gi, more, q):
                if q == 0:
                    act.wait_ge(b_scan, T.at(GROUPS, more + 1))
                    act.wait_ge(dec_f_in, T.at(GROUPS, more + 1))
                act.wait_ge(dec_mm, T.at(4 * GROUPS, 4 * more + q + 1))
                bank = p_dec[:, q % 2, :].rearrange("p (a b) -> p a b", a=2)
                if q < QUADS - 1:
                    fn(planes(dec_b, q, 1), bank.rearrange("p (o a) b -> p o a b", o=1),
                       ACT.Exp, scale=a_neg[:, gi:gi + 1]).then_inc(exp_done, 1)
                else:
                    fn(dec_b[:, :, q], bank[:, 0, :], ACT.Exp, scale=a_neg[:, gi:gi + 1])
                    act.wait_ge(f_scan, T.at(GROUPS, more + 1))
                    fn(dec_f[:, :, TOK - 1], bank[:, 1, :], ACT.Exp, scale=a_neg[:, gi:gi + 1]).then_inc(exp_done, 1)
                    act.wait_ge(exp_done, T.at(4 * GROUPS, 4 * more + 6))
                    fn(dec_f[:, :, 1:TOK - 1], dec_b[:, :, 1:TOK - 1], ACT.Identity).then_inc(dec_f_in, 1)

            def misc_use(T, t, gi, slot):
                nb = 1 - T.buf
                if (gi, slot) == (1, 2) and not T.first:
                    outputs(T, t)
                if T.last:
                    return
                if (gi, slot) == (1, 1):
                    if not T.first:
                        act.wait_ge(yg_ok, T.at(HALVES, 0))
                    inner(T, nb, 0)
                if (gi, slot) == (1, 3):
                    inner(T, nb, 1)
                if (gi, slot) == (2, 1):
                    step_sizes(T)
                if (gi, slot) in ((2, 2), (3, 1)):
                    soft_in(T, nb, gi - 2)
                if (gi, slot) == (3, 2):
                    b_and_c(T)
                if (gi, slot) == (3, 4):
                    softplus(T, nb, 1)
                if (gi, slot) in ((4, 2), (4, 3)):
                    gates(T, nb, slot - 2)
                if (gi, slot) in ((5, 1), (5, 2)):
                    repeat(T, crep[:, nb, :, :], slot - 1)
                if (gi, slot) in ((6, 2), (6, 3)):
                    act.wait_ge(g_done, T.at(2 * GROUPS, 2 * 7 + 3))
                    repeat(T, brep, slot - 2)
                if (gi, slot) in ((7, 0), (7, 1)):
                    act.wait_ge(g_done, T.at(2 * GROUPS, 2 * 7 + 4))
                    repeat(T, brep, slot + 2)
                if (gi, slot) in ((7, 2), (7, 3)):
                    repeat(T, crep[:, nb, :, :], slot)

            def tile_steps(T, t):
                for gi in range(GROUPS):
                    misc_use(T, t, gi, 0)
                    for half in range(2):
                        if gi < 7 or not T.last:
                            exps(T, (gi + 1) % GROUPS, gi + 1, 2 * half)
                            exps(T, (gi + 1) % GROUPS, gi + 1, 2 * half + 1)
                        misc_use(T, t, gi, 1 + half)
                    misc_use(T, t, gi, 3)
                    misc_use(T, t, gi, 4)

            def begin(T, n):
                if n == 0:
                    T.misc = 0
                if n < 2:
                    inner(T, 0, n)
                if n == 2:
                    step_sizes(T)
                if n > 2:
                    soft_in(T, 0, n - 3)
                if n == 4:
                    softplus(T, 0, 0)

            def lead(T, image):
                T.misc = 5
                b_and_c(T)
                exps(T, 0, 0, 0)
                exps(T, 0, 0, 1)
                for q in range(QUADS):
                    repeat(T, brep, q)
                exps(T, 0, 0, 2)
                exps(T, 0, 0, 3)
                for q in range(QUADS):
                    repeat(T, crep[:, 0, :, :], q)
                act.wait_ge(img_free, image + 1)
                gates(T, 0, 0)
                gates(T, 0, 1)

            def norm_root(image, use, cols):
                act.wait_ge(gn_vec, image * NORM_VEC + (NORM_AT[use] + cols + 5))
                fn(gns[:, 3, 0:cols], gns[:, 2, 0:cols], ACT.Sqrt, bias=eps[:]).then_inc(gn_act, 1)

            def tap_out(n, rb, i):
                act.wait_ge(pp_mm, n * 4 + (i + 1))
                fn(pp[:, i, rows(rb, 1), 1:W + 1], grid(p_dec[:, i % 2, :]), ACT.Identity).then_inc(pp_ev, 1)

            def tap_edges(n, rb):
                act.wait_ge(pp_ev, n * 4 + 6)
                for to, at in ((0, 1), (PW - 1, W)):
                    fn(pp[:, :, rows(rb, 1), to:to + 1], pp[:, :, rows(rb, 1), at:at + 1], ACT.Identity).then_inc(pads, 1)

            def tap_edge_rows(image, to, at, count):
                act.wait_ge(pads, image * PADS + count)
                fn(pp[:, :, to, :], pp[:, :, at, :], ACT.Identity).then_inc(pads, 1)

            def bends(n2, block):
                act.wait_ge(off_sum, n2 + 2)
                act.wait_ge(bc_mm, n2 * 4 + 4)
                fn(th[0:4, :], acc[0:4, :], ACT.Tanh, bias=off_b[:, block:block + 1]).then_inc(tanh_ok, 1)

            def block1_sample(image, rb, ahead, nxt):
                n, n2 = image * BLOCKS + rb, image * (2 * BLOCKS) + rb
                if ahead:
                    for i in range(4):
                        tap_out(n + 2, rb + 2, i)
                    tap_edges(n + 2, rb + 2)
                if nxt:
                    bends(n2 + 1, 0)

            def conv1(n, k):
                act.wait_ge(conv_mm, n + 1)
                act.wait_ge(fuse_mm, n + 1)
                fn(at1[:, k, :], p_dec[:, k, :], ACT.Silu, bias=v1[:, 0:1]).then_inc(conv_ev, 1)

            def relu1(rb):
                for m in range(2):
                    fn(m1[:, m, cols(rb)], m1[:, m, cols(rb)], ACT.Relu,
                       scale=gns[:, 4, m:m + 1], bias=gns[:, 5, m:m + 1]).then_inc(relu_ok, 1)

            def fuse1(n, rb, k):
                act.wait_ge(fuse_mm, n + 3)
                fn(hz[:, rows(rb, 1), 1:W + 1], grid(p_du[:, k, :]), ACT.Silu, bias=v1[:, 7:8]).then_inc(fuse_ev, 1)

            def block2_out(n, rb, m):
                for o in range(2):
                    act.wait_ge(o2_mm, n * 4 + (2 * m + o + 5))
                    fn(m2[:, 2 * m + o, cols(rb)], p_dec[:, o, :], ACT.Identity,
                       bias=v2[:, 2 + 2 * m + o:3 + 2 * m + o]).then_inc(o2_ev, 1)

            def block2_sample(image, rb, first, nxt):
                n, n2 = image * BLOCKS + rb, image * (2 * BLOCKS) + (BLOCKS + rb)
                if not first:
                    block2_out(n - 1, rb - 1, 1)
                if nxt:
                    bends(n2 + 1, 1)
                block2_out(n, rb, 0)

            def conv2(n, k, m):
                act.wait_ge(a2_mm, n * 2 + (m + 1))
                act.wait_ge(f2_mm, n * 2 + 2)
                fn(at2[:, k, m, :], p_dec[:, m, :], ACT.Silu, bias=v2[:, m:m + 1]).then_inc(a2_ev, 1)

            def relu2(rb):
                for c in range(4):
                    fn(m2[:, c, cols(rb)], m2[:, c, cols(rb)], ACT.Relu,
                       scale=gns[:, 4, c:c + 1], bias=gns[:, 5, c:c + 1]).then_inc(relu2_ok, 1)

            def fuse2(n, k, o, half):
                act.wait_ge(f2_mm, n * 2 + (o + 5))
                if o == 0:
                    act.wait_ge(stored[k], half * 16 + 16)
                fn(ht[:, k, o, :], p_du[:, o, :], ACT.Silu, bias=v2[:, 14 + o:15 + o]).then_inc(h2_ok, 1)

            def normed(image, use, cols):
                act.wait_ge(gn_vec, image * NORM_VEC + (NORM_AT[use] + cols + 9))

            def layer1(image, nxt):
                n0, n20, half0 = image * BLOCKS, image * (2 * BLOCKS), image * (BLOCKS // 2)
                for rb in range(2):
                    for i in range(4):
                        tap_out(n0 + rb, rb, i)
                    tap_edges(n0 + rb, rb)
                    if rb == 0:
                        tap_edge_rows(image, 0, 1, 2)
                        bends(n20, 0)
                with act.Fori(0, BLOCKS - 2) as rb:
                    block1_sample(image, rb, True, True)
                tap_edge_rows(image, PH - 1, H, PADS - 1)
                block1_sample(image, BLOCKS - 2, False, True)
                act.wait_ge(gn_vec, image * NORM_VEC + (NORM_AT[1] + 1))
                conv1(n0, 0)
                norm_root(image, 1, 2)
                normed(image, 1, 2)
                relu1(0)
                with act.Fori(0, BLOCKS // 2 - 1) as r:
                    for k in range(2):
                        conv1(n0 + r * 2 + (k + 1), 1 - k)
                        relu1(r * 2 + (k + 1))
                        fuse1(n0 + r * 2 + k, r * 2 + k, k)
                conv1(n0 + (BLOCKS - 1), 1)
                relu1(BLOCKS - 1)
                fuse1(n0 + (BLOCKS - 2), BLOCKS - 2, 0)
                fuse1(n0 + (BLOCKS - 1), BLOCKS - 1, 1)
                bends(n20 + BLOCKS, 1)
                block2_sample(image, 0, True, True)
                with act.Fori(1, BLOCKS - 1) as rb:
                    block2_sample(image, rb, False, True)
                block2_sample(image, BLOCKS - 1, False, False)
                block2_out(n0 + (BLOCKS - 1), BLOCKS - 1, 1)
                act.wait_ge(gn_vec, image * NORM_VEC + (NORM_AT[2] + 1))
                conv2(n0, 0, 0)
                norm_root(image, 2, 4)
                conv2(n0, 0, 1)
                normed(image, 2, 4)
                relu2(0)
                with act.Fori(0, BLOCKS // 2 - 1) as r:
                    for k in range(2):
                        for m in range(2):
                            conv2(n0 + r * 2 + (k + 1), 1 - k, m)
                        relu2(r * 2 + (k + 1))
                        for m in range(2):
                            fuse2(n0 + r * 2 + k, k, m, half0 + r)
                T = Tile(image * TILES, TILES, 0)
                for m in range(2):
                    if nxt:
                        begin(T, m)
                    conv2(n0 + (BLOCKS - 1), 1, m)
                relu2(BLOCKS - 1)
                for k in range(2):
                    for m in range(2):
                        if nxt and 2 * k + m < 3:
                            begin(T, 2 + 2 * k + m)
                        fuse2(n0 + (BLOCKS - 2 + k), k, m, half0 + (BLOCKS // 2 - 1))

            for s, n in ((bc_mm, 4), (fuse_mm, 2), (f2_mm, 4), (stored[0], 16), (stored[1], 16)):
                act.sem_inc(s, n)
            act.sem_inc(f_scan, 1)
            act.sem_inc(b_scan, 1)
            act.sem_inc(dec_f_in, 1)
            act.sem_inc(w_ready, 1)
            act.wait_ge(weights, NWEIGHTS)
            act.wait_ge(cleared, 2)
            fn(a_neg[:], a_neg[:], ACT.Exp).then_inc(a_exp, 1)
            act.wait_ge(a_exp, 2)
            act.wait_ge(consts, 3)
            fn(logc[:, 2:3], logc[:, 3:4], ACT.Ln, bias=logc[:, 1:2]).then_inc(a_exp, 1)

            def one_image(image, nxt):
                lead(Tile(image * TILES, 0, 0), image)
                walk(act, image, tile_steps)
                T = Tile(image * TILES, TILES, 0)
                T.misc = -1
                outputs(T, TILES)
                norm_root(image, 0, CC)
                act.wait_ge(gn_vec, image * NORM_VEC + (NORM_AT[0] + CC + 9))
                for r in range(0, H, XROWS):
                    for c in range(CC):
                        part = img[:, c, 1 + r:1 + r + XROWS, 1:W + 1]
                        fn(part, part, ACT.Identity, scale=gns[:, 4, c:c + 1], bias=gns[:, 5, c:c + 1]).then_inc(x1_mul, 1)
                layer1(image, nxt)

            T = Tile(0, 0, 0)
            for n in range(5):
                begin(T, n)
            with act.Fori(0, IMAGES - 1) as image:
                one_image(image, True)
            one_image(IMAGES - 1, False)

        @block.vector
        def _(dve):
            tt = nc.vector.tensor_tensor
            stt = nc.vector.scalar_tensor_tensor

            def step(T, i):
                i.then_inc(vec, 1)
                T.vec += 1

            def settled(T, but=0):
                dve.wait_ge(vec, T.at(VPER, T.vec - but))

            def gate(T, buf, h, tile_more):
                dve.wait_ge(y_done, T.at(GROUPS, GPH * (h + 1) - GROUPS * (1 - tile_more) + 1))
                tt(yg[:, h, :], gz[:, buf, h, :], p_y[:], ALU.mult).then_inc(yg_ok, 1)

            def deltas(T, buf, more):
                dve.wait_ge(soft_act, T.at(5, 5 * more + 5))
                step(T, nc.vector.tensor_scalar(sp_e[:], sp_e[:], SMALL, None, ALU.min))
                step(T, stt(out=delta[:, buf, :, :], in0=delta[:, buf, :, :], scalar=0.0, in1=du[:, buf, :, :],
                            op0=ALU.max, op1=ALU.add))
                settled(T, 1)
                step(T, stt(out=sp_u[:], in0=sp_u[:], scalar=7.0 / 18, in1=sp_e[:], op0=ALU.add, op1=ALU.mult))
                settled(T)
                step(T, stt(out=sp_u[:], in0=sp_u[:], scalar=1.0, in1=sp_e[:], op0=ALU.subtract, op1=ALU.mult))
                settled(T)
                step(T, stt(out=delta[:, buf, :, :], in0=delta[:, buf, :, :], scalar=logc[:, 2:3], in1=sp_u[:],
                            op0=ALU.subtract, op1=ALU.subtract))
                settled(T)
                tt(du[:, buf, :, :], delta[:, buf, :, :], u[:, buf, :, :], ALU.mult).then_inc(delta_ok, 1)

            def tile_stats(T, t):
                dve.wait_ge(misc_free, T.at(PER, LEAD + (1 if T.last else 2)))
                for c in range(CC):
                    step(T, nc.vector.bn_stats(st0[:, c, bass.ds(t - 1, 1), :],
                                               img[:, c, bass.ds(t * TROWS - (TROWS - 1), TROWS), 1:W + 1]))

            def by_quad(t):
                return t.rearrange("p (q a) b -> p q a b", a=2)

            def products(T, gi, more, half):
                dve.wait_ge(du_mm, T.at(2 * GROUPS, 2 * more + half + 1))
                pl = slice(4 * half, 4 * half + 4)
                tt(planes(g[:, gi % 2, :, :], 2 * half, 2),
                   p_du[:, 2 * half:2 * half + 2, :].rearrange("p q (a b) -> p q a b", a=2),
                   by_quad(brep[:, pl, :]), ALU.mult).then_inc(g_done, 1)

            def products_ahead(T, gi, half):
                if gi == 7 and T.last:
                    return
                if half == 0:
                    dve.wait_ge(y_done, T.at(GROUPS, gi + 1))
                if gi == 7:
                    dve.wait_ge(misc_free, T.at(PER, LEAD + 13 + 2 * half))
                products(T, gi + 1, gi + 1, half)

            def tile_steps(T, t):
                b, nb = T.buf, 1 - T.buf
                for gi in range(GROUPS):
                    gk, back = g2[:, gi % 2, :], slice(None, None, -1)
                    f, d, bw, db = [a.rearrange("p n j -> p (n j)") for a in (hf, dec_f, hb, dec_b)]
                    dve.wait_ge(g_done, T.at(2 * GROUPS, 2 * gi + 4))
                    settled(T)
                    dve.wait_ge(exp_done, T.at(4 * GROUPS, 4 * gi + 6))
                    nc.vector.tensor_tensor_scan(bw[:, back], db[:, back], gk[:, back], 0.0,
                                                 ALU.mult, ALU.add).then_inc(b_scan, 1)
                    dve.wait_ge(dec_f_in, T.at(GROUPS, gi + 2))
                    dve.wait_ge(w_ready, T.at(GROUPS, gi + 1))
                    nc.vector.tensor_tensor_scan(f, d, gk, 0.0, ALU.mult, ALU.add).then_inc(f_scan, 1)
                    if gi == 0 and not T.first:
                        gate(T, nb, 1, 0)
                    if gi == 4:
                        if not T.first:
                            dve.wait_ge(misc_free, T.at(PER, LEAD + (1 if T.last else 2)))
                        gate(T, b, 0, 1)
                    if gi == 5 and not T.last:
                        deltas(T, nb, 1)
                    if gi == 2 and not T.first:
                        tile_stats(T, t)
                    products_ahead(T, gi, 0)
                    dve.wait_ge(f_scan, T.at(GROUPS, gi + 2))
                    step(T, tt(hf[:], hf[:], hb[:], ALU.add))
                    products_ahead(T, gi, 1)
                    settled(T)
                    if gi == 0:
                        dve.wait_ge(misc_free, T.at(PER, (LEAD if T.first else LEAD - 1) + 1))
                    tt(by_quad(wc[:, gi % 2, :, :]), planes(hf, 0, QUADS), by_quad(crep[:, b, :, :]),
                       ALU.mult).then_inc(w_ready, 1)

            def norm(image, use, cols, rows_stats, gain, shift):
                done = [NORM_AT[use]]

                def counted(i):
                    i.then_inc(gn_vec, 1)
                    done[0] += 1

                def ready():
                    dve.wait_ge(gn_vec, image * NORM_VEC + done[0])

                r = [gns[:, n, 0:cols] for n in range(8)]
                nc.vector.memset(gns[:, 7, :], 0.0)
                for c in range(cols):
                    counted(nc.vector.bn_aggr(mv[:, c, :], rows_stats(c)))
                dve.wait_ge(gn_mm, image * (2 * NORMS) + (2 * use + 1))
                counted(nc.vector.tensor_copy(r[1], p_misc[:, 0:cols]))
                ready()
                counted(tt(r[6], mv[:, 0:cols, 0], r[1], ALU.subtract))
                ready()
                counted(tt(r[7], r[6], r[6], ALU.mult))
                ready()
                counted(tt(r[0], r[7], mv[:, 0:cols, 1], ALU.add))
                dve.wait_ge(gn_mm, image * (2 * NORMS) + (2 * use + 2))
                counted(nc.vector.tensor_copy(r[2], p_misc[:, 0:cols]))
                dve.wait_ge(gn_act, image * NORMS + (use + 1))
                counted(nc.vector.reciprocal(r[3], r[3]))
                ready()
                counted(tt(r[4], r[3], gain, ALU.mult))
                ready()
                counted(tt(r[6], r[1], r[4], ALU.mult))
                ready()
                counted(tt(r[5], shift, r[6], ALU.subtract))

            class Count:
                def __init__(self, base, n):
                    self.base, self.n = base, n

                def step(self, i):
                    i.then_inc(vec1, 1)
                    self.n += 1

                def settled(self, but=0):
                    dve.wait_ge(vec1, self.base + (self.n - but))

            def offset_sum(v, n2):
                dve.wait_ge(off_mm, n2 + 1)
                dve.wait_ge(tanh_ok, n2 + 1)
                off, a4 = [grid(p_du[32 * dx:32 * dx + 4, 0, :]) for dx in range(3)], grid(acc[0:4, :])
                v.step(nc.vector.tensor_copy(a4, off[1]))
                v.settled()
                v.step(tt(a4[:, :, 1:W], off[0][:, :, 0:W - 1], a4[:, :, 1:W], ALU.add))
                v.settled()
                tt(a4[:, :, 0:W - 1], off[2][:, :, 1:W], a4[:, :, 0:W - 1], ALU.add).then_inc(off_sum, 1)

            def weigh(v, n2, m, diffs, to, low):
                for s in range(2):
                    if s == 0:
                        v.settled()
                    dve.wait_ge(bc_mm, n2 * 4 + (2 * m + s + 5))
                    v.step(stt(out=grid(to[s]), in0=grid(p_du[:, 1 + s, :]), scalar=0.0, in1=diffs[s][0],
                               op0=ALU.max, op1=ALU.mult))
                for s in range(2):
                    stt(out=grid(low[s]), in0=grid(p_du[:, 1 + s, :]), scalar=0.0, in1=diffs[s][1],
                        op0=ALU.min, op1=ALU.mult).then_inc(bc_used, 1)
                for s in range(2):
                    dve.wait_ge(bc_used, n2 * 4 + (2 * m + s + 3))
                    v.step(tt(to[s], to[s], low[s], ALU.add))

            def block1_sample(v, image, rb, nxt):
                n, n2 = image * BLOCKS + rb, image * (2 * BLOCKS) + rb
                start = v.n
                dve.wait_ge(pads, image * PADS + (PADS if not nxt else rb * 2 + 5))
                for m in range(2):
                    d, base, diffs = [], [], []
                    for s in range(2):
                        t, by = pp[:, 2 * m + s, :, :], 2 * s - 1
                        if m == 0:
                            d.append(df[:, s, :].rearrange("p (h w) -> p h w", w=W))
                            cs = slice(1 + by, 1 + by + W)
                            v.step(tt(d[s], t[:, rows9(rb, 1), cs], t[:, rows9(rb, 0), cs], ALU.subtract))
                            base.append(t[:, rows(rb, 1), cs])
                            diffs.append((d[s][:, 1:RB + 1, :], d[s][:, 0:RB, :]))
                        else:
                            d.append(df[:, s, 0:RB * (W + 1)].rearrange("p (h w) -> p h w", w=W + 1))
                            rs = rows(rb, 1 + by)
                            v.step(tt(d[s], t[:, rs, 1:PW], t[:, rs, 0:PW - 1], ALU.subtract))
                            base.append(t[:, rs, 1:W + 1])
                            diffs.append((d[s][:, :, 1:W + 1], d[s][:, :, 0:W]))
                    to, low = [tm[:, 0, :], tm[:, 1, :]], [tm[:, 2, :], tm[:, 3, :]]
                    weigh(v, n2, m, diffs, to, low)
                    for s in range(2):
                        v.settled(1)
                        v.step(tt(grid(to[s]), grid(to[s]), base[s], ALU.add))
                    v.settled()
                    v.step(tt(to[0], to[0], to[1], ALU.add))
                    if m == 0 and nxt:
                        offset_sum(v, n2 + 1)
                    v.settled()
                    dve.wait_ge(cen_mm, n * 2 + (m + 1))
                    stt(out=m1[:, m, cols(rb)], in0=CENTRE[m], scalar=v1[:, 1 + m:2 + m], in1=to[0],
                        op0=ALU.add, op1=ALU.add).then_inc(cen_used, 1)
                    dve.wait_ge(cen_used, n * 2 + (m + 3))
                    nc.vector.bn_stats(stat(m, rb), m1[:, m, cols(rb)]).then_inc(bn1, 1)
                assert v.n - start == (V1 if nxt else V1 - 2)

            def copy_back(n, rb):
                dve.wait_ge(fuse_ev, n + 3)
                nc.vector.tensor_copy(hr[:, rows(rb, 1), 1:W + 1], hz[:, rows(rb, 1), 1:W + 1]).then_inc(h1_ok, 1)
                for to, at in ((0, 1), (PW - 1, W)):
                    nc.vector.tensor_copy(hr[:, rows(rb, 1), to:to + 1], hz[:, rows(rb, 1), at:at + 1]).then_inc(h1_ok, 1)

            def block2_stats(n, rb):
                dve.wait_ge(o2_ev, n * 4 + 6)
                for c in range(4):
                    nc.vector.bn_stats(stat(c, rb), m2[:, c, cols(rb)]).then_inc(bn1, 1)

            def block2_sample(v, image, rb, first, nxt):
                n, n2 = image * BLOCKS + rb, image * (2 * BLOCKS) + (BLOCKS + rb)
                start = v.n
                v.step(tt(dv[:], hr[:, rows9(rb, 1), :], hr[:, rows9(rb, 0), :], ALU.subtract))
                v.step(tt(dh[:], hr[:, rows10(rb), 1:PW], hr[:, rows10(rb), 0:PW - 1], ALU.subtract))
                for m in range(2):
                    base, diffs = [], []
                    for s in range(2):
                        by = 2 * s - 1
                        if m == 0:
                            cs = slice(1 + by, 1 + by + W)
                            base.append(hr[:, rows(rb, 1), cs])
                            diffs.append((dv[:, 1:RB + 1, cs], dv[:, 0:RB, cs]))
                        else:
                            rs = slice(1 + by, 1 + by + RB)
                            base.append(hr[:, rows(rb, 1 + by), 1:W + 1])
                            diffs.append((dh[:, rs, 1:W + 1], dh[:, rs, 0:W]))
                    to, low = [sm[:, 2 * m, :], sm[:, 2 * m + 1, :]], [tn[:, 0, :], tn[:, 1, :]]
                    dve.wait_ge(o2_mm, n * 4 + (2 * m + 2))
                    weigh(v, n2, m, diffs, to, low)
                    for s in range(2):
                        v.settled(1 - s)
                        tt(grid(to[s]), grid(to[s]), base[s], ALU.add).then_inc(s_ok, 1)
                    if m == 0 and nxt:
                        offset_sum(v, n2 + 1)
                if not first:
                    block2_stats(n - 1, rb - 1)
                assert v.n - start == (V2 if nxt else V2 - 2)

            def residual(n20, r, k):
                for o in range(2):
                    dve.wait_ge(h2_ok, n20 + r * 4 + (2 * k + o + 3))
                    tt(grid(ht[:, k, o, :]), grid(ht[:, k, o, :]), img[:, o, rows(r * 2 + k, 1), 1:W + 1],
                       ALU.add).then_inc(res_ok, 1)

            def begin(image):
                T = Tile(image * TILES, 0, 0)
                T.vec = 0
                deltas(T, 0, 0)

            def layer1(image, nxt):
                n0, n20, at = image * BLOCKS, image * (2 * BLOCKS), image * VEC1
                offset_sum(Count(at, 0), n20)
                with dve.Fori(0, BLOCKS - 2) as rb:
                    block1_sample(Count(at + rb * V1, 2), image, rb, True)
                block1_sample(Count(at, 2 + V1 * (BLOCKS - 2)), image, BLOCKS - 2, True)
                block1_sample(Count(at, 2 + V1 * (BLOCKS - 1)), image, BLOCKS - 1, False)
                dve.wait_ge(bn1, image * BNS + 2 * BLOCKS)
                norm(image, 1, 2, lambda c: st1[:, c, :, :], v1[:, 3:5], v1[:, 5:7])
                for part in (hz[:, 0, :], hz[:, PH - 1, :], hz[:, 1:H + 1, 0:1], hz[:, 1:H + 1, PW - 1:PW]):
                    nc.vector.memset(part, 0.0).then_inc(hz_clear, 1)
                with dve.Fori(0, BLOCKS) as rb:
                    copy_back(n0 + rb, rb)
                dve.wait_ge(h1_ok, image * H1 + 3 * BLOCKS)
                for to, frm in ((0, 1), (PH - 1, H)):
                    nc.vector.tensor_copy(hr[:, to, :], hr[:, frm, :]).then_inc(h1_ok, 1)
                dve.wait_ge(h1_ok, image * H1 + H1)
                offset_sum(Count(at, V1 * BLOCKS), n20 + BLOCKS)
                first = V1 * BLOCKS + 2
                block2_sample(Count(at, first), image, 0, True, True)
                with dve.Fori(1, BLOCKS - 1) as rb:
                    block2_sample(Count(at + rb * V2, first), image, rb, False, True)
                block2_sample(Count(at, first + V2 * (BLOCKS - 1)), image, BLOCKS - 1, False, False)
                block2_stats(n0 + (BLOCKS - 1), BLOCKS - 1)
                dve.wait_ge(bn1, image * BNS + BNS)
                norm(image, 2, 4, lambda c: st1[:, c, :, :], v2[:, 6:10], v2[:, 10:14])
                with dve.Fori(0, BLOCKS // 2 - 1) as r:
                    for k in range(2):
                        residual(n20, r, k)
                residual(n20, BLOCKS // 2 - 1, 0)
                if nxt:
                    begin(image + 1)
                residual(n20, BLOCKS // 2 - 1, 1)

            for s, n in ((tanh_ok, 1), (o2_mm, 4)):
                dve.sem_inc(s, n)
            dve.sem_inc(y_done, 1)
            dve.sem_inc(img_free, 1)
            dve.memset(eps[:], EPS).then_inc(consts, 1)
            dve.memset(gns[:], 0.0).then_inc(consts, 1)
            for n, value in enumerate((-SMALL, 1.0 + SMALL, 0.0, 0.0, SMALL, SMALL / 2 - 1.0 / 3)):
                dve.memset(logc[:, n:n + 1], value)
            dve.wait_ge(weights, NWEIGHTS)
            dve.wait_ge(cleared, 2)
            dve.wait_ge(a_exp, 1)
            nc.vector.tensor_scalar(a_neg[:], a_neg[:], -1.0, None, ALU.mult).then_inc(a_exp, 1)
            for h in range(HALVES):
                nc.vector.tensor_scalar(skip[:, h, :], ident[:], ds[:, h:h + 1], 2.0, ALU.mult, ALU.mult)
            nc.vector.tensor_scalar(bdt2[:], bdt2[:], 2.0, None, ALU.mult).then_inc(consts, 1)
            dve.wait_ge(consts, 3)
            dve.wait_ge(a_exp, 3)

            def one_image(image, nxt):
                lead = Tile(image * TILES, 0, 0)
                nc.vector.memset(dec_b[:, :, TOK - 1], 0.0).then_inc(zeroed, 1)
                nc.vector.memset(dec_f[:, :, 0], 0.0).then_inc(zeroed, 1)
                dve.wait_ge(zeroed, image * 2 + 2)
                dve.wait_ge(misc_free, lead.at(PER, LEAD - QUADS - HALVES + 1))
                for half in range(2):
                    products(lead, 0, 0, half)
                walk(dve, image, tile_steps)
                T = Tile(image * TILES, TILES, 0)
                T.vec = -2
                gate(T, 1, 1, 0)
                dve.wait_ge(misc_free, T.at(PER, 1))
                for c in range(CC):
                    step(T, nc.vector.bn_stats(st0[:, c, TILES - 1, :], img[:, c, H - TROWS + 1:H + 1, 1:W + 1]))
                settled(T)
                norm(image, 0, CC, lambda c: st0[:, c, :, :], gn0[:, 0, :], gn0[:, 1, :])
                dve.wait_ge(x_again, image * 16 + 16)
                for r in range(0, H, XROWS):
                    for c in range(CC):
                        dve.wait_ge(x1_mul, image * XPARTS + (r // XROWS * CC + c + 1))
                        part = img[:, c, 1 + r:1 + r + XROWS, 1:W + 1]
                        tt(part, part, grid(x_old[:, c, r * W:(r + XROWS) * W]), ALU.add).then_inc(x1_ok, 1)
                layer1(image, nxt)

            begin(0)
            with dve.Fori(0, IMAGES - 1) as image:
                one_image(image, True)
            one_image(IMAGES - 1, False)


def kernel(**inputs):
    import numpy as np
    import concourse.bacc as bacc
    from concourse import mybir
    from concourse.bass_utils import run_bass_kernel_spmd
    a = {n: np.asarray(v) for n, v in inputs.items()}
    p = {n[len("L0_conv_"):]: v for n, v in a.items() if n.startswith("L0_conv_")}
    d = {"x": a["x"]}

    def blocks(m):
        halves, n_in, n_out = m.shape
        b = np.zeros((4, n_in, halves, 4, n_out), np.float32)
        for q in range(4):
            b[q, :, :, q, :] = m.transpose(1, 0, 2)
        return b.reshape(4 * n_in, halves, 4 * n_out)

    w_in = p["W_in"].reshape(32, 2, 2, 32).transpose(1, 2, 0, 3)
    w_x = p["W_x"].reshape(2, 32, 34)
    d["W_in_x"], d["W_in_z"] = blocks(w_in[0]), blocks(w_in[1])
    d["W_dts"], d["W_BC"] = blocks(w_x[:, :, 0:2]), blocks(w_x[:, :, 2:34])
    d["W_dt"] = blocks(p["W_dt"].reshape(2, 2, 32).transpose(1, 0, 2))
    d["W_out"] = blocks(p["W_out"].reshape(2, 32, 32))
    d["Ds"] = np.tile(p["Ds"].reshape(2, 32).T, (4, 1))
    d["b_dt"] = np.tile(p["b_dt"].reshape(2, 32).T, (4, 1))
    d["A_logs"] = p["A_logs"].reshape(8, 128).T
    d["gn"] = np.stack([p["gn_w"].reshape(2, 128).T, p["gn_b"].reshape(2, 128).T], axis=1)
    rows = np.arange(128)
    spread = np.zeros((128, 4, 4, 128), np.float32)
    gather = np.zeros((128, 4, 32), np.float32)
    for n in range(4):
        for q in range(4):
            spread[:, q, n, :] = rows[:, None] == 32 * q + 8 * n + rows[None, :] // 16
        gather[:, n, :] = 8 * n + rows[:, None] // 16 == np.arange(32)[None, :]
    d["spread"] = spread
    for name, at in (("copy_b", 0), ("copy_c", 16)):
        d[name] = np.stack([rows[:, None] == 32 * q + at + rows[None, :] % 16 for q in range(4)], axis=1).astype(np.float32)
    d["gather"] = gather
    d["ident"] = np.eye(128, dtype=np.float32)
    d["same64"] = (rows[:, None] // 64 == rows[None, :] // 64).astype(np.float32) / 64
    one = {n[len("L1_conv_cv1_"):]: v for n, v in a.items() if n.startswith("L1_conv_cv1_")}
    two = {n[len("L1_conv_cv2_"):]: v for n, v in a.items() if n.startswith("L1_conv_cv2_")}

    def chunks(m):
        m = m.reshape((m.shape[0] // 128, 128) + m.shape[1:])
        return np.moveaxis(m, 0, 1).reshape(128, -1)

    def layout(b):
        conv = b["conv0_w"].transpose(1, 2, 3, 0)
        dsc = np.stack([b["dscx_w"], b["dscy_w"]]).transpose(2, 0, 3, 1)
        fuse = b["fuse_w"].T
        offs = np.stack([b["offx_w"][0], b["offx_w"][2], b["offy_w"][3], b["offy_w"][5]])
        off = np.zeros((offs.shape[1], 3, 3, 32), np.float32)
        off[..., 0:4] = offs.transpose(1, 2, 3, 0)
        return chunks(conv), chunks(dsc), chunks(fuse), chunks(off)

    conv, dsc, fuse, off = layout(one)
    d["block1"] = np.concatenate([conv, dsc, fuse], axis=1)
    d["off1"] = off.reshape(128, 2, 3, 96)
    conv, dsc, fuse, off = layout(two)
    d["block2"] = np.concatenate([conv, fuse], axis=1)
    d["off2"] = off.reshape(128, 3, 96)
    d["dsc2"] = dsc.reshape(128, 6, 256)
    pick = np.zeros((128, 4, 128), np.float32)
    for n in range(4):
        pick[n, n, :] = 1
    d["pick"] = pick
    d["same4"] = (rows[:, None] // 4 == rows[None, :] // 4).astype(np.float32) / 4
    names = ("conv0_b", "dscx_b", "dscy_b", "gnx_g", "gny_g", "gnx_b", "gny_b", "fuse_b")
    d["v1"] = np.stack([one[n] for n in names], axis=1)
    d["v2"] = np.concatenate([two[n].reshape(2, 128) for n in names]).T
    d["off_b"] = np.stack([np.array([b["offx_b"][0], b["offx_b"][2], b["offy_b"][3], b["offy_b"][5]])
                           for b in (one, two)], axis=1)
    d = {n: np.ascontiguousarray(v) for n, v in d.items()}
    nc = bacc.Bacc("TRN2", target_bir_lowering=False, num_devices=1)
    aps = {n: nc.dram_tensor("in_" + n, v.shape, mybir.dt.float32, kind="ExternalInput").ap() for n, v in d.items()}
    out = nc.dram_tensor("out_0", (4, 256, 64, 64), mybir.dt.float32, kind="ExternalOutput").ap()
    two_layer_program(nc, aps, out)
    r = run_bass_kernel_spmd(nc, [{"in_" + n: v for n, v in d.items()}], core_ids=[0])
    return r.results[0]["out_0"]
```
